# Optimizing a Trainium2 kernel written in Bass

```python
import numpy as np
import jax
import jax.numpy as jnp

def _softmax(x, axis=-1):
    return jax.nn.softmax(x, axis=axis)

def _gelu(x):
    return jax.nn.gelu(x, approximate=True)

def _silu(x):
    return jax.nn.silu(x)

def _sigmoid(x):
    return jax.nn.sigmoid(x)

def _layernorm(x, axis=-1, eps=1e-05):
    m = jnp.mean(x, axis=axis, keepdims=True)
    v = jnp.var(x, axis=axis, keepdims=True)
    return (x - m) / jnp.sqrt(v + eps)

def _scatter_add(tgt, idx, src, axis=0):
    return tgt.at[idx].add(src)

def _segment_sum(src, seg, n):
    return jax.ops.segment_sum(src, seg, n)
kernel_name = 'mk_gnn_ffn_d1_gnn_r32_6d5f16'

def setup_inputs(seed: int=0):
    np.random.seed(seed)
    _w = jnp.asarray

    def _rec_inputs():
        import jax
        import jax.numpy as jnp
        _gk = jax.random.key(seed)
        x = -8.776e-05 + 1 * jax.random.normal(jax.random.fold_in(_gk, 1), (3125, 256), jnp.float32)
        _s = jax.random.randint(jax.random.fold_in(_gk, 2), (25000,), 0, 3125, jnp.int32)
        _d = jax.random.randint(jax.random.fold_in(_gk, 3), (25000,), 0, 3125, jnp.int32)
        _loop = jnp.arange(3125, dtype=jnp.int32)
        src = jnp.concatenate([_s, _d, _loop])
        dst = jnp.concatenate([_d, _s, _loop])
        _o = jnp.argsort(dst, stable=True)
        src = src[_o]
        dst = dst[_o]
        return (x, src, dst)
    x, src, dst = _rec_inputs()

    def _L0_gnn_setup():
        import jax, jax.numpy as jnp
        import numpy as np
        N = 625
        E = 10000
        D_IN = 256
        HID = 64
        HEADS = 4
        D_OUT = 256
        EPS = 1e-05
        SLOPE = 0.2

        def _gat(x, src, dst, W, a_src, a_dst, b, heads, ch, concat):
            n = x.shape[0]
            h = (x @ W).reshape(n, heads, ch)
            es = (h * a_src).sum(-1)
            ed = (h * a_dst).sum(-1)
            e = jax.nn.leaky_relu(es[src] + ed[dst], SLOPE)
            m = jax.ops.segment_max(e, dst, num_segments=n)
            w = jnp.exp(e - m[dst])
            den = jax.ops.segment_sum(w, dst, num_segments=n)
            alpha = w / den[dst]
            msg = h[src] * alpha[:, :, None]
            out = jax.ops.segment_sum(msg, dst, num_segments=n)
            out = out.reshape(n, heads * ch) if concat else out.mean(axis=1)
            return out + b

        def _layernorm(x, g, b):
            mu = x.mean(-1, keepdims=True)
            v = ((x - mu) ** 2).mean(-1, keepdims=True)
            return (x - mu) * jax.lax.rsqrt(v + EPS) * g + b
        key = jax.random.key(seed)
        ks = jax.random.split(key, 10)

        def glorot(k, shape):
            fan_in, fan_out = (shape[0], int(np.prod(shape[1:])))
            s = np.sqrt(2.0 / (fan_in + fan_out)).astype(np.float32)
            return jax.random.normal(k, shape, dtype=jnp.float32) * s
        x = jax.random.normal(ks[0], (N, D_IN), dtype=jnp.float32)
        edge_index = jax.random.randint(ks[1], (2, E), 0, N, dtype=jnp.int64)
        return {'x': x, 'edge_index': edge_index, 'W1': glorot(ks[2], (D_IN, HEADS * HID)), 'a1_src': glorot(ks[3], (HEADS, HID)), 'a1_dst': glorot(ks[4], (HEADS, HID)), 'b1': jnp.zeros((HEADS * HID,), jnp.float32), 'ln_g': jnp.ones((HEADS * HID,), jnp.float32), 'ln_b': jnp.zeros((HEADS * HID,), jnp.float32), 'W2': glorot(ks[5], (HEADS * HID, D_OUT)), 'a2_src': glorot(ks[6], (1, D_OUT)), 'a2_dst': glorot(ks[7], (1, D_OUT)), 'b2': jnp.zeros((D_OUT,), jnp.float32)}
    _L0_gnn_all = _L0_gnn_setup()
    _L0_gnn_in = {k: v for k, v in _L0_gnn_all.items() if k in ('W1', 'a1_src', 'a1_dst', 'b1', 'ln_g', 'ln_b', 'W2', 'a2_src', 'a2_dst', 'b2')}
    del _L0_gnn_all

    def _L0_ffn_setup():
        import jax, jax.numpy as jnp
        import numpy as np
        TOP_K = 2
        LN_EPS = 1e-05
        key = jax.random.key(seed)
        ks = jax.random.split(key, 8)
        B, S, D, E, H = (16, 1024, 256, 8, 1024)
        x = jax.random.normal(ks[0], (B, S, D), dtype=jnp.float32)
        Wr = jax.random.normal(ks[1], (D, E), dtype=jnp.float32) * 0.1
        br = jnp.zeros((E,), dtype=jnp.float32)
        ln_g = jnp.ones((E, D), dtype=jnp.float32)
        ln_b = jnp.zeros((E, D), dtype=jnp.float32)
        W1 = jax.random.normal(ks[2], (E, D, H), dtype=jnp.float32) * (1.0 / np.sqrt(D))
        b1 = jnp.zeros((E, H), dtype=jnp.float32)
        W2 = jax.random.normal(ks[3], (E, H, D), dtype=jnp.float32) * (1.0 / np.sqrt(H))
        b2 = jnp.zeros((E, D), dtype=jnp.float32)
        return {'x': x, 'Wr': Wr, 'br': br, 'ln_g': ln_g, 'ln_b': ln_b, 'W1': W1, 'b1': b1, 'W2': W2, 'b2': b2}
    _L0_ffn_all = _L0_ffn_setup()
    _L0_ffn_in = {k: v for k, v in _L0_ffn_all.items() if k in ('Wr', 'br', 'ln_g', 'ln_b', 'W1', 'b1', 'W2', 'b2')}
    del _L0_ffn_all
    return {'x': x, 'src': src, 'dst': dst, 'L0_gnn_W1': _L0_gnn_in['W1'], 'L0_gnn_a1_src': _L0_gnn_in['a1_src'], 'L0_gnn_a1_dst': _L0_gnn_in['a1_dst'], 'L0_gnn_b1': _L0_gnn_in['b1'], 'L0_gnn_ln_g': _L0_gnn_in['ln_g'], 'L0_gnn_ln_b': _L0_gnn_in['ln_b'], 'L0_gnn_W2': _L0_gnn_in['W2'], 'L0_gnn_a2_src': _L0_gnn_in['a2_src'], 'L0_gnn_a2_dst': _L0_gnn_in['a2_dst'], 'L0_gnn_b2': _L0_gnn_in['b2'], 'L0_ffn_Wr': _L0_ffn_in['Wr'], 'L0_ffn_br': _L0_ffn_in['br'], 'L0_ffn_ln_g': _L0_ffn_in['ln_g'], 'L0_ffn_ln_b': _L0_ffn_in['ln_b'], 'L0_ffn_W1': _L0_ffn_in['W1'], 'L0_ffn_b1': _L0_ffn_in['b1'], 'L0_ffn_W2': _L0_ffn_in['W2'], 'L0_ffn_b2': _L0_ffn_in['b2']}

def reference(x, src, dst, L0_gnn_W1, L0_gnn_a1_src, L0_gnn_a1_dst, L0_gnn_b1, L0_gnn_ln_g, L0_gnn_ln_b, L0_gnn_W2, L0_gnn_a2_src, L0_gnn_a2_dst, L0_gnn_b2, L0_ffn_Wr, L0_ffn_br, L0_ffn_ln_g, L0_ffn_ln_b, L0_ffn_W1, L0_ffn_b1, L0_ffn_W2, L0_ffn_b2):
    import jax
    import jax.numpy as jnp

    def _L0_gnn_ref(x, edge_index, W1, a1_src, a1_dst, b1, ln_g, ln_b, W2, a2_src, a2_dst, b2):
        import jax, jax.numpy as jnp
        import numpy as np
        N = 625
        E = 10000
        D_IN = 256
        HID = 64
        HEADS = 4
        D_OUT = 256
        EPS = 1e-05
        SLOPE = 0.2

        def _gat(x, src, dst, W, a_src, a_dst, b, heads, ch, concat):
            n = x.shape[0]
            h = (x @ W).reshape(n, heads, ch)
            es = (h * a_src).sum(-1)
            ed = (h * a_dst).sum(-1)
            e = jax.nn.leaky_relu(es[src] + ed[dst], SLOPE)
            m = jax.ops.segment_max(e, dst, num_segments=n)
            w = jnp.exp(e - m[dst])
            den = jax.ops.segment_sum(w, dst, num_segments=n)
            alpha = w / den[dst]
            msg = h[src] * alpha[:, :, None]
            out = jax.ops.segment_sum(msg, dst, num_segments=n)
            out = out.reshape(n, heads * ch) if concat else out.mean(axis=1)
            return out + b

        def _layernorm(x, g, b):
            mu = x.mean(-1, keepdims=True)
            v = ((x - mu) ** 2).mean(-1, keepdims=True)
            return (x - mu) * jax.lax.rsqrt(v + EPS) * g + b
        loops = jnp.arange(N, dtype=edge_index.dtype)
        src = jnp.concatenate([edge_index[0], loops])
        dst = jnp.concatenate([edge_index[1], loops])
        h = _gat(x, src, dst, W1, a1_src, a1_dst, b1, HEADS, HID, True)
        h = jax.nn.relu(_layernorm(h, ln_g, ln_b))
        out = _gat(h, src, dst, W2, a2_src, a2_dst, b2, 1, D_OUT, False)
        return out

    def _L0_ffn_ref(x, Wr, br, ln_g, ln_b, W1, b1, W2, b2):
        import jax, jax.numpy as jnp
        import numpy as np
        TOP_K = 2
        LN_EPS = 1e-05
        B, S, D = x.shape
        N = B * S
        xt = x.reshape(N, D)
        logits = xt @ Wr + br
        probs = jax.nn.softmax(logits, axis=-1)
        top_p, top_idx = jax.lax.top_k(probs, TOP_K)
        weights = top_p / top_p.sum(axis=-1, keepdims=True)
        mu = xt.mean(axis=-1, keepdims=True)
        var = ((xt - mu) ** 2).mean(axis=-1, keepdims=True)
        xn = (xt - mu) * jax.lax.rsqrt(var + LN_EPS)
        xe = xn[None, :, :] * ln_g[:, None, :] + ln_b[:, None, :]
        h = jax.nn.gelu(jnp.einsum('end,edh->enh', xe, W1) + b1[:, None, :], approximate=False)
        y = jnp.einsum('enh,ehd->end', h, W2) + b2[:, None, :]
        y_tok = jnp.transpose(y, (1, 0, 2))
        sel = jnp.take_along_axis(y_tok, top_idx[:, :, None], axis=1)
        out = (weights[:, :, None] * sel).sum(axis=1)
        return out.reshape(B, S, D)
    edge_index = jnp.stack([src, dst])
    x = x + _L0_gnn_ref(_layernorm(x, axis=-1), edge_index, L0_gnn_W1, L0_gnn_a1_src, L0_gnn_a1_dst, L0_gnn_b1, L0_gnn_ln_g, L0_gnn_ln_b, L0_gnn_W2, L0_gnn_a2_src, L0_gnn_a2_dst, L0_gnn_b2)
    x = x + _L0_ffn_ref(_layernorm(x, axis=-1)[None], L0_ffn_Wr, L0_ffn_br, L0_ffn_ln_g, L0_ffn_ln_b, L0_ffn_W1, L0_ffn_b1, L0_ffn_W2, L0_ffn_b2)[0]
    return x

_drawn_inputs = setup_inputs


def setup_inputs(seed=0):
    import zlib

    import numpy as np

    out = dict(_drawn_inputs(seed))
    spreads = {'L0_gnn_b1': (0.0, 0.1),
     'L0_gnn_ln_g': (1.0, 0.2),
     'L0_gnn_ln_b': (0.0, 0.1),
     'L0_gnn_b2': (0.0, 0.1),
     'L0_ffn_br': (0.0, 0.1),
     'L0_ffn_ln_g': (1.0, 0.2),
     'L0_ffn_ln_b': (0.0, 0.1),
     'L0_ffn_b1': (0.0, 0.1),
     'L0_ffn_b2': (0.0, 0.1)}
    factors = {}
    for name, (base, spread) in spreads.items():
        noise = np.random.default_rng([zlib.crc32(name.encode()), seed]).standard_normal(out[name].shape)
        drawn = base * np.exp(spread * noise) if base else spread * noise
        out[name] = jnp.asarray(drawn.astype(out[name].dtype))
    for name, factor in factors.items():
        out[name] = (out[name] * factor).astype(out[name].dtype)
    return out
```

```python
import numpy as np
import concourse.bass as bass
from concourse import mybir
from contextlib import ExitStack

P = 128
N, D = 3125, 256
HEADS, CH = 4, 64
E_IN = 53125
LOOPS = 625
EXPERTS, HID = 8, 1024
SLOPE, EPS = 0.2, 1e-5

NT = (N + P - 1) // P
LAST = N - (NT - 1) * P
NPAD = NT * P
ROWS = (E_IN + P - 1) // P
LOOP_ROWS = (LOOPS + P - 1) // P
VIS_G = ROWS + NT - 1
VIS = 448
VC, VP = 4, VIS // 4
PAD_ROWS = ROWS + LOOP_ROWS + (VIS - VIS_G - LOOP_ROWS)
EMPTY_ROW = ROWS + LOOP_ROWS
PAD_DST = 9999
BV = 4
NB = VIS // BV
QB = 4
IT = NB // QB
AHEAD = 2
VTAB = VIS + AHEAD * BV
H1, W1T, TAB1 = HEADS, HEADS * (CH + 1), HEADS * (CH + 1) + 2 * HEADS
H2, W2T, TAB2 = 1, D + 1, D + 3
SPREAD = 60.0
MAX_TILES = (2 * N + EXPERTS * (P - 1)) // P + EXPERTS - 1
SLOT_TILES = 96
CHOICE_ROWS = 2 * NPAD
FC = HID // P
XCH = 6
BIG = 3.0e38

assert (VIS_G + LOOP_ROWS) <= VIS and VIS % (BV * QB) == 0
assert MAX_TILES + NT + 1 <= SLOT_TILES

FORCE_SORT = False
FORCE_MAX = False


def build(nc, x, src, dst, g_w1, g_a1s, g_a1d, g_b1, g_lng, g_lnb, g_w2, g_a2s, g_a2d, g_b2,
          f_wr, f_br, f_lng, f_lnb, f_w1, f_b1, f_w2, f_b2, out):
    f32, i32 = mybir.dt.float32, mybir.dt.int32
    ALU, ACT, AX = mybir.AluOpType, mybir.ActivationFunctionType, mybir.AxisListType
    RED = bass.bass_isa.ReduceOp
    ds = bass.ds

    def dram(name, shape, dt=f32):
        return nc.dram_tensor(name, shape, dt, kind="Internal").ap()

    edge_src = dram("edge_src", (PAD_ROWS * P, 1), i32)
    edge_dst = dram("edge_dst", (PAD_ROWS * P, 1), i32)
    tab1 = dram("tab1", (NPAD, TAB1))
    tab2 = dram("tab2", (NPAD, TAB2))
    xtab = dram("xtab", (NPAD, D))
    ytab = dram("ytab", (CHOICE_ROWS + P, D))

    with ExitStack() as ctx:
        def sb(name, shape, dt=f32):
            return ctx.enter_context(nc.sbuf_tensor(name, shape, dt))

        def sem(name):
            return ctx.enter_context(nc.semaphore(name))

        def sems(name, n):
            return [sem(f"{name}{k}") for k in range(n)]

        xs = sb("xs", [P, NT, D])
        tabs = sb("tabs", [P, NT, TAB1])
        acc = sb("acc", [P, NT + 1, W1T])
        G = sb("G", [P, QB * BV, TAB1])
        OH = sb("OH", [P, QB, BV, P])
        OHT = sb("OHT", [P, 2, BV * P])
        MSG = sb("MSG", [P, 2, BV, W1T])
        src_v = sb("src_v", [P, VTAB], i32)
        dst_v = sb("dst_v", [P, VTAB])
        tile_v = sb("tile_v", [1, VTAB], i32)
        IDX = sb("IDX", [P, QB, BV], i32)
        ident = sb("ident", [P, P])
        ones = sb("ones", [P, P])
        upper = sb("upper", [P, P])
        iota_p = sb("iota_p", [P, P])
        iota_i = sb("iota_i", [P, P], i32)
        part_i = sb("part_i", [P, 1], i32)
        part_f = sb("part_f", [P, 1])
        ed = sb("ed", [P, NT, HEADS])
        shift = sb("shift", [P, NT, HEADS])
        edc = sb("edc", [P, NT + 1, 2 * HEADS])
        es_mm = sb("es_mm", [P, 2 * HEADS])
        es_all = sb("es_all", [P, 2 * HEADS])
        Z = sb("Z", [P, 2, BV, 2 * HEADS])
        U = sb("U", [P, 2, BV, HEADS])
        WT = sb("WT", [P, 2, BV, HEADS])
        xn = sb("xn", [P, 2, D])
        xnT = sb("xnT", [P, 2, 2, P])
        stats = sb("stats", [P, NT, 6])
        mean = sb("mean", [P, NT])
        rstd = sb("rstd", [P, NT])
        tmp_a = sb("tmp_a", [P, NT])
        tmp_b = sb("tmp_b", [P, NT])
        var = sb("var", [P, NT])
        root = sb("root", [P, NT])
        tmp_c = sb("tmp_c", [P, NT])
        rden = sb("rden", [P, NT, HEADS])
        w1a = sb("w1a", [P, 2, D + 2 * HEADS])
        w2a = sb("w2a", [P, 2, D + 2])
        wr = sb("wr", [P, 2, EXPERTS])
        a1 = sb("a1", [P, 2, D])
        a2 = sb("a2", [P, 2, D])
        b1r = sb("b1r", [P, D])
        b2r = sb("b2r", [P, D])
        brr = sb("brr", [P, EXPERTS])
        prod = sb("prod", [P, D])
        vecs = sb("vecs", [P, P])
        cols = sb("cols", [P, 100])
        d_i = sb("d_i", [P, ROWS], i32)
        d_f = sb("d_f", [P, ROWS])
        dn_i = sb("dn_i", [P, 2], i32)
        junk = sb("junk", [P, ROWS])
        cnt = sb("cnt", [P, NT + 3])
        st = sb("st", [P, NT + 3])
        st_i = sb("st_i", [P, 2, NT], i32)
        lo_hi = sb("lo_hi", [P, 2, NT])
        nvis = sb("nvis", [P, NT])
        cum = sb("cum", [P, NT])
        off = sb("off", [P, NT])
        vnum = sb("vnum", [P, VC])
        v_i = sb("v_i", [P, VC], i32)
        ge = sb("ge", [P, VC, NT])
        vt = sb("vt", [P, VC])
        vr = sb("vr", [P, VC])
        vx = sb("vx", [P, VC])
        vy = sb("vy", [P, VC])
        row_i = sb("row_i", [P, VC], i32)
        rows_i = sb("rows_i", [P, 2, VC, P], i32)
        rows_f = sb("rows_f", [P, 2, VC, P])
        flags = sb("flags", [P, 3], i32)
        fl_f = sb("fl_f", [P, HEADS])
        bound = sb("bound", [P, NT + 1, HEADS])
        max_e = sb("max_e", [P, HEADS])
        below = sb("below", [P, NT + 2])
        limit = sb("limit", [P, NT + 2])
        start = sb("start", [P, NT + 1])
        ends = sb("ends", [P, 2], i32)
        lg = sb("lg", [P, NT, EXPERTS])
        lg2 = sb("lg2", [P, NT, EXPERTS])
        oh = sb("oh", [P, 2, NT, EXPERTS])
        ohm = sb("ohm", [P, NT, EXPERTS])
        cand = sb("cand", [P, NT, EXPERTS])
        inc = sb("inc", [P, NT, EXPERTS])
        pos_e = sb("pos_e", [P, NT, EXPERTS])
        top = sb("top", [P, 2, NT])
        first = sb("first", [P, NT])
        gate = sb("gate", [P, 2, NT])
        valid = sb("valid", [P, NT])
        iota_m8 = sb("iota_m8", [P, EXPERTS])
        pos = sb("pos", [P, 2, NT])
        pos_i = sb("pos_i", [P, 2, NT], i32)
        pa = sb("pa", [P, 2, NT])
        pb = sb("pb", [P, 2, NT])
        pai = sb("pai", [P, 2, NT], i32)
        pbi = sb("pbi", [P, 2, NT], i32)
        cid = sb("cid", [P, 2, NT])
        cid_i = sb("cid_i", [P, 2, NT], i32)
        ohb = sb("ohb", [P, 2, P])
        oha = sb("oha", [P, 2, SLOT_TILES])
        nt_i = sb("nt_i", [P, EXPERTS], i32)
        ntf = sb("ntf", [P, EXPERTS])
        ecum = sb("ecum", [P, EXPERTS])
        ebase = sb("ebase", [P, EXPERTS])
        etab = sb("etab", [P, 2, EXPERTS], i32)
        slot_f = sb("slot_f", [P, SLOT_TILES])
        slot_e = sb("slot_e", [P, SLOT_TILES])
        slot_g = sb("slot_g", [P, SLOT_TILES], i32)
        slot_s = sb("slot_s", [P, SLOT_TILES], i32)
        gi = sb("gi", [P, 1], i32)
        si = sb("si", [P, 1], i32)
        fw1 = sb("fw1", [P, 2, 2, HID])
        fw2 = sb("fw2", [P, 2, FC, D])
        fb2 = sb("fb2", [P, 2, D])
        g_flat = G[:, :, :].rearrange("p s c -> p (s c)")
        m_flat = MSG[:, :, :, :].rearrange("p a k c -> p (a k c)")
        xg = m_flat[:, 0:D]
        xeT = m_flat[:, D:2 * D].rearrange("p (k n) -> p k n", k=2)
        ys = m_flat[:, 2 * D:3 * D]
        hid = OHT[:, :, :].rearrange("p a (f n) -> p (a f) n", n=P)
        YL = g_flat[:, 0:4 * D].rearrange("p (s c) -> p s c", s=2)
        yo = g_flat[:, 4 * D:6 * D].rearrange("p (s c) -> p s c", s=2)
        yo2 = g_flat[:, 6 * D:8 * D].rearrange("p (s c) -> p s c", s=2)

        bank = [ctx.enter_context(nc.psum_tensor(f"bank{k}", [P, 512], f32)) for k in range(8)]

        HB = (0, 1, 4, 5)

        s_x = sems("x_loaded", 5)
        s_dst = sem("dst_loaded")
        s_dn = sem("dst_next_loaded")
        s_copy = sem("edges_copied")
        s_w = sem("graph_weights_loaded")
        s_vec = sem("vectors_loaded")
        s_pool = sem("pool_constants")
        s_zero = sem("tail_zeroed")
        s_dve = sem("dve_chain")
        s_cnt = sem("counts_ready")
        s_starts = sem("starts_summed")
        s_rows = sem("visit_rows_ready")
        s_tilt = sem("visit_tiles_on_one_row")
        s_rg = sem("edge_rows_gathered")
        s_rf = sem("edge_rows_as_float")
        s_rT = sem("edge_rows_transposed")
        s_vtab = sem("visit_tables_ready")
        s_vecT = sem("vectors_transposed")
        s_xn = sem("xn_ready")
        s_T = sem("tile_transposed")
        s_TS = sem("transposed_tile_in_sbuf")
        s_H = sem("tile_projected")
        s_HS = sem("projection_in_sbuf")
        s_HE = sem("scores_in_sbuf")
        s_tabw = sem("table_written")
        s_mm = sem("local_extremes")
        s_ar = sem("global_extremes")
        s_shift = sem("shifts_ready")
        s_oh = sem("onehot_ready")
        s_ohT = sem("onehot_transposed")
        s_ohS = sem("onehot_T_in_sbuf")
        s_look = sem("destination_scores_looked_up")
        s_u = sem("exponents_ready")
        s_exp = sem("weights_ready")
        s_msg = sem("messages_ready")
        s_idx = sem("indices_ready")
        s_grant = sem("gather_granted")
        s_sum = sem("messages_summed")
        s_acc = sem("sums_accumulated")
        s_g = sems("row_gathered", QB * BV)
        s_lg = sem("logits_ready")
        s_gx = sem("gate_exponent_ready")
        s_ge = sem("gate_exp_done")
        s_ohm = sem("choices_ready")
        s_pre = sem("ranks_ready")
        s_ob = sem("slot_onehot_ready")
        s_om = sem("slot_onehot_used")
        s_slot = sem("slots_ready")
        s_xt = sems("tokens_written", 2)
        s_fw = sems("expert_weights_loaded", 2)
        s_fwu = sem("expert_weights_used")
        s_gi = sem("token_indices_ready")
        s_gig = sem("token_gather_granted")
        s_xg = sem("tokens_gathered")
        s_xT = sem("tokens_transposed")
        s_xe = sem("expert_input_ready")
        s_h = sem("hidden_ready")
        s_hg = sem("hidden_activated")
        s_y = sem("expert_output_ready")
        s_ys = sem("expert_output_in_sbuf")
        s_sc = sem("results_scattered")
        s_yl = sems("results_loaded", 2)
        s_o = sem("output_ready")
        s_st = sems("output_stored", 2)
        s_var = sem("variances_ready")
        s_root = sem("roots_ready")
        s_ph = sem("phase_over")
        s_flag = sem("flags_ready")
        s_below = sem("edges_before_summed")
        s_src = sem("sources_loaded")
        s_sort = sem("sort_chain")
        s_place = sem("edge_place_ready")
        s_moved = sem("edge_moved")
        s_mi = sems("max_source_ready", 2)
        s_mg = sems("max_row_gathered", 2)
        s_md = sems("max_operands_ready", 2)
        s_mt = sems("max_scores_spread", 2)
        s_mc = sems("max_chain", 2)

        class Chain:
            def __init__(self, eng, sem_):
                self.eng, self.sem, self.n, self.i = eng, sem_, 0, None

            def link(self, ins):
                self.n += 1
                ins.then_inc(self.sem, 1)
                at = self.n if self.i is None else self.i * self.per + (self.n - self.first * self.per)
                self.eng.wait_ge(self.sem, at)

            def enter(self, i, first, per):
                self.i, self.first, self.per, self.start = i, first, per, self.n

            def leave(self, passes):
                assert self.n - self.start == self.per, (self.n - self.start, self.per)
                self.n = self.start + self.per * passes
                self.i = None

        def for_tiles(eng, body, chain=None, per=0):
            body(0, 0)
            body(1, 1)
            with eng.Fori(1, NT // 2) as j:
                if chain:
                    chain.enter(j, 1, 2 * per)
                t = j * 2
                body(t, 0)
                body(t + 1, 1)
            if chain:
                chain.leave(NT // 2 - 1)
            body(NT - 1, 0)

        def after(eng, sem_, value):
            if not isinstance(value, int) or value > 0:
                eng.wait_ge(sem_, value)

        def ring(eng, sem_, base, t):
            if not isinstance(t, int) or t >= 2:
                eng.wait_ge(sem_, base + t - 1)

        def for_tiles_but_last(eng, body):
            body(0, 0)
            body(1, 1)
            with eng.Fori(1, NT // 2) as j:
                t = j * 2
                body(t, 0)
                body(t + 1, 1)

        def skewed(eng, lead, follow):
            lead(0, 0)
            lead(1, 1)
            follow(0, 0)
            lead(2, 0)
            follow(1, 1)
            with eng.Fori(1, NT // 2) as j:
                t = j * 2
                lead(t + 1, 1)
                follow(t, 0)
                lead(t + 2, 0)
                follow(t + 1, 1)
            follow(NT - 1, 0)

        block = ctx.enter_context(nc.Block())

        @block.sync
        def _(sp):
            sp.dma_start(d_i[:, :], dst[0:ROWS, :].rearrange("r c -> (r c)").rearrange("(p j) -> p j", p=P)).then_inc(s_dst, 16)
            for c in range(NT // XCH):
                sp.dma_start(xs[:, c * XCH:(c + 1) * XCH, :],
                             x[c * XCH * P:(c + 1) * XCH * P, :].rearrange("(t p) d -> p t d", p=P)).then_inc(s_x[c], 16)
            sp.wait_ge(s_zero, 2)
            sp.dma_start(xs[0:LAST, NT - 1, :], x[(NT - 1) * P:N, :]).then_inc(s_x[4], 16)
            for c in range(2):
                sp.dma_start(fw1[:, c, :, :], f_w1[c].rearrange("(k p) n -> p k n", p=P)).then_inc(s_fw[c], 16)
                sp.dma_start(fw2[:, c, :, :], f_w2[c].rearrange("(k p) n -> p k n", p=P)).then_inc(s_fw[c], 16)
                sp.dma_start(fb2[:, c, :], f_b2[c:c + 1, :].partition_broadcast(P)).then_inc(s_fw[c], 16)

            for layer, (tab, width) in enumerate(((tab1, TAB1), (tab2, TAB2))):
                def write_tab(t):
                    sp.wait_ge(s_HS, layer * NT + t + 1)
                    sp.wait_ge(s_HE, layer * NT + t + 1)
                    sp.dma_start(tab[ds(t * P, P), :], tabs[:, t, 0:width]).then_inc(s_tabw, 16)
                with sp.Fori(0, NT) as t:
                    write_tab(t)
            def write_tokens(t, s):
                sp.wait_ge(s_xn, 2 * NT + t + 1)
                sp.dma_start(xtab[ds(t * P, P), :], xn[:, s, :]).then_inc(s_xt[s], 16)
            for_tiles(sp, write_tokens)
            with sp.Fori(1, EXPERTS // 2) as j:
                for c in range(2):
                    e = j * 2 + c
                    sp.wait_ge(s_fwu, e - 1)
                    sp.dma_start(fw1[:, c, :, :], f_w1[ds(e, 1)].rearrange("o (k p) n -> p (o k) n", p=P)).then_inc(s_fw[c], 16)
                    sp.dma_start(fw2[:, c, :, :], f_w2[ds(e, 1)].rearrange("o (k p) n -> p (o k) n", p=P)).then_inc(s_fw[c], 16)
                    sp.dma_start(fb2[:, c, :], f_b2[ds(e, 1), :].partition_broadcast(P)).then_inc(s_fw[c], 16)
            sp.wait_ge(s_ph, 5)
            ypair = ytab[0:CHOICE_ROWS, :].rearrange("(n k) d -> n (k d)", k=2)

            def load(t, s):
                ring(sp, s_o, 0, t)
                sp.dma_start(YL[:, s, :], ypair[ds(t * P, P), :]).then_inc(s_yl[s], 16)
            for_tiles_but_last(sp, load)
            sp.wait_ge(s_o, NT - 2)
            sp.dma_start(YL[0:LAST, 0, :], ypair[(NT - 1) * P:N, :]).then_inc(s_yl[0], 16)

        @block.gpsimd
        def _(pool):
            pool.memset(ident[:, :], 0.0).then_inc(s_pool, 1)
            pool.memset(ones[:, :], 1.0).then_inc(s_pool, 1)
            pool.iota(iota_i[:, :], [[1, P]], base=0, channel_multiplier=0).then_inc(s_pool, 1)
            pool.iota(part_i[:, :], [[1, 1]], base=0, channel_multiplier=1).then_inc(s_pool, 1)
            pool.iota(v_i[:, :], [[VP, VC]], base=0, channel_multiplier=1).then_inc(s_pool, 1)
            pool.iota(cid_i[:, :, :], [[1, 2], [2 * P, NT]], base=1, channel_multiplier=2).then_inc(s_pool, 1)
            pool.wait_ge(s_pool, 6)
            pool.affine_select(out=ident[:, :], in_=ident[:, :], compare_op=ALU.not_equal, fill=1.0,
                               base=0, pattern=[[-1, P]], channel_multiplier=1).then_inc(s_pool, 1)
            pool.affine_select(out=upper[:, :], in_=ones[:, :], compare_op=ALU.is_gt, fill=0.0,
                               base=0, pattern=[[1, P]], channel_multiplier=-1).then_inc(s_pool, 1)
            pool.wait_ge(s_copy, 32)
            pool.wait_ge(s_flag, 1)
            unsorted = pool.value_load(flags[0:1, 0:1], min_val=0, max_val=1)
            with pool.If(unsorted > 0):
                pool.dma_start(d_i[:, :], src[0:ROWS, :].rearrange("r c -> (r c)").rearrange("(p j) -> p j", p=P)).then_inc(s_src, 16)
                with pool.Fori(0, ROWS) as j:
                    pool.wait_ge(s_place, j + 1)
                    pool.sem_inc(s_grant, 1)
                    for k, tab in enumerate((edge_src, edge_dst)):
                        pool.indirect_dma_start(tab, bass.IndirectOffsetOnAxis(gi[:, 0:1], 0), ends[:, k:k + 1], None
                                                ).then_inc(s_moved, 16)
                pool.wait_ge(s_moved, 32 * ROWS)
            pool.wait_ge(s_rows, 1)
            for k, tab in enumerate((edge_src, edge_dst)):
                for c in range(VC):
                    pool.indirect_dma_start(rows_i[0:VP, k, c, :], None, tab.rearrange("(r c) o -> r (c o)", c=P),
                                            bass.IndirectOffsetOnAxis(row_i[0:VP, c:c + 1], 0)).then_inc(s_rg, 16)
            for layer, (tab, width, heads) in enumerate(((tab1, TAB1, H1), (tab2, TAB2, H2))):
                pool.wait_ge(s_mm, layer + 1)
                pool.partition_all_reduce(es_all[:, 0:2 * heads], es_mm[:, 0:2 * heads], P, RED.max).then_inc(s_ar, 1)
                pool.wait_ge(s_tabw, 16 * NT * (layer + 1))
                pool.wait_ge(s_flag, layer + 2)
                wide = pool.value_load(flags[0:1, layer + 1:layer + 2], min_val=0, max_val=1)
                with pool.If(wide > 0):
                    with pool.Fori(0, VIS) as n:
                        pool.wait_ge(s_mi[layer], n + 1)
                        pool.sem_inc(s_grant, 1)
                        pool.indirect_dma_start(G[:, 0, 0:width], None, tab, bass.IndirectOffsetOnAxis(gi[:, 0:1], 0)
                                                ).then_inc(s_mg[layer], 16)
                    pool.wait_ge(s_mg[layer], 16 * VIS)
                    pool.wait_ge(s_mt[layer], VIS)
                with pool.Fori(0, IT) as i:
                    for q in range(QB):
                        pool.wait_ge(s_idx, i * QB + (layer * NB + q + 1))
                        pool.sem_inc(s_grant, 1)
                        for k in range(BV):
                            pool.indirect_dma_start(G[:, q * BV + k, 0:width], None, tab,
                                                    bass.IndirectOffsetOnAxis(IDX[:, q, k:k + 1], 0)
                                                    ).then_inc(s_g[q * BV + k], 16)
            pool.wait_ge(s_xt[0], 16 * (NT // 2 + 1))
            pool.wait_ge(s_xt[1], 16 * (NT // 2))
            pool.wait_ge(s_slot, 1)
            pool.indirect_dma_start(ytab, bass.IndirectOffsetOnAxis(si[:, 0:1], 0), ys, None).then_inc(s_sc, 16)

            def gather_tokens(n):
                pool.wait_ge(s_gi, n + 1)
                pool.sem_inc(s_gig, 1)
                pool.indirect_dma_start(xg, None, xtab, bass.IndirectOffsetOnAxis(gi[:, 0:1], 0)).then_inc(s_xg, 16)

            with pool.Fori(0, EXPERTS // 2) as j:
                for c in range(2):
                    e = j * 2 + c
                    n_e = pool.value_load(etab[0:1, 0, ds(e, 1)], min_val=1, max_val=NT)
                    b_e = pool.value_load(etab[0:1, 1, ds(e, 1)], min_val=0, max_val=MAX_TILES)
                    gather_tokens(b_e + e)
                    with pool.Fori(0, n_e) as i:
                        gather_tokens(b_e + e + i + 1)
                        pool.wait_ge(s_ys, b_e + i + 2)
                        pool.sem_inc(s_gig, 1)
                        pool.indirect_dma_start(ytab, bass.IndirectOffsetOnAxis(si[:, 0:1], 0), ys, None
                                                ).then_inc(s_sc, 16)

        @block.scalar
        def _(act):
            act.dma_start(edge_src.rearrange("(r c) o -> r (c o)", c=P), src).then_inc(s_copy, 16)
            act.dma_start(edge_dst.rearrange("(r c) o -> r (c o)", c=P), dst).then_inc(s_copy, 16)
            act.wait_ge(s_zero, 2)
            act.dma_start(dn_i[0:P - 1, :], dst[0:ROWS, :].rearrange("r c -> (r c)").rearrange("(p j) -> p j", p=P)[1:P, 0:2]).then_inc(s_dn, 16)
            act.dma_start(w1a[:, :, 0:D], g_w1.rearrange("(k p) n -> p k n", p=P)).then_inc(s_w, 16)
            for k, a in enumerate((g_a1s, g_a1d)):
                act.dma_start(a1[:, k, :], a.rearrange("h c -> (h c)").unsqueeze(0).partition_broadcast(P)).then_inc(s_w, 16)
            act.dma_start(w2a[:, :, 0:D], g_w2.rearrange("(k p) n -> p k n", p=P)).then_inc(s_w, 16)
            for k, a in enumerate((g_a2s, g_a2d)):
                act.dma_start(a2[:, k, :], a.partition_broadcast(P)).then_inc(s_w, 16)
            act.dma_start(wr[:, :, :], f_wr.rearrange("(k p) n -> p k n", p=P)).then_inc(s_w, 16)
            act.dma_start(b1r[:, :], g_b1.unsqueeze(0).partition_broadcast(P)).then_inc(s_w, 16)
            act.dma_start(b2r[:, :], g_b2.unsqueeze(0).partition_broadcast(P)).then_inc(s_w, 16)
            act.dma_start(brr[:, :], f_br.unsqueeze(0).partition_broadcast(P)).then_inc(s_w, 16)
            r = 0
            for v in (f_b1, f_lng, f_lnb):
                n = v.shape[0] * v.shape[1] // P
                act.dma_start(vecs[r:r + n, :], v.rearrange("e (c p) -> (e c) p", p=P)).then_inc(s_vec, 16)
                r += n
            for v in (g_lng, g_lnb):
                act.dma_start(vecs[r:r + 2, :], v.rearrange("(c p) -> c p", p=P)).then_inc(s_vec, 16)
                r += 2

            def roots(n):
                act.wait_ge(s_var, n)
                act.activation(root[:, :], tmp_a[:, :], ACT.Sqrt).then_inc(s_root, 1)

            for layer, heads in enumerate((H1, H2)):
                nb = layer * NT
                roots(layer + 1)
                def put_T(t, s):
                    act.wait_ge(s_T, nb + t + 1)
                    ring(act, s_H, nb, t)
                    psT = bank[s][:, 0:D].rearrange("p (k n) -> p k n", k=2)
                    if layer == 0:
                        act.activation(xnT[:, s, :, :], psT, ACT.Copy).then_inc(s_TS, 1)
                    else:
                        for k in range(2):
                            ins = act.activation(xnT[:, s, k, :], psT[:, k, :], ACT.Relu,
                                                 scale=cols[:, 96 + k:97 + k], bias=cols[:, 98 + k:99 + k])
                        ins.then_inc(s_TS, 1)

                def put_H(t, s):
                    act.wait_ge(s_HE, nb + t + 1)
                    if layer == 0:
                        row = tabs[:, t, 0:W1T].rearrange("p (h c) -> p h c", c=CH + 1)[:, :, 0:CH]
                        act.activation(row, bank[2 + s][:, 0:D].rearrange("p (h c) -> p h c", c=CH), ACT.Copy).then_inc(s_HS, 1)
                    else:
                        act.activation(tabs[:, t, 0:D], bank[2 + s][:, 0:D], ACT.Copy).then_inc(s_HS, 1)
                if layer == 1:
                    act.wait_ge(s_vecT, 2)
                    act.wait_ge(s_tabw, 16 * NT)
                skewed(act, put_T, put_H)

                def put_onehot_T(i, q, ahead):
                    b = i * QB + (layer * (NB + AHEAD) + q + ahead)
                    act.wait_ge(s_ohT, b + 1)
                    after(act, s_look, b - 1)
                    act.activation(OHT[:, (q + ahead) % 2, :], bank[(q + ahead) % 2][:, :], ACT.Copy).then_inc(s_ohS, 1)

                def put_indices(i, q, col):
                    act.activation(IDX[:, q, :], src_v[:, ds(col, BV)] if not isinstance(col, int) else src_v[:, col:col + BV],
                                   ACT.Copy).then_inc(s_idx, 1)

                def step(i, q):
                    put_onehot_T(i, q, AHEAD)
                    act.wait_ge(s_u, i * QB + (layer * NB + q + 1))
                    act.activation(WT[:, q % 2, :, 0:heads], U[:, q % 2, :, 0:heads], ACT.Exp).then_inc(s_exp, 1)

                if layer == 0:
                    act.wait_ge(s_vtab, 1)
                after(act, s_msg, layer * NB)
                for q in range(3):
                    put_indices(0, q, q * BV)
                for b in range(AHEAD):
                    put_onehot_T(0, 0, b)

                def body(i, last=False, first=False):
                    for q in range(QB):
                        step(i, q)
                        if not (last and q > 0):
                            if not (first and q == 0):
                                act.wait_ge(s_msg, i * QB + (layer * NB + q))
                            elif layer == 1:
                                pass
                            put_indices(i, (q + 3) % QB, i * (QB * BV) + (q + 3) * BV)
                body(0, first=True)
                with act.Fori(1, IT - 1) as i:
                    body(i)
                body(IT - 1, last=True)

            roots(3)
            roots(4)
            def put_T3(t, s):
                act.wait_ge(s_T, 2 * NT + t + 1)
                ring(act, s_H, 2 * NT, t)
                act.activation(xnT[:, s, :, :], bank[s][:, 0:D].rearrange("p (k n) -> p k n", k=2), ACT.Copy).then_inc(s_TS, 1)
            for_tiles(act, put_T3)
            act.wait_ge(s_gx, 1)
            act.activation(gate[:, 1, :], first[:, :], ACT.Exp).then_inc(s_ge, 1)

            act.wait_ge(s_slot, 1)
            with act.Fori(0, EXPERTS // 2) as j:
                for c in range(2):
                    e = j * 2 + c
                    n_e = act.value_load(etab[0:1, 0, ds(e, 1)], min_val=1, max_val=NT)
                    b_e = act.value_load(etab[0:1, 1, ds(e, 1)], min_val=0, max_val=MAX_TILES)
                    with act.Fori(0, n_e) as i:
                        for f in range(FC):
                            if f % 2 == 0:
                                act.wait_ge(s_h, (b_e + i) * (FC // 2) + (f // 2 + 1))
                            act.activation(hid[:, f, :], bank[HB[f // 2]][:, (f % 2) * P:(f % 2 + 1) * P], ACT.Gelu,
                                           bias=cols[:, ds(e * FC + f, 1)]).then_inc(s_hg, 1)
            def store(t, s):
                act.wait_ge(s_o, t + 1)
                act.dma_start(out[ds(t * P, P), :], yo2[:, s, :]).then_inc(s_st[s], 16)
            for_tiles_but_last(act, store)
            act.wait_ge(s_o, NT)
            act.dma_start(out[(NT - 1) * P:N, :], yo2[0:LAST, 0, :]).then_inc(s_st[0], 16)
            act.wait_ge(s_st[0], 16 * (NT // 2 + 1))
            act.wait_ge(s_st[1], 16 * (NT // 2))

        @block.tensor
        def _(pe):
            pe.wait_ge(s_pool, 8)
            pe.wait_ge(s_cnt, 1)
            pe.matmul(bank[4][:, 0:NT + 3], ones[:, :], cnt[:, :], start=True, stop=True).then_inc(s_starts, 1)
            pe.matmul(bank[3][:, 0:NT + 1], upper[:, :], cnt[:, 0:NT + 1], start=True, stop=True).then_inc(s_below, 1)
            pe.wait_ge(s_vec, 16 * 5)
            pe.transpose(bank[5][:, 0:100], vecs[0:100, :], ident[0:100, 0:100]).then_inc(s_vecT, 1)
            pe.wait_ge(s_rows, 1)
            for c in range(VC):
                ins = pe.matmul(bank[4][0:1, c * VP:(c + 1) * VP], vt[0:VP, c:c + 1], ident[0:VP, 0:VP], start=True, stop=True)
            ins.then_inc(s_tilt, 1)
            pe.wait_ge(s_rf, 1)
            for k in range(2):
                for c in range(VC):
                    ins = pe.transpose(bank[6 + k][:, c * VP:(c + 1) * VP], rows_f[0:VP, k, c, :], ident[0:VP, 0:VP])
            ins.then_inc(s_rT, 1)

            def node_phase(ph, rhs, width):
                nb = ph * NT

                def T(t, s):
                    pe.wait_ge(s_xn, nb + t + 1)
                    ring(pe, s_TS, nb, t)
                    for k in range(2):
                        ins = pe.transpose(bank[s][:, k * P:(k + 1) * P], xn[:, s, k * P:(k + 1) * P], ident[:, :])
                    ins.then_inc(s_T, 1)

                def Hm(t, s):
                    pe.wait_ge(s_TS, nb + t + 1)
                    if ph < 2:
                        ring(pe, s_HS, nb, t)
                    ring(pe, s_HE, nb, t)
                    for k in range(2):
                        ins = pe.matmul(bank[2 + s][:, 0:width], xnT[:, s, k, :], rhs[:, k, :], start=(k == 0), stop=(k == 1))
                    ins.then_inc(s_H, 1)
                skewed(pe, T, Hm)

            for layer, (rhs, heads, width) in enumerate(((w1a, H1, W1T), (w2a, H2, W2T))):
                node_phase(layer, rhs, D + 2 * heads)

                def transpose_onehot(i, q, ahead):
                    b = i * QB + (layer * (NB + AHEAD) + q + ahead)
                    pe.wait_ge(s_oh, b + 1)
                    after(pe, s_ohS, b - 1)
                    for k in range(BV):
                        ins = pe.transpose(bank[(q + ahead) % 2][:, k * P:(k + 1) * P], OH[:, (q + ahead) % QB, k, :], ident[:, :])
                    ins.then_inc(s_ohT, 1)

                def look_up(i, q, ahead):
                    b = i * QB + (layer * (NB + AHEAD) + q + ahead)
                    pe.wait_ge(s_ohS, b + 1)
                    if not (isinstance(i, int) and i * QB + q + ahead < 2):
                        pe.wait_ge(s_u, i * QB + (layer * NB + q + ahead - 1))
                    for k in range(BV):
                        col = i * (QB * BV) + ((q + ahead) * BV + k)
                        ti = pe.value_load(tile_v[0:1, ds(col, 1)] if not isinstance(col, int) else tile_v[0:1, col:col + 1],
                                           min_val=0, max_val=NT)
                        ins = pe.matmul(bank[2 + (q + ahead) % 2][:, k * 2 * HEADS:(k + 1) * 2 * HEADS],
                                        OHT[:, (q + ahead) % 2, k * P:(k + 1) * P], edc[:, ds(ti, 1), :],
                                        start=True, stop=True)
                    ins.then_inc(s_look, 1)

                def sum_messages(i, q):
                    b = i * QB + (layer * NB + q)
                    pe.wait_ge(s_msg, b + 1)
                    for k in range(BV):
                        after(pe, s_acc, (b - 1) * BV + k + 1)
                        pe.matmul(bank[4 + k][:, 0:width], OH[:, q, k, :], MSG[:, q % 2, k, 0:width],
                                  start=True, stop=True).then_inc(s_sum, 1)

                pe.wait_ge(s_flag, layer + 2)
                wide = pe.value_load(flags[0:1, layer + 1:layer + 2], min_val=0, max_val=1)
                with pe.If(wide > 0):
                    with pe.Fori(0, VIS) as n:
                        pe.wait_ge(s_md[layer], n + 1)
                        pe.transpose(bank[0][:, 0:P], OH[:, 0, 0, :], ident[:, :])
                        pe.matmul(bank[1][:, 0:heads * P], ones[:, :], OHT[:, 0, 0:heads * P], start=True, stop=True
                                  ).then_inc(s_mt[layer], 1)
                pe.wait_ge(s_shift, layer + 1)
                for b in range(AHEAD):
                    transpose_onehot(0, 0, b)
                look_up(0, 0, 0)

                def body(i):
                    for q in range(QB):
                        transpose_onehot(i, q, AHEAD)
                        look_up(i, q, 1)
                        sum_messages(i, q)
                body(0)
                with pe.Fori(1, IT) as i:
                    body(i)
                look_up(IT - 1, QB - 1, AHEAD)

            node_phase(2, wr, EXPERTS)
            pe.wait_ge(s_ohm, 1)
            m = ohm[:, :, :].rearrange("p t e -> p (t e)")
            pe.matmul(bank[4][:, 0:NT * EXPERTS], upper[:, :], m, start=True, stop=True)
            pe.matmul(bank[5][:, 0:NT * EXPERTS], ones[:, :], m, start=True, stop=True).then_inc(s_pre, 1)

            def place(n, s, t_first, t_last):
                pe.wait_ge(s_ob, n + 1)
                pe.matmul(bank[6][:, 0:SLOT_TILES], ohb[:, s, :], oha[:, s, :], start=t_first, stop=t_last).then_inc(s_om, 1)
            place(0, 0, True, False)
            place(1, 1, False, False)
            with pe.Fori(1, NT - 1) as t:
                for k in range(2):
                    place(t * 2 + k, k, False, False)
            place(2 * NT - 2, 0, False, False)
            place(2 * NT - 1, 1, False, True)

            def tokens_T(n):
                pe.wait_ge(s_xg, (n + 1) * 16)
                for k in range(2):
                    ins = pe.transpose(bank[2][:, k * P:(k + 1) * P], xg[:, k * P:(k + 1) * P], ident[:, :])
                ins.then_inc(s_xT, 1)

            pe.wait_ge(s_slot, 1)
            with pe.Fori(0, EXPERTS // 2) as j:
                for c in range(2):
                    e = j * 2 + c
                    n_e = pe.value_load(etab[0:1, 0, ds(e, 1)], min_val=1, max_val=NT)
                    b_e = pe.value_load(etab[0:1, 1, ds(e, 1)], min_val=0, max_val=MAX_TILES)
                    pe.wait_ge(s_fw[c], j * 48 + 48)
                    tokens_T(b_e + e)
                    with pe.Fori(0, n_e) as i:
                        g = b_e + i
                        pe.wait_ge(s_xe, g + e + 1)
                        for f in range(FC):
                            for k in range(2):
                                ins = pe.matmul(bank[HB[f // 2]][:, (f % 2) * P:(f % 2 + 1) * P],
                                                fw1[:, c, k, f * P:(f + 1) * P], xeT[:, k, :], start=(k == 0), stop=(k == 1))
                            if f % 2:
                                ins.then_inc(s_h, 1)
                        tokens_T(g + e + 1)
                        pe.wait_ge(s_ys, g + 1)
                        for f in range(FC):
                            pe.wait_ge(s_hg, g * FC + (f + 1))
                            ins = pe.matmul(bank[3][:, 0:D], hid[:, f, :], fw2[:, c, f, :], start=(f == 0), stop=(f == FC - 1))
                        ins.then_inc(s_y, 1)
                    pe.wait_ge(s_xe, b_e + n_e + e + 1)

        @block.vector
        def _(v):
            ch = Chain(v, s_dve)
            link = ch.link

            def sort_edges():
                so = Chain(v, s_sort)
                v.wait_ge(s_below, 1)
                v.tensor_copy(below[:, 0:NT + 1], bank[3][:, 0:NT + 1])
                so.link(v.tensor_scalar(below[:, NT + 1:NT + 2], part_f[:, :], float(ROWS), None, ALU.mult))
                v.tensor_scalar(limit[:, :], iota_p[:, 0:NT + 2], float(P), None, ALU.mult)
                so.link(v.tensor_tensor(start[:, :], below[:, 1:NT + 2], below[:, 0:NT + 1], ALU.subtract))
                so.link(v.scalar_tensor_tensor(start[:, :], start[:, :], -1.0, st[:, 0:NT + 1], ALU.add, ALU.add))
                place, inside, rank = (acc[:, k * 2:k * 2 + 2, :].rearrange("p t c -> p (t c)")[:, 0:ROWS] for k in range(3))
                all_ones = acc[:, 6:8, :].rearrange("p t c -> p (t c)")[:, 0:ROWS]
                v.memset(all_ones, 1.0)
                so.link(v.memset(limit[:, NT + 1:NT + 2], 10.0 * PAD_DST))
                so.link(v.memset(place, 0.0))
                with v.Fori(0, NT + 1) as t:
                    so.enter(t, 0, 5)
                    so.link(v.tensor_scalar(junk[:, :], d_f[:, :], limit[:, ds(t + 1, 1)], None, ALU.is_lt))
                    so.link(v.scalar_tensor_tensor(inside, d_f[:, :], limit[:, ds(t, 1)], junk[:, :], ALU.is_ge, ALU.mult))
                    so.link(v.tensor_tensor_scan(rank, all_ones, inside, 0.0, ALU.mult, ALU.add))
                    so.link(v.scalar_tensor_tensor(rank, rank, start[:, ds(t, 1)], inside, ALU.add, ALU.mult))
                    so.link(v.tensor_tensor(place, place, rank, ALU.add))
                so.leave(NT + 1)
                v.wait_ge(s_src, 16)

                def move(j):
                    v.tensor_copy(gi[:, :], place[:, ds(j, 1)] if not isinstance(j, int) else place[:, j:j + 1])
                    v.tensor_copy(ends[:, 0:1], d_i[:, ds(j, 1)])
                    v.tensor_copy(ends[:, 1:2], d_f[:, ds(j, 1)]).then_inc(s_place, 1)
                move(0)
                with v.Fori(1, ROWS) as j:
                    v.wait_ge(s_moved, j * 32)
                    move(j)
                v.wait_ge(s_moved, ROWS * 32)

            def true_maxima(layer, heads, wt):
                mc = Chain(v, s_mc[layer])
                least = es_all[:, heads:2 * heads].unsqueeze(1).broadcast_to([P, NT + 1, heads])
                mc.link(v.tensor_scalar(bound[:, :, 0:heads], least, -1.0, None, ALU.mult))
                spread = OHT[:, 0, 0:heads * P].rearrange("p (h e) -> p h e", h=heads)
                with v.Fori(0, VIS) as n:
                    mc.enter(n, 0, 5)
                    v.tensor_copy(gi[:, :], src_v[:, ds(n, 1)]).then_inc(s_mi[layer], 1)
                    v.tensor_scalar(OH[:, 0, 0, :], iota_p[:, :], dst_v[:, ds(n, 1)], None, ALU.is_equal)
                    v.wait_ge(s_mg[layer], n * 16 + 16)
                    for h in range(heads):
                        ins = v.tensor_scalar(spread[:, h, :], ident[:, :], G[:, 0, wt + h:wt + h + 1], None, ALU.mult)
                    mc.link(ins)
                    v.sem_inc(s_md[layer], 1)
                    v.wait_ge(s_mt[layer], n + 1)
                    mc.link(v.tensor_scalar(OHT[:, 1, 0:P], bank[0][:, 0:P], 1e30, -1e30, ALU.mult, ALU.add))
                    mc.link(v.tensor_tensor(spread, bank[1][:, 0:heads * P].rearrange("p (h e) -> p h e", h=heads),
                                            OHT[:, 1, 0:P].unsqueeze(1).broadcast_to([P, heads, P]), ALU.add))
                    mc.link(v.tensor_reduce(max_e[:, 0:heads], spread, AX.X, ALU.max))
                    ti = v.value_load(tile_v[0:1, ds(n, 1)], min_val=0, max_val=NT)
                    b = bound[:, ds(ti, 1), 0:heads].rearrange("p o h -> p (o h)")
                    mc.link(v.tensor_tensor(b, b, max_e[:, 0:heads], ALU.max))
                mc.leave(VIS)

            v.memset(dn_i[:, :], PAD_DST).then_inc(s_zero, 1)
            v.memset(xs[:, NT - 1, :], 0.0).then_inc(s_zero, 1)
            v.memset(tabs[:, :, :], 1.0)
            v.memset(dst_v[:, :], float(PAD_DST))
            v.memset(cnt[:, :], 0.0)
            link(v.memset(tile_v[:, :], 0))
            v.sem_inc(s_ph, 1)

            v.wait_ge(s_pool, 8)
            v.tensor_copy(iota_p[:, :], iota_i[:, :])
            v.tensor_copy(part_f[:, :], part_i[:, :])
            v.tensor_copy(vnum[:, :], v_i[:, :])
            v.wait_ge(s_dst, 16)
            link(v.tensor_copy(d_f[:, :], d_i[:, :]))
            for t in range(1, NT + 1):
                link(v.tensor_scalar(junk[:, :], d_f[:, :], float(t * P), 0.0, ALU.is_lt, ALU.add, accum_out=cnt[:, t:t + 1]))
            link(v.tensor_tensor(junk[:, 0:ROWS - 1], d_f[:, 0:ROWS - 1], d_f[:, 1:ROWS], ALU.is_gt))
            v.tensor_reduce(cnt[:, NT + 1:NT + 2], junk[:, 0:ROWS - 1], AX.X, ALU.add)
            v.wait_ge(s_dn, 16)
            link(v.tensor_tensor(cnt[:, NT + 2:NT + 3], d_i[:, ROWS - 1:ROWS], dn_i[:, 0:1], ALU.is_gt))
            v.sem_inc(s_cnt, 1)
            v.wait_ge(s_starts, 1)
            link(v.tensor_copy(st[:, :], bank[4][:, 0:NT + 3]))
            link(v.tensor_tensor(fl_f[:, 0:1], st[:, NT + 1:NT + 2], st[:, NT + 2:NT + 3], ALU.add))
            link(v.tensor_scalar(flags[:, 0:1], fl_f[:, 0:1], -1.0 if FORCE_SORT else 0.0, None, ALU.is_gt))
            v.sem_inc(s_flag, 1)
            unsorted = v.value_load(flags[0:1, 0:1], min_val=0, max_val=1)
            with v.If(unsorted > 0):
                sort_edges()
            v.tensor_copy(st_i[:, 0, :], st[:, 0:NT])
            link(v.tensor_scalar(st_i[:, 1, :], st[:, 1:NT + 1], float(P - 1), None, ALU.add))
            link(v.tensor_scalar(st_i[:, :, :], st_i[:, :, :], 7, None, ALU.arith_shift_right))
            link(v.tensor_copy(lo_hi[:, :, :], st_i[:, :, :]))
            link(v.tensor_tensor(nvis[:, :], lo_hi[:, 1, :], lo_hi[:, 0, :], ALU.subtract))
            link(v.tensor_tensor(off[:, :], st[:, 1:NT + 1], st[:, 0:NT], ALU.is_gt))
            link(v.tensor_tensor(nvis[:, :], nvis[:, :], off[:, :], ALU.mult))
            link(v.tensor_tensor_scan(cum[:, :], ones[:, 0:NT], nvis[:, :], 0.0, ALU.mult, ALU.add))
            link(v.tensor_tensor(off[:, :], lo_hi[:, 0, :], cum[:, :], ALU.subtract))
            link(v.tensor_tensor(off[:, :], off[:, :], nvis[:, :], ALU.add))
            vb = vnum[:, :].unsqueeze(2).broadcast_to([P, VC, NT])
            link(v.tensor_tensor(ge[:, :, :], vb, cum[:, :].unsqueeze(1).broadcast_to([P, VC, NT]), ALU.is_ge))
            link(v.tensor_reduce(vt[:, :], ge[:, :, :], AX.X, ALU.add))
            link(v.tensor_tensor(ge[:, :, :], vt[:, :].unsqueeze(2).broadcast_to([P, VC, NT]),
                                 iota_p[:, 0:NT].unsqueeze(1).broadcast_to([P, VC, NT]), ALU.is_equal))
            link(v.tensor_tensor(ge[:, :, :], ge[:, :, :], off[:, :].unsqueeze(1).broadcast_to([P, VC, NT]), ALU.mult))
            link(v.tensor_reduce(vr[:, :], ge[:, :, :], AX.X, ALU.add))
            link(v.tensor_tensor(vr[:, :], vr[:, :], vnum[:, :], ALU.add))
            v.tensor_scalar(vx[:, :], vnum[:, :], -1.0, float(EMPTY_ROW), ALU.mult, ALU.add)
            link(v.tensor_scalar(vy[:, :], vt[:, :], float(NT), None, ALU.is_ge))
            link(v.tensor_tensor(vx[:, :], vx[:, :], vy[:, :], ALU.mult))
            link(v.tensor_tensor(vr[:, :], vr[:, :], vx[:, :], ALU.add))
            link(v.tensor_scalar(vy[:, :], vnum[:, :], float(VIS_G), None, ALU.is_ge))
            link(v.tensor_scalar(vx[:, :], vnum[:, :], float(ROWS - VIS_G - EMPTY_ROW), None, ALU.add))
            link(v.tensor_tensor(vx[:, :], vx[:, :], vy[:, :], ALU.mult))
            link(v.tensor_tensor(vr[:, :], vr[:, :], vx[:, :], ALU.add))
            link(v.tensor_scalar(vx[:, :], vnum[:, :], float(-VIS_G - NT), None, ALU.add))
            link(v.tensor_tensor(vx[:, :], vx[:, :], vy[:, :], ALU.mult))
            link(v.tensor_tensor(vt[:, :], vt[:, :], vx[:, :], ALU.add))
            link(v.tensor_copy(row_i[:, :], vr[:, :]))
            v.sem_inc(s_rows, 1)
            link(v.tensor_scalar(vx[:, :], vt[:, :], float(-P), None, ALU.mult))

            v.wait_ge(s_w, 16 * 10)
            for wa, a, heads in ((w1a, a1, H1), (w2a, a2, H2)):
                for k in range(2):
                    for sd in range(2):
                        link(v.tensor_tensor(prod[:, :], wa[:, k, 0:D], a[:, sd, :], ALU.mult))
                        link(v.tensor_reduce(wa[:, k, D + sd * heads:D + (sd + 1) * heads],
                                             prod[:, :].rearrange("p (h c) -> p h c", h=heads), AX.X, ALU.add))
            v.sem_inc(s_ph, 1)
            v.wait_ge(s_vecT, 1)
            v.tensor_copy(cols[:, :], bank[5][:, 0:100]).then_inc(s_vecT, 1)
            v.wait_ge(s_tilt, 1)
            v.tensor_copy(tile_v[0:1, 0:VIS], bank[4][0:1, 0:VIS])
            v.wait_ge(s_rg, 16 * 2 * VC)
            v.tensor_copy(rows_f[0:VP, 0, :, :], rows_i[0:VP, 0, :, :])
            for c in range(VC):
                ins = v.tensor_scalar(rows_f[0:VP, 1, c, :], rows_i[0:VP, 1, c, :], vx[0:VP, c:c + 1], None, ALU.add)
            link(ins)
            v.sem_inc(s_rf, 1)
            v.wait_ge(s_rT, 1)
            v.tensor_copy(src_v[:, 0:VIS], bank[6][:, 0:VIS])
            link(v.tensor_copy(dst_v[:, 0:VIS], bank[7][:, 0:VIS]))
            v.sem_inc(s_vtab, 1)

            def combine():
                m0, m1 = stats[:, :, 1], stats[:, :, 4]
                v.tensor_tensor(tmp_a[:, :], stats[:, :, 2], stats[:, :, 5], ALU.add)
                v.tensor_tensor(tmp_b[:, :], m0, m1, ALU.subtract)
                link(v.tensor_tensor(mean[:, :], m0, m1, ALU.add))
                v.tensor_scalar(mean[:, :], mean[:, :], 0.5, None, ALU.mult)
                link(v.tensor_tensor(tmp_b[:, :], tmp_b[:, :], tmp_b[:, :], ALU.mult))
                link(v.tensor_scalar(tmp_b[:, :], tmp_b[:, :], 0.25, None, ALU.mult))
                link(v.scalar_tensor_tensor(var[:, :], tmp_a[:, :], 1.0 / D, tmp_b[:, :], ALU.mult, ALU.add))

            def inverse_root(n):
                link(v.tensor_scalar(tmp_a[:, :], var[:, :], EPS, None, ALU.add))
                v.sem_inc(s_var, 1)
                v.wait_ge(s_root, n)
                link(v.reciprocal(rstd[:, :], root[:, :]))
                link(v.tensor_tensor(tmp_c[:, :], rstd[:, :], rstd[:, :], ALU.mult))
                link(v.tensor_tensor(tmp_c[:, :], tmp_c[:, :], tmp_a[:, :], ALU.mult))
                link(v.tensor_scalar(tmp_c[:, :], tmp_c[:, :], -0.5, 1.5, ALU.mult, ALU.add))
                link(v.tensor_tensor(rstd[:, :], rstd[:, :], tmp_c[:, :], ALU.mult))

            def normalise(ph, source):
                def one(t, s):
                    ring(v, s_T, ph * NT, t)
                    v.tensor_scalar(xn[:, s, :], source(t), mean[:, ds(t, 1)], rstd[:, ds(t, 1)],
                                    ALU.subtract, ALU.mult).then_inc(s_xn, 1)
                return one

            def scores_out(ph, heads):
                def one(t, s):
                    v.wait_ge(s_H, ph * NT + t + 1)
                    wt = W1T if heads == H1 else W2T
                    v.tensor_copy(tabs[:, t, wt:wt + heads], bank[2 + s][:, D:D + heads])
                    v.tensor_scalar(tabs[:, t, wt + heads:wt + 2 * heads], bank[2 + s][:, D:D + heads], SLOPE, None, ALU.mult)
                    v.tensor_copy(ed[:, t, 0:heads], bank[2 + s][:, D + heads:D + 2 * heads]).then_inc(s_HE, 1)
                return one

            def shifts(layer, heads, wt):
                es = tabs[:, :, wt:wt + heads].rearrange("p t h -> p h t")
                v.wait_ge(s_HE, (layer + 1) * NT)
                link(v.tensor_reduce(es_mm[:, 0:heads], es, AX.X, ALU.max))
                link(v.tensor_reduce(es_mm[:, heads:2 * heads], es, AX.X, ALU.min))
                link(v.tensor_scalar(es_mm[:, heads:2 * heads], es_mm[:, heads:2 * heads], -1.0, None, ALU.mult))
                v.sem_inc(s_mm, 1)
                v.wait_ge(s_ar, layer + 1)
                v.tensor_copy(bound[:, :, 0:heads], es_all[:, 0:heads].unsqueeze(1).broadcast_to([P, NT + 1, heads]))
                link(v.tensor_tensor(fl_f[:, 0:heads], es_all[:, 0:heads], es_all[:, heads:2 * heads], ALU.add))
                link(v.tensor_reduce(fl_f[:, 0:1], fl_f[:, 0:heads], AX.X, ALU.max))
                link(v.tensor_scalar(flags[:, layer + 1:layer + 2], fl_f[:, 0:1], -1.0 if FORCE_MAX else SPREAD, None, ALU.is_gt))
                v.sem_inc(s_flag, 1)
                wide = v.value_load(flags[0:1, layer + 1:layer + 2], min_val=0, max_val=1)
                with v.If(wide > 0):
                    v.wait_ge(s_vtab, 1)
                    true_maxima(layer, heads, wt)
                c = shift[:, :, 0:heads]
                link(v.tensor_tensor(c, ed[:, :, 0:heads], bound[:, 0:NT, 0:heads], ALU.add))
                link(v.scalar_tensor_tensor(c, c, SLOPE, c, ALU.mult, ALU.max))
                v.tensor_tensor(edc[:, 0:NT, 0:heads], ed[:, :, 0:heads], c, ALU.subtract)
                link(v.scalar_tensor_tensor(edc[:, 0:NT, heads:2 * heads], ed[:, :, 0:heads], SLOPE, c, ALU.mult, ALU.subtract))
                v.sem_inc(s_shift, 1)

            def edge_loop(layer, heads, wt):
                v.wait_ge(s_vtab, 1)

                def onehot(i, q, ahead):
                    col = i * (QB * BV) + (q + ahead) * BV
                    b = i * QB + (layer * NB + q + ahead)
                    if not (isinstance(i, int) and i * QB + q + ahead < QB):
                        v.wait_ge(s_sum, (b - QB + 1) * BV)
                    cols_ = dst_v[:, ds(col, BV)] if not isinstance(col, int) else dst_v[:, col:col + BV]
                    v.tensor_tensor(OH[:, (q + ahead) % QB, :, :], cols_.unsqueeze(2).broadcast_to([P, BV, P]),
                                    iota_p[:, :].unsqueeze(1).broadcast_to([P, BV, P]), ALU.is_equal).then_inc(s_oh, 1)

                def accumulate(i, q, ks=range(BV)):
                    for k in ks:
                        col = i * (QB * BV) + (q * BV + k)
                        ti = v.value_load(tile_v[0:1, ds(col, 1)] if not isinstance(col, int) else tile_v[0:1, col:col + 1],
                                          min_val=0, max_val=NT)
                        n = i * (QB * BV) + (layer * VIS + q * BV + k)
                        v.wait_ge(s_sum, n + 1)
                        after(v, s_acc, n)
                        a = acc[:, ds(ti, 1), 0:wt].rearrange("p o c -> p (o c)")
                        v.tensor_tensor(a, a, bank[4 + k][:, 0:wt], ALU.add).then_inc(s_acc, 1)

                def step(i, q, first=False):
                    onehot(i, q, AHEAD)
                    h, b = q % 2, i * QB + (layer * NB + q)
                    v.wait_ge(s_look, i * QB + (layer * (NB + AHEAD) + q + 1))
                    for k in range(BV):
                        v.wait_ge(s_g[q * BV + k], i * 16 + (layer * IT * 16 + 16))
                    ps = bank[2 + h][:, 0:BV * 2 * HEADS].rearrange("p (k c) -> p k c", k=BV)
                    rows = G[:, q * BV:(q + 1) * BV, :]
                    link(v.tensor_tensor(Z[:, h, :, 0:2 * heads], rows[:, :, wt:wt + 2 * heads], ps[:, :, 0:2 * heads], ALU.add))
                    v.tensor_tensor(U[:, h, :, 0:heads], Z[:, h, :, 0:heads], Z[:, h, :, heads:2 * heads], ALU.max).then_inc(s_u, 1)
                    if not first:
                        accumulate(*((i, q - 1) if q else (i - 1, QB - 1)), range(0, 2))
                    v.wait_ge(s_exp, b + 1)
                    wexp = WT[:, h, :, 0:heads]
                    if heads == 4:
                        for k in range(BV):
                            ins = v.tensor_tensor(MSG[:, h, k, 0:wt].rearrange("p (h c) -> p h c", c=CH + 1),
                                                  rows[:, k, 0:wt].rearrange("p (h c) -> p h c", c=CH + 1),
                                                  WT[:, h, k, :].unsqueeze(2).broadcast_to([P, HEADS, CH + 1]), ALU.mult)
                    else:
                        for k in range(BV):
                            ins = v.tensor_scalar(MSG[:, h, k, 0:wt], rows[:, k, 0:wt], WT[:, h, k, 0:1], None, ALU.mult)
                    ins.then_inc(s_msg, 1)
                    if not first:
                        accumulate(*((i, q - 1) if q else (i - 1, QB - 1)), range(2, BV))

                for b in range(AHEAD):
                    onehot(0, 0, b)
                for q in range(QB):
                    step(0, q, first=(q == 0))
                with v.Fori(1, IT) as i:
                    ch.enter(i, 1, QB)
                    for q in range(QB):
                        step(i, q)
                ch.leave(IT - 1)
                accumulate(IT - 1, QB - 1)
                v.wait_ge(s_acc, (layer + 1) * VIS)

            def row_stats(source, tiles=range(NT)):
                with v.Fori(tiles[0], tiles[-1] + 1) as t:
                    ins = v.bn_stats(stats[:, t, :], source(t))

            v.memset(acc[:, :, :], 0.0)
            link(v.memset(edc[:, :, :], 0.0))
            for c in range(NT // XCH):
                v.wait_ge(s_x[c], 16)
                row_stats(lambda t: xs[:, t, :], range(c * XCH, (c + 1) * XCH))
            v.wait_ge(s_x[4], 16)
            link(v.bn_stats(stats[:, NT - 1, :], xs[:, NT - 1, :]))
            combine()
            inverse_root(1)
            skewed(v, normalise(0, lambda t: xs[:, t, :]), scores_out(0, H1))
            shifts(0, H1, W1T)
            edge_loop(0, H1, W1T)

            heads_view = acc[:, 0:NT, :].rearrange("p t (h c) -> p (t h) c", c=CH + 1)
            rd = rden[:, :, :].rearrange("p t h -> p (t h)")
            link(v.tensor_scalar(rd, heads_view[:, :, CH], 1e-37, None, ALU.max))
            link(v.reciprocal(rd, rd))
            link(v.tensor_tensor(heads_view[:, :, 0:CH], heads_view[:, :, 0:CH],
                                 rd.unsqueeze(2).broadcast_to([P, NT * HEADS, CH]), ALU.mult))
            o1 = acc[:, 0:NT, :].rearrange("p t (h c) -> p t h c", c=CH + 1)[:, :, :, 0:CH]
            for h in range(HEADS):
                ins = v.tensor_tensor(o1[:, :, h, :], o1[:, :, h, :],
                                      b1r[:, h * CH:(h + 1) * CH].unsqueeze(1).broadcast_to([P, NT, CH]), ALU.add)
            link(ins)

            def o1_row(t):
                return acc[:, ds(t, 1), :].rearrange("p o (h c) -> p (o h) c", c=CH + 1)[:, :, 0:CH]
            row_stats(o1_row)
            link(v.tensor_copy(tmp_b[:, :], mean[:, :]))
            combine()
            inverse_root(2)
            v.wait_ge(s_tabw, 16 * NT)
            link(v.memset(tabs[:, :, D:D + 1], 1.0))
            v.sem_inc(s_ph, 1)

            def normalise1(t, s):
                ring(v, s_T, NT, t)
                v.tensor_scalar(xn[:, s, :].rearrange("p (h c) -> p h c", c=CH), o1_row(t), mean[:, ds(t, 1)], rstd[:, ds(t, 1)],
                                ALU.subtract, ALU.mult).then_inc(s_xn, 1)
            skewed(v, normalise1, scores_out(1, H2))
            shifts(1, H2, W2T)
            v.wait_ge(s_xn, 2 * NT)
            link(v.memset(acc[:, :, :], 0.0))
            edge_loop(1, H2, W2T)

            rd2 = rden[:, :, 0]
            link(v.tensor_scalar(rd2, acc[:, 0:NT, D], 1e-37, None, ALU.max))
            link(v.reciprocal(rd2, rd2))
            link(v.tensor_tensor(acc[:, 0:NT, 0:D], acc[:, 0:NT, 0:D], rd2.unsqueeze(2).broadcast_to([P, NT, D]), ALU.mult))
            link(v.tensor_tensor(acc[:, 0:NT, 0:D], acc[:, 0:NT, 0:D], b2r[:, :].unsqueeze(1).broadcast_to([P, NT, D]), ALU.add))
            link(v.tensor_tensor(xs[:, :, :], xs[:, :, :], acc[:, 0:NT, 0:D], ALU.add))
            row_stats(lambda t: xs[:, t, :])
            link(v.tensor_copy(tmp_b[:, :], mean[:, :]))
            combine()
            inverse_root(3)
            link(v.tensor_copy(tmp_b[:, :], rstd[:, :]))
            for _ in range(2):
                link(v.tensor_tensor(var[:, :], var[:, :], rstd[:, :], ALU.mult))
            inverse_root(4)
            link(v.tensor_tensor(rstd[:, :], rstd[:, :], tmp_b[:, :], ALU.mult))

            def normalise2(t, s):
                ring(v, s_T, 2 * NT, t)
                if not isinstance(t, int) or t >= 2:
                    v.wait_ge(s_xt[s], (t - s) * 8)
                v.tensor_scalar(xn[:, s, :], xs[:, t, :], mean[:, ds(t, 1)], rstd[:, ds(t, 1)],
                                ALU.subtract, ALU.mult).then_inc(s_xn, 1)

            def logits_out(t, s):
                v.wait_ge(s_H, 2 * NT + t + 1)
                v.tensor_copy(lg[:, t, :], bank[2 + s][:, 0:EXPERTS]).then_inc(s_HE, 1)
            skewed(v, normalise2, logits_out)
            v.wait_ge(s_HE, 3 * NT)

            def over_e(a):
                return a.unsqueeze(2).broadcast_to([P, NT, EXPERTS])
            i8 = iota_m8[:, :].unsqueeze(1).broadcast_to([P, NT, EXPERTS])
            v.tensor_scalar(iota_m8[:, :], iota_p[:, 0:EXPERTS], float(-EXPERTS), None, ALU.add)
            v.memset(valid[:, :], 1.0)
            link(v.tensor_tensor(lg[:, :, :], lg[:, :, :], brr[:, :].unsqueeze(1).broadcast_to([P, NT, EXPERTS]), ALU.add))
            link(v.tensor_scalar(valid[:, NT - 1:NT], part_f[:, :], float(LAST), None, ALU.is_lt))
            for k in range(2):
                l = (lg, lg2)[k]
                link(v.tensor_reduce(top[:, k, :], l[:, :, :], AX.X, ALU.max))
                link(v.tensor_tensor(cand[:, :, :], l[:, :, :], over_e(top[:, k, :]), ALU.is_equal))
                link(v.tensor_tensor(cand[:, :, :], cand[:, :, :], i8, ALU.mult))
                link(v.tensor_reduce(first[:, :], cand[:, :, :], AX.X, ALU.min))
                link(v.tensor_tensor(oh[:, k, :, :], over_e(first[:, :]), i8, ALU.is_equal))
                if k == 0:
                    link(v.scalar_tensor_tensor(lg2[:, :, :], oh[:, 0, :, :], -BIG, lg[:, :, :], ALU.mult, ALU.add))
            link(v.tensor_tensor(first[:, :], top[:, 1, :], top[:, 0, :], ALU.subtract))
            v.sem_inc(s_gx, 1)
            link(v.tensor_tensor(ohm[:, :, :], oh[:, 0, :, :], oh[:, 1, :, :], ALU.add))
            link(v.tensor_tensor(ohm[:, :, :], ohm[:, :, :], over_e(valid[:, :]), ALU.mult))
            v.sem_inc(s_ohm, 1)
            v.wait_ge(s_ge, 1)
            link(v.tensor_scalar(gate[:, 0, :], gate[:, 1, :], 1.0, None, ALU.add))
            link(v.reciprocal(gate[:, 0, :], gate[:, 0, :]))
            link(v.tensor_tensor(gate[:, 1, :], gate[:, 1, :], gate[:, 0, :], ALU.mult))
            v.wait_ge(s_pre, 1)
            tot = bank[5][:, 0:NT * EXPERTS].rearrange("p (t e) -> p t e", e=EXPERTS)
            for e in range(EXPERTS):
                ins = v.tensor_tensor_scan(inc[:, :, e], ones[:, 0:NT], tot[:, :, e], 0.0, ALU.mult, ALU.add)
            link(ins)
            link(v.tensor_tensor(pos_e[:, :, :], inc[:, :, :], tot, ALU.subtract))
            link(v.tensor_tensor(pos_e[:, :, :], pos_e[:, :, :], bank[4][:, 0:NT * EXPERTS].rearrange("p (t e) -> p t e", e=EXPERTS), ALU.add))
            link(v.tensor_scalar(nt_i[:, :], inc[:, NT - 1, :], float(P - 1), None, ALU.add))
            link(v.tensor_scalar(nt_i[:, :], nt_i[:, :], 7, None, ALU.arith_shift_right))
            link(v.tensor_scalar(ntf[:, :], nt_i[:, :], 1.0, None, ALU.max))
            link(v.tensor_tensor_scan(ecum[:, :], ones[:, 0:EXPERTS], ntf[:, :], 0.0, ALU.mult, ALU.add))
            link(v.tensor_tensor(ebase[:, :], ecum[:, :], ntf[:, :], ALU.subtract))
            v.tensor_copy(etab[:, 0, :], ntf[:, :])
            v.tensor_copy(etab[:, 1, :], ebase[:, :])
            link(v.tensor_scalar(ebase[:, :], ebase[:, :], float(P), None, ALU.mult))
            link(v.tensor_tensor(pos_e[:, :, :], pos_e[:, :, :], ebase[:, :].unsqueeze(1).broadcast_to([P, NT, EXPERTS]), ALU.add))
            for k in range(2):
                link(v.tensor_tensor(cand[:, :, :], oh[:, k, :, :], pos_e[:, :, :], ALU.mult))
                link(v.tensor_reduce(pos[:, k, :], cand[:, :, :], AX.X, ALU.add))
            link(v.tensor_copy(pos_i[:, :, :], pos[:, :, :]))
            v.tensor_scalar(pai[:, :, :], pos_i[:, :, :], 7, None, ALU.arith_shift_right)
            link(v.tensor_scalar(pbi[:, :, :], pos_i[:, :, :], P - 1, None, ALU.bitwise_and))
            v.tensor_copy(pa[:, :, :], pai[:, :, :])
            v.tensor_copy(pb[:, :, :], pbi[:, :, :])
            link(v.tensor_copy(cid[:, :, :], cid_i[:, :, :]))
            link(v.tensor_tensor(cid[:, :, :], cid[:, :, :], valid[:, :].unsqueeze(1).broadcast_to([P, 2, NT]), ALU.mult))

            def one_place(t, k):
                n = t * 2 + k
                if not isinstance(t, int) or t >= 1:
                    v.wait_ge(s_om, n - 1)
                v.tensor_scalar(ohb[:, k, :], iota_p[:, :], pb[:, k, ds(t, 1)], None, ALU.is_equal)
                v.tensor_scalar(oha[:, k, :], iota_p[:, 0:SLOT_TILES], pa[:, k, ds(t, 1)], cid[:, k, ds(t, 1)],
                                ALU.is_equal, ALU.mult).then_inc(s_ob, 1)
            one_place(0, 0)
            one_place(0, 1)
            with v.Fori(1, NT) as t:
                one_place(t, 0)
                one_place(t, 1)
            v.wait_ge(s_om, 2 * NT)
            link(v.tensor_scalar(slot_f[:, :], bank[6][:, 0:SLOT_TILES], -1.0, None, ALU.add))
            link(v.tensor_scalar(slot_e[:, :], slot_f[:, :], 0.0, None, ALU.is_lt))
            link(v.tensor_scalar(slot_f[:, :], slot_f[:, :], 0.0, None, ALU.max))
            v.tensor_scalar(first[:, 0:1], part_f[:, :], float(CHOICE_ROWS), None, ALU.add)
            link(v.tensor_copy(slot_g[:, :], slot_f[:, :]))
            v.tensor_copy(si[:, :], first[:, 0:1])
            link(v.tensor_scalar(slot_g[:, :], slot_g[:, :], 1, None, ALU.arith_shift_right))
            link(v.tensor_scalar(slot_e[:, :], slot_e[:, :], first[:, 0:1], None, ALU.mult))
            link(v.tensor_tensor(slot_s[:, :], slot_f[:, :], slot_e[:, :], ALU.add))
            v.sem_inc(s_slot, 1)

            def token_indices(g):
                v.tensor_copy(gi[:, :], slot_g[:, ds(g, 1)]).then_inc(s_gi, 1)

            def expert_input(n, e):
                v.wait_ge(s_xT, n + 1)
                for k in range(2):
                    ins = v.tensor_scalar(xeT[:, k, :], bank[2][:, k * P:(k + 1) * P], cols[:, ds(e * 2 + (64 + k), 1)],
                                          cols[:, ds(e * 2 + (80 + k), 1)], ALU.mult, ALU.add)
                ins.then_inc(s_xe, 1)
            v.sem_inc(s_ys, 1)
            with v.Fori(0, EXPERTS // 2) as j:
                for c in range(2):
                    e = j * 2 + c
                    n_e = v.value_load(etab[0:1, 0, ds(e, 1)], min_val=1, max_val=NT)
                    b_e = v.value_load(etab[0:1, 1, ds(e, 1)], min_val=0, max_val=MAX_TILES)
                    v.wait_ge(s_fw[c], j * 48 + 48)
                    token_indices(b_e)
                    expert_input(b_e + e, e)
                    with v.Fori(0, n_e) as i:
                        g = b_e + i
                        n = g + e + 1
                        token_indices(g + 1)
                        v.wait_ge(s_h, (g + 1) * (FC // 2))
                        expert_input(n, e)
                        v.wait_ge(s_y, g + 1)
                        v.wait_ge(s_sc, g * 16 + 16)
                        v.tensor_copy(si[:, :], slot_s[:, ds(g, 1)])
                        link2 = v.tensor_tensor(ys, bank[3][:, 0:D], fb2[:, c, :], ALU.add)
                        link2.then_inc(s_ys, 1)
                    v.wait_ge(s_ys, b_e + n_e + 1)
                    v.sem_inc(s_fwu, 1)
            total = v.value_load(etab[0:1, 1, EXPERTS - 1:EXPERTS], min_val=0, max_val=MAX_TILES)
            n_last = v.value_load(etab[0:1, 0, EXPERTS - 1:EXPERTS], min_val=1, max_val=NT)
            v.wait_ge(s_sc, (total + n_last) * 16 + 16)
            v.sem_inc(s_ph, 2)

            def one_out(t, s, j):
                v.wait_ge(s_yl[s], j * 16 + 16)
                if not isinstance(j, int) or j >= 1:
                    v.wait_ge(s_st[s], j * 16)
                r = slice(0, P)
                if isinstance(t, int) and t == NT - 1:
                    r = slice(0, LAST)
                link(v.scalar_tensor_tensor(yo[r, s, :], YL[r, s, 0:D], gate[r, 0, ds(t, 1)], xs[r, t, :], ALU.mult, ALU.add))
                v.scalar_tensor_tensor(yo2[r, s, :], YL[r, s, D:2 * D], gate[r, 1, ds(t, 1)], yo[r, s, :],
                                       ALU.mult, ALU.add).then_inc(s_o, 1)
            one_out(0, 0, 0)
            one_out(1, 1, 0)
            with v.Fori(1, NT // 2) as j:
                ch.enter(j, 1, 2)
                one_out(j * 2, 0, j)
                one_out(j * 2 + 1, 1, j)
            ch.leave(NT // 2 - 1)
            one_out(NT - 1, 0, NT // 2)


_INS = ['x', 'src', 'dst', 'L0_gnn_W1', 'L0_gnn_a1_src', 'L0_gnn_a1_dst', 'L0_gnn_b1', 'L0_gnn_ln_g', 'L0_gnn_ln_b',
        'L0_gnn_W2', 'L0_gnn_a2_src', 'L0_gnn_a2_dst', 'L0_gnn_b2', 'L0_ffn_Wr', 'L0_ffn_br', 'L0_ffn_ln_g',
        'L0_ffn_ln_b', 'L0_ffn_W1', 'L0_ffn_b1', 'L0_ffn_W2', 'L0_ffn_b2']


def edge_rows(a, spare, loops):
    rows = np.full((PAD_ROWS * P,), spare, a.dtype)
    rows[:E_IN] = a
    rows[ROWS * P:ROWS * P + LOOPS] = loops
    return rows.reshape(PAD_ROWS, P)


def kernel(**inputs):
    import concourse.bacc as bacc
    from concourse.bass_utils import run_bass_kernel_spmd as run

    nc = bacc.Bacc("TRN2", target_bir_lowering=False, num_devices=1)
    arrays, args = {}, []
    loops = np.arange(LOOPS)
    for name in _INS:
        a = np.ascontiguousarray(inputs[name])
        if name in ("src", "dst"):
            a = edge_rows(a, PAD_DST if name == "dst" else 0, loops)
        arrays[f"in_{name}"] = a
        args.append(nc.dram_tensor(f"in_{name}", a.shape, mybir.dt.from_np(a.dtype), kind="ExternalInput").ap())
    out = nc.dram_tensor("out_x", (N, D), mybir.dt.float32, kind="ExternalOutput").ap()
    build(nc, *args, out)
    result = run(nc, [arrays], core_ids=[0])
    return result.results[0]["out_x"]
```

```python
import numpy as np
import concourse.bass as bass
from concourse import mybir
from contextlib import ExitStack

P = 128
N, D = 3125, 256
HEADS, CH = 4, 64
E_IN = 53125
LOOPS = 625
EXPERTS, HID = 8, 1024
SLOPE, EPS = 0.2, 1e-5

NT = (N + P - 1) // P
LAST = N - (NT - 1) * P
NPAD = NT * P
ROWS = (E_IN + P - 1) // P
LOOP_ROWS = (LOOPS + P - 1) // P
BV = 4
VIS = 472
VC, VP = 4, VIS // 4
EMPTY_ROW = ROWS + LOOP_ROWS
PAD_ROWS = EMPTY_ROW + 1
PAD_DST = 9999
NB = VIS // BV
QB = 4
IT = NB // QB
TAIL = NB % QB
AHEAD = 3
RUN = NB + 2
VTAB = VIS + AHEAD * BV
H1, W1T, TAB1 = HEADS, HEADS * (CH + 1), HEADS * (CH + 1) + 2 * HEADS
H2, W2T, TAB2 = 1, D + 1, D + 3
SPREAD = 60.0
MAX_TILES = (2 * N + EXPERTS * (P - 1)) // P + EXPERTS - 1
SLOT_TILES = 96
CHOICE_ROWS = 2 * NPAD
FC = HID // P
XCH = 6
BIG = 3.0e38

assert (ROWS + NT - 1) + LOOP_ROWS + NT <= VIS and VIS % BV == 0 and 0 < TAIL < QB
assert MAX_TILES + NT + 1 <= SLOT_TILES

FORCE_SORT = False
FORCE_MAX = False


def build(nc, x, src, dst, g_w1, g_a1s, g_a1d, g_b1, g_lng, g_lnb, g_w2, g_a2s, g_a2d, g_b2,
          f_wr, f_br, f_lng, f_lnb, f_w1, f_b1, f_w2, f_b2, out):
    f32, i32, bf16 = mybir.dt.float32, mybir.dt.int32, mybir.dt.bfloat16
    ALU, ACT, AX = mybir.AluOpType, mybir.ActivationFunctionType, mybir.AxisListType
    RED = bass.bass_isa.ReduceOp
    ds = bass.ds

    def dram(name, shape, dt=f32):
        return nc.dram_tensor(name, shape, dt, kind="Internal").ap()

    edge_src = dram("edge_src", (PAD_ROWS * P, 1), i32)
    edge_dst = dram("edge_dst", (PAD_ROWS * P, 1), i32)
    tab1 = dram("tab1", (NPAD, TAB1))
    tab2 = dram("tab2", (NPAD, TAB2))
    xtab = dram("xtab", (NPAD, D))
    ytab = dram("ytab", (CHOICE_ROWS + P, D))

    with ExitStack() as ctx:
        def sb(name, shape, dt=f32):
            return ctx.enter_context(nc.sbuf_tensor(name, shape, dt))

        def sem(name):
            return ctx.enter_context(nc.semaphore(name))

        def sems(name, n):
            return [sem(f"{name}{k}") for k in range(n)]

        xs = sb("xs", [P, NT, D])
        tabs = sb("tabs", [P, NT, TAB1])
        acc = sb("acc", [P, NT + 1, W1T])
        G = sb("G", [P, QB * BV, TAB1])
        OH = sb("OH", [P, QB, BV, P])
        OHB = sb("OHB", [P, QB, BV, P], bf16)
        OHT = sb("OHT", [P, 2, BV * P], bf16)
        oh_flat = OH[:, :, :, :].rearrange("p q k c -> p (q k c)")
        wide = oh_flat[:, 2 * BV * P:4 * BV * P].rearrange("p (a n) -> p a n", a=2)
        ident_b = sb("ident_b", [P, P], bf16)
        MSG = sb("MSG", [P, 2, BV, W1T])
        rows_f = MSG[:, 0:1, :, :].rearrange("p a k c -> p (a k c)")[:, 0:2 * VC * P].rearrange("p (k c n) -> p k c n", k=2, c=VC)
        src_v = sb("src_v", [P, VTAB], i32)
        dst_v = sb("dst_v", [P, VTAB])
        tile_v = sb("tile_v", [1, VTAB], i32)
        IDX = sb("IDX", [P, QB, BV], i32)
        ident = sb("ident", [P, P])
        ones = sb("ones", [P, P])
        upper = sb("upper", [P, P])
        iota_p = sb("iota_p", [P, P])
        iota_i = sb("iota_i", [P, P], i32)
        part_i = sb("part_i", [P, 1], i32)
        part_f = sb("part_f", [P, 1])
        ed = sb("ed", [P, NT, HEADS])
        shift = sb("shift", [P, NT, HEADS])
        edc = sb("edc", [P, NT + 1, 2 * HEADS])
        edp = sb("edp", [P, NT + 1, 3, 2 * HEADS], bf16)
        edr = sb("edr", [P, NT + 1, 2 * HEADS])
        es_mm = sb("es_mm", [P, 2 * HEADS])
        es_all = sb("es_all", [P, 2 * HEADS])
        Z = sb("Z", [P, 2, BV, 2 * HEADS])
        U = sb("U", [P, 2, BV, HEADS])
        WT = sb("WT", [P, 2, BV, HEADS])
        xn = sb("xn", [P, 2, D])
        xnT = sb("xnT", [P, 2, 2, P])
        stats = sb("stats", [P, NT, 6])
        mean = sb("mean", [P, NT])
        rstd = sb("rstd", [P, NT])
        tmp_a = sb("tmp_a", [P, NT])
        tmp_b = sb("tmp_b", [P, NT])
        var = sb("var", [P, NT])
        root = sb("root", [P, NT])
        tmp_c = sb("tmp_c", [P, NT])
        rden = sb("rden", [P, NT, HEADS])
        w1a = sb("w1a", [P, 2, D + 2 * HEADS])
        w2a = sb("w2a", [P, 2, D + 2])
        wr = sb("wr", [P, 2, EXPERTS])
        a1 = sb("a1", [P, 2, D])
        a2 = sb("a2", [P, 2, D])
        b1r = sb("b1r", [P, D])
        b2r = sb("b2r", [P, D])
        brr = sb("brr", [P, EXPERTS])
        prod = sb("prod", [P, D])
        vecs = sb("vecs", [P, P])
        cols = sb("cols", [P, 100])
        d_i = sb("d_i", [P, ROWS], i32)
        d_t = sb("d_t", [P, ROWS], i32)
        d_b = sb("d_b", [P, ROWS], bf16)
        junk_b = sb("junk_b", [P, 2, ROWS], bf16)
        dn_i = sb("dn_i", [P, 2], i32)
        cnt = sb("cnt", [P, NT + 3])
        st = sb("st", [P, NT + 3])
        st_i = sb("st_i", [P, 2, NT], i32)
        lo_hi = sb("lo_hi", [P, 2, NT])
        nvis = sb("nvis", [P, NT])
        cum = sb("cum", [P, NT])
        off = sb("off", [P, NT])
        vnum = sb("vnum", [P, VC])
        v_i = sb("v_i", [P, VC], i32)
        ge = sb("ge", [P, VC, NT])
        vt = sb("vt", [P, VC])
        vr = sb("vr", [P, VC])
        vx = sb("vx", [P, VC])
        vy = sb("vy", [P, VC])
        vz = sb("vz", [P, VC])
        ge2 = sb("ge2", [P, VC, NT])
        nall = sb("nall", [P, NT])
        row_i = sb("row_i", [P, VC], i32)
        rows_i = sb("rows_i", [P, 2, VC, P], i32)
        flags = sb("flags", [P, 3], i32)
        fl_f = sb("fl_f", [P, HEADS])
        bound = sb("bound", [P, NT + 1, HEADS])
        max_e = sb("max_e", [P, HEADS])
        below = sb("below", [P, NT + 2])
        limit = sb("limit", [P, NT + 2])
        start = sb("start", [P, NT + 1])
        ends = sb("ends", [P, 2], i32)
        lg = sb("lg", [P, NT, EXPERTS])
        lg2 = sb("lg2", [P, NT, EXPERTS])
        oh = sb("oh", [P, 2, NT, EXPERTS])
        ohm = sb("ohm", [P, NT, EXPERTS])
        cand = sb("cand", [P, NT, EXPERTS])
        inc = sb("inc", [P, NT, EXPERTS])
        pos_e = sb("pos_e", [P, NT, EXPERTS])
        top = sb("top", [P, 2, NT])
        first = sb("first", [P, NT])
        gate = sb("gate", [P, 2, NT])
        valid = sb("valid", [P, NT])
        iota_m8 = sb("iota_m8", [P, EXPERTS])
        pos = sb("pos", [P, 2, NT])
        pos_i = sb("pos_i", [P, 2, NT], i32)
        pa = sb("pa", [P, 2, NT])
        pb = sb("pb", [P, 2, NT])
        pai = sb("pai", [P, 2, NT], i32)
        pbi = sb("pbi", [P, 2, NT], i32)
        cid = sb("cid", [P, 2, NT])
        cid_i = sb("cid_i", [P, 2, NT], i32)
        ohb = sb("ohb", [P, 2, P])
        oha = sb("oha", [P, 2, SLOT_TILES])
        nt_i = sb("nt_i", [P, EXPERTS], i32)
        ntf = sb("ntf", [P, EXPERTS])
        ecum = sb("ecum", [P, EXPERTS])
        ebase = sb("ebase", [P, EXPERTS])
        etab = sb("etab", [P, 2, EXPERTS], i32)
        slot_f = sb("slot_f", [P, SLOT_TILES])
        slot_e = sb("slot_e", [P, SLOT_TILES])
        slot_g = sb("slot_g", [P, SLOT_TILES], i32)
        slot_s = sb("slot_s", [P, SLOT_TILES], i32)
        gi = sb("gi", [P, 1], i32)
        si = sb("si", [P, 1], i32)
        fw1 = sb("fw1", [P, 2, 2, HID])
        fw2 = sb("fw2", [P, 2, FC, D])
        fb2 = sb("fb2", [P, 2, D])
        g_flat = G[:, :, :].rearrange("p s c -> p (s c)")
        m_flat = MSG[:, :, :, :].rearrange("p a k c -> p (a k c)")
        xg = m_flat[:, 0:D]
        xeT = m_flat[:, D:2 * D].rearrange("p (k n) -> p k n", k=2)
        ys = m_flat[:, 2 * D:3 * D]
        hid = oh_flat[:, 0:HID].rearrange("p (f n) -> p f n", n=P)
        YL = g_flat[:, 0:4 * D].rearrange("p (s c) -> p s c", s=2)
        yo = g_flat[:, 4 * D:6 * D].rearrange("p (s c) -> p s c", s=2)
        yo2 = g_flat[:, 6 * D:8 * D].rearrange("p (s c) -> p s c", s=2)

        bank = [ctx.enter_context(nc.psum_tensor(f"bank{k}", [P, 512], f32)) for k in range(8)]
        bankb = [bank[k][:, :].bitcast(bf16)[:, 0:BV * P] for k in range(2)]

        HB = (0, 1, 4, 5)

        s_x = sems("x_loaded", 5)
        s_dst = sem("dst_loaded")
        s_dn = sem("dst_next_loaded")
        s_copy = sem("edges_copied")
        s_w = sem("graph_weights_loaded")
        s_vec = sem("vectors_loaded")
        s_pool = sem("pool_constants")
        s_zero = sem("tail_zeroed")
        s_dve = sem("dve_chain")
        s_cnt = sem("counts_ready")
        s_starts = sem("starts_summed")
        s_rows = sem("visit_rows_ready")
        s_tilt = sem("visit_tiles_on_one_row")
        s_rg = sem("edge_rows_gathered")
        s_rf = sem("edge_rows_as_float")
        s_rT = sem("edge_rows_transposed")
        s_vtab = sem("visit_tables_ready")
        s_vecT = sem("vectors_transposed")
        s_xn = sem("xn_ready")
        s_T = sem("tile_transposed")
        s_TS = sem("transposed_tile_in_sbuf")
        s_H = sem("tile_projected")
        s_HS = sem("projection_in_sbuf")
        s_HE = sem("scores_in_sbuf")
        s_tabw = sem("table_written")
        s_mm = sem("local_extremes")
        s_ar = sem("global_extremes")
        s_shift = sem("shifts_ready")
        s_oh = sem("onehot_ready")
        s_ohf = sem("onehot_in_float32")
        s_ohT = sem("onehot_transposed")
        s_ohS = sem("onehot_T_in_sbuf")
        s_look = sem("destination_scores_looked_up")
        s_u = sem("exponents_ready")
        s_exp = sem("weights_ready")
        s_msg = sem("messages_ready")
        s_idx = sem("indices_ready")
        s_grant = sem("gather_granted")
        s_sum = sem("messages_summed")
        s_acc = sem("sums_accumulated")
        s_g = sems("row_gathered", QB * BV)
        s_lg = sem("logits_ready")
        s_gx = sem("gate_exponent_ready")
        s_ge = sem("gate_exp_done")
        s_ohm = sem("choices_ready")
        s_pre = sem("ranks_ready")
        s_ob = sem("slot_onehot_ready")
        s_om = sem("slot_onehot_used")
        s_slot = sem("slots_ready")
        s_xt = sems("tokens_written", 2)
        s_fw = sems("expert_weights_loaded", 2)
        s_fwu = sem("expert_weights_used")
        s_begun = sem("expert_begun")
        s_gi = sem("token_indices_ready")
        s_gig = sem("token_gather_granted")
        s_xg = sem("tokens_gathered")
        s_xT = sem("tokens_transposed")
        s_xe = sem("expert_input_ready")
        s_h = sem("hidden_ready")
        s_hg = sem("hidden_activated")
        s_y = sem("expert_output_ready")
        s_ys = sem("expert_output_in_sbuf")
        s_sc = sem("results_scattered")
        s_yl = sems("results_loaded", 2)
        s_o = sem("output_ready")
        s_st = sems("output_stored", 2)
        s_var = sem("variances_ready")
        s_root = sem("roots_ready")
        s_ph = sem("phase_over")
        s_clear = sem("sums_cleared")
        s_flag = sem("flags_ready")
        s_below = sem("edges_before_summed")
        s_kept = sem("destinations_kept")
        s_src = sem("sources_loaded")
        s_sort = sem("sort_chain")
        s_place = sem("edge_place_ready")
        s_moved = sem("edge_moved")
        s_mi = sems("max_source_ready", 2)
        s_mg = sems("max_row_gathered", 2)
        s_md = sems("max_operands_ready", 2)
        s_mt = sems("max_scores_spread", 2)
        s_mc = sems("max_chain", 2)

        class Chain:
            def __init__(self, eng, sem_):
                self.eng, self.sem, self.n, self.i = eng, sem_, 0, None

            def link(self, ins):
                self.n += 1
                ins.then_inc(self.sem, 1)
                at = self.n if self.i is None else self.i * self.per + (self.n - self.first * self.per)
                self.eng.wait_ge(self.sem, at)

            def enter(self, i, first, per):
                self.i, self.first, self.per, self.start = i, first, per, self.n

            def leave(self, passes):
                assert self.n - self.start == self.per, (self.n - self.start, self.per)
                self.n = self.start + self.per * passes
                self.i = None

        def for_tiles(eng, body, chain=None, per=0):
            body(0, 0)
            body(1, 1)
            with eng.Fori(1, NT // 2) as j:
                if chain:
                    chain.enter(j, 1, 2 * per)
                t = j * 2
                body(t, 0)
                body(t + 1, 1)
            if chain:
                chain.leave(NT // 2 - 1)
            body(NT - 1, 0)

        def after(eng, sem_, value):
            if not isinstance(value, int) or value > 0:
                eng.wait_ge(sem_, value)

        def ring(eng, sem_, base, t):
            if not isinstance(t, int) or t >= 2:
                eng.wait_ge(sem_, base + t - 1)

        def for_tiles_but_last(eng, body):
            body(0, 0)
            body(1, 1)
            with eng.Fori(1, NT // 2) as j:
                t = j * 2
                body(t, 0)
                body(t + 1, 1)

        def skewed(eng, lead, follow):
            lead(0, 0)
            lead(1, 1)
            follow(0, 0)
            lead(2, 0)
            follow(1, 1)
            with eng.Fori(1, NT // 2) as j:
                t = j * 2
                lead(t + 1, 1)
                follow(t, 0)
                lead(t + 2, 0)
                follow(t + 1, 1)
            follow(NT - 1, 0)

        def skewed_by_two(eng, lead, follow):
            for t in range(3):
                lead(t, t % 2)
            follow(0, 0)
            lead(3, 1)
            follow(1, 1)
            with eng.Fori(1, NT // 2 - 1) as j:
                t = j * 2
                for k in range(2):
                    lead(t + (2 + k), k)
                    follow(t + k, k)
            lead(NT - 1, 0)
            for t in range(NT - 3, NT):
                follow(t, t % 2)

        block = ctx.enter_context(nc.Block())

        @block.sync
        def _(sp):
            sp.dma_start(d_i[:, :], dst[0:ROWS, :].rearrange("r c -> (r c)").rearrange("(p j) -> p j", p=P)).then_inc(s_dst, 16)
            for c in range(NT // XCH):
                sp.dma_start(xs[:, c * XCH:(c + 1) * XCH, :],
                             x[c * XCH * P:(c + 1) * XCH * P, :].rearrange("(t p) d -> p t d", p=P)).then_inc(s_x[c], 16)
            sp.wait_ge(s_zero, 2)
            sp.dma_start(xs[0:LAST, NT - 1, :], x[(NT - 1) * P:N, :]).then_inc(s_x[4], 16)
            for c in range(2):
                sp.dma_start(fw1[:, c, :, :], f_w1[c].rearrange("(k p) n -> p k n", p=P)).then_inc(s_fw[c], 16)
                sp.dma_start(fw2[:, c, :, :], f_w2[c].rearrange("(k p) n -> p k n", p=P)).then_inc(s_fw[c], 16)
                sp.dma_start(fb2[:, c, :], f_b2[c:c + 1, :].partition_broadcast(P)).then_inc(s_fw[c], 16)

            for layer, (tab, width) in enumerate(((tab1, TAB1), (tab2, TAB2))):
                def write_tab(t):
                    sp.wait_ge(s_HS, layer * NT + t + 1)
                    sp.wait_ge(s_HE, layer * NT + t + 1)
                    sp.dma_start(tab[ds(t * P, P), :], tabs[:, t, 0:width]).then_inc(s_tabw, 16)
                with sp.Fori(0, NT) as t:
                    write_tab(t)
            def write_tokens(t, s):
                sp.wait_ge(s_xn, 2 * NT + t + 1)
                sp.dma_start(xtab[ds(t * P, P), :], xn[:, s, :]).then_inc(s_xt[s], 16)
            for_tiles(sp, write_tokens)
            with sp.Fori(1, EXPERTS // 2) as j:
                for c in range(2):
                    e = j * 2 + c
                    sp.wait_ge(s_fwu, e - 1)
                    sp.dma_start(fw1[:, c, :, :], f_w1[ds(e, 1)].rearrange("o (k p) n -> p (o k) n", p=P)).then_inc(s_fw[c], 16)
                    sp.dma_start(fw2[:, c, :, :], f_w2[ds(e, 1)].rearrange("o (k p) n -> p (o k) n", p=P)).then_inc(s_fw[c], 16)
                    sp.dma_start(fb2[:, c, :], f_b2[ds(e, 1), :].partition_broadcast(P)).then_inc(s_fw[c], 16)
            sp.wait_ge(s_ph, 5)
            ypair = ytab[0:CHOICE_ROWS, :].rearrange("(n k) d -> n (k d)", k=2)

            def load(t, s):
                ring(sp, s_o, 0, t)
                sp.dma_start(YL[:, s, :], ypair[ds(t * P, P), :]).then_inc(s_yl[s], 16)
            for_tiles_but_last(sp, load)
            sp.wait_ge(s_o, NT - 2)
            sp.dma_start(YL[0:LAST, 0, :], ypair[(NT - 1) * P:N, :]).then_inc(s_yl[0], 16)

        @block.gpsimd
        def _(pool):
            pool.memset(ident[:, :], 0.0).then_inc(s_pool, 1)
            pool.memset(ones[:, :], 1.0).then_inc(s_pool, 1)
            pool.iota(iota_i[:, :], [[1, P]], base=0, channel_multiplier=0).then_inc(s_pool, 1)
            pool.iota(part_i[:, :], [[1, 1]], base=0, channel_multiplier=1).then_inc(s_pool, 1)
            pool.iota(v_i[:, :], [[VP, VC]], base=0, channel_multiplier=1).then_inc(s_pool, 1)
            pool.iota(cid_i[:, :, :], [[1, 2], [2 * P, NT]], base=1, channel_multiplier=2).then_inc(s_pool, 1)
            pool.wait_ge(s_pool, 6)
            pool.affine_select(out=ident[:, :], in_=ident[:, :], compare_op=ALU.not_equal, fill=1.0,
                               base=0, pattern=[[-1, P]], channel_multiplier=1).then_inc(s_pool, 1)
            pool.affine_select(out=upper[:, :], in_=ones[:, :], compare_op=ALU.is_gt, fill=0.0,
                               base=0, pattern=[[1, P]], channel_multiplier=-1).then_inc(s_pool, 1)
            pool.wait_ge(s_flag, 1)
            unsorted = pool.value_load(flags[0:1, 0:1], min_val=0, max_val=1)
            pool.wait_ge(s_copy, 32)
            with pool.If(unsorted > 0):
                pool.wait_ge(s_kept, 1)
                pool.dma_start(d_i[:, :], src[0:ROWS, :].rearrange("r c -> (r c)").rearrange("(p j) -> p j", p=P)).then_inc(s_src, 16)
                with pool.Fori(0, ROWS) as j:
                    pool.wait_ge(s_place, j + 1)
                    pool.sem_inc(s_grant, 1)
                    for k, tab in enumerate((edge_src, edge_dst)):
                        pool.indirect_dma_start(tab, bass.IndirectOffsetOnAxis(gi[:, 0:1], 0), ends[:, k:k + 1], None
                                                ).then_inc(s_moved, 16)
                pool.wait_ge(s_moved, 32 * ROWS)
            pool.wait_ge(s_rows, 1)
            for k, tab in enumerate((edge_src, edge_dst)):
                for c in range(VC):
                    pool.indirect_dma_start(rows_i[0:VP, k, c, :], None, tab.rearrange("(r c) o -> r (c o)", c=P),
                                            bass.IndirectOffsetOnAxis(row_i[0:VP, c:c + 1], 0)).then_inc(s_rg, 16)
            for layer, (tab, width, heads) in enumerate(((tab1, TAB1, H1), (tab2, TAB2, H2))):
                if layer == 1:
                    pool.wait_ge(s_xn, 2 * NT)
                pool.memset(acc[:, :, :], 0.0).then_inc(s_clear, 1)
                pool.wait_ge(s_mm, layer + 1)
                pool.partition_all_reduce(es_all[:, 0:2 * heads], es_mm[:, 0:2 * heads], P, RED.max).then_inc(s_ar, 1)
                pool.wait_ge(s_tabw, 16 * NT * (layer + 1))
                pool.wait_ge(s_flag, layer + 2)
                wide_spread = pool.value_load(flags[0:1, layer + 1:layer + 2], min_val=0, max_val=1)
                with pool.If(wide_spread > 0):
                    with pool.Fori(0, VIS) as n:
                        pool.wait_ge(s_mi[layer], n + 1)
                        pool.sem_inc(s_grant, 1)
                        pool.indirect_dma_start(G[:, 0, 0:width], None, tab, bass.IndirectOffsetOnAxis(gi[:, 0:1], 0)
                                                ).then_inc(s_mg[layer], 16)
                    pool.wait_ge(s_mg[layer], 16 * VIS)
                    pool.wait_ge(s_mt[layer], VIS)
                def gather_batch(i, q):
                    pool.wait_ge(s_idx, i * QB + (layer * NB + q + 1))
                    pool.sem_inc(s_grant, 1)
                    for k in range(BV):
                        pool.indirect_dma_start(G[:, q * BV + k, 0:width], None, tab,
                                                bass.IndirectOffsetOnAxis(IDX[:, q, k:k + 1], 0)
                                                ).then_inc(s_g[q * BV + k], 16)
                with pool.Fori(0, IT) as i:
                    for q in range(QB):
                        gather_batch(i, q)
                for q in range(TAIL):
                    gather_batch(IT, q)
            pool.wait_ge(s_xt[0], 16 * (NT // 2 + 1))
            pool.wait_ge(s_xt[1], 16 * (NT // 2))
            pool.wait_ge(s_slot, 1)

            def gather_tokens(g):
                pool.wait_ge(s_gi, g + 1)
                pool.sem_inc(s_gig, 1)
                pool.indirect_dma_start(xg, None, xtab, bass.IndirectOffsetOnAxis(gi[:, 0:1], 0)).then_inc(s_xg, 16)

            def scatter_results(n):
                pool.wait_ge(s_ys, n + 1)
                pool.sem_inc(s_gig, 1)
                pool.indirect_dma_start(ytab, bass.IndirectOffsetOnAxis(si[:, 0:1], 0), ys, None).then_inc(s_sc, 16)

            gather_tokens(0)
            with pool.Fori(0, EXPERTS) as e:
                n_e = pool.value_load(etab[0:1, 0, ds(e, 1)], min_val=1, max_val=NT)
                b_e = pool.value_load(etab[0:1, 1, ds(e, 1)], min_val=0, max_val=MAX_TILES)
                with pool.Fori(0, n_e) as i:
                    gather_tokens(b_e + i + 1)
                    scatter_results(b_e + i)
            b_e = pool.value_load(etab[0:1, 1, EXPERTS - 1:EXPERTS], min_val=0, max_val=MAX_TILES)
            n_e = pool.value_load(etab[0:1, 0, EXPERTS - 1:EXPERTS], min_val=1, max_val=NT)
            scatter_results(b_e + n_e)

        @block.scalar
        def _(act):
            act.dma_start(edge_src.rearrange("(r c) o -> r (c o)", c=P), src).then_inc(s_copy, 16)
            act.dma_start(edge_dst.rearrange("(r c) o -> r (c o)", c=P), dst).then_inc(s_copy, 16)
            act.wait_ge(s_zero, 2)
            act.dma_start(dn_i[0:P - 1, :], dst[0:ROWS, :].rearrange("r c -> (r c)").rearrange("(p j) -> p j", p=P)[1:P, 0:2]).then_inc(s_dn, 16)
            act.dma_start(w1a[:, :, 0:D], g_w1.rearrange("(k p) n -> p k n", p=P)).then_inc(s_w, 16)
            for k, a in enumerate((g_a1s, g_a1d)):
                act.dma_start(a1[:, k, :], a.rearrange("h c -> (h c)").unsqueeze(0).partition_broadcast(P)).then_inc(s_w, 16)
            act.dma_start(w2a[:, :, 0:D], g_w2.rearrange("(k p) n -> p k n", p=P)).then_inc(s_w, 16)
            for k, a in enumerate((g_a2s, g_a2d)):
                act.dma_start(a2[:, k, :], a.partition_broadcast(P)).then_inc(s_w, 16)
            act.dma_start(wr[:, :, :], f_wr.rearrange("(k p) n -> p k n", p=P)).then_inc(s_w, 16)
            act.dma_start(b1r[:, :], g_b1.unsqueeze(0).partition_broadcast(P)).then_inc(s_w, 16)
            act.dma_start(b2r[:, :], g_b2.unsqueeze(0).partition_broadcast(P)).then_inc(s_w, 16)
            act.dma_start(brr[:, :], f_br.unsqueeze(0).partition_broadcast(P)).then_inc(s_w, 16)
            r = 0
            for v in (f_b1, f_lng, f_lnb):
                n = v.shape[0] * v.shape[1] // P
                act.dma_start(vecs[r:r + n, :], v.rearrange("e (c p) -> (e c) p", p=P)).then_inc(s_vec, 16)
                r += n
            for v in (g_lng, g_lnb):
                act.dma_start(vecs[r:r + 2, :], v.rearrange("(c p) -> c p", p=P)).then_inc(s_vec, 16)
                r += 2

            def roots(n):
                act.wait_ge(s_var, n)
                act.activation(root[:, :], tmp_a[:, :], ACT.Sqrt).then_inc(s_root, 1)

            for layer, heads in enumerate((H1, H2)):
                nb = layer * NT
                roots(layer + 1)
                def put_T(t, s):
                    act.wait_ge(s_T, nb + t + 1)
                    ring(act, s_H, nb, t)
                    psT = bank[s][:, 0:D].rearrange("p (k n) -> p k n", k=2)
                    if layer == 0:
                        act.activation(xnT[:, s, :, :], psT, ACT.Copy).then_inc(s_TS, 1)
                    else:
                        for k in range(2):
                            ins = act.activation(xnT[:, s, k, :], psT[:, k, :], ACT.Relu,
                                                 scale=cols[:, 96 + k:97 + k], bias=cols[:, 98 + k:99 + k])
                        ins.then_inc(s_TS, 1)

                def put_H(t, s):
                    act.wait_ge(s_HE, nb + t + 1)
                    if layer == 0:
                        row = tabs[:, t, 0:W1T].rearrange("p (h c) -> p h c", c=CH + 1)[:, :, 0:CH]
                        act.activation(row, bank[2 + s][:, 0:D].rearrange("p (h c) -> p h c", c=CH), ACT.Copy).then_inc(s_HS, 1)
                    else:
                        act.activation(tabs[:, t, 0:D], bank[2 + s][:, 0:D], ACT.Copy).then_inc(s_HS, 1)
                if layer == 1:
                    act.wait_ge(s_vecT, 2)
                    act.wait_ge(s_tabw, 16 * NT)
                skewed(act, put_T, put_H)

                def local(i, q):
                    return i * QB + q if isinstance(i, int) else None

                def put_onehot_T(i, q):
                    if local(i, q) is None or local(i, q) < RUN:
                        b = i * QB + (layer * RUN + q)
                        act.wait_ge(s_ohT, b + 1)
                        after(act, s_look, b - 1)
                        act.activation(OHT[:, q % 2, :], bankb[q % 2], ACT.Copy).then_inc(s_ohS, 1)

                def put_onehot(i, q):
                    if local(i, q) is None or local(i, q) < NB:
                        act.wait_ge(s_oh, i * QB + (layer * RUN + q + 1))
                        if local(i, q) is None or local(i, q) >= QB:
                            act.wait_ge(s_sum, (i * QB + (layer * NB + q) - QB + 1) * 2)
                        act.activation(OH[:, q % QB, :, :], OHB[:, q % QB, :, :], ACT.Copy).then_inc(s_ohf, 1)

                def put_indices(i, q):
                    if local(i, q) is None or local(i, q) < NB:
                        col = i * (QB * BV) + q * BV
                        act.activation(IDX[:, q % QB, :], src_v[:, ds(col, BV)] if not isinstance(col, int) else src_v[:, col:col + BV],
                                       ACT.Copy).then_inc(s_idx, 1)

                def weights(i, q):
                    if local(i, q) is None or local(i, q) < NB:
                        act.wait_ge(s_u, i * QB + (layer * NB + q + 1))
                        act.activation(WT[:, q % 2, :, 0:heads], U[:, q % 2, :, 0:heads], ACT.Exp).then_inc(s_exp, 1)

                if layer == 0:
                    act.wait_ge(s_vtab, 1)
                after(act, s_msg, layer * NB)
                for q in range(3):
                    put_indices(0, q)
                for q in range(AHEAD):
                    put_onehot_T(0, q)
                weights(0, 0)
                put_onehot(0, 0)

                def body(i, batches=QB):
                    for q in range(batches):
                        after(act, s_msg, i * QB + (layer * NB + q))
                        put_indices(i, q + 3)
                        weights(i, q + 1)
                        put_onehot(i, q + 1)
                        put_onehot_T(i, q + AHEAD)
                body(0)
                with act.Fori(1, IT - 1) as i:
                    body(i)
                body(IT - 1)
                body(IT, TAIL)

            roots(3)
            roots(4)
            def put_T3(t, s):
                act.wait_ge(s_T, 2 * NT + t + 1)
                ring(act, s_H, 2 * NT, t)
                act.activation(xnT[:, s, :, :], bank[s][:, 0:D].rearrange("p (k n) -> p k n", k=2), ACT.Copy).then_inc(s_TS, 1)
            for_tiles(act, put_T3)
            act.wait_ge(s_gx, 1)
            act.activation(gate[:, 1, :], first[:, :], ACT.Exp).then_inc(s_ge, 1)

            act.wait_ge(s_slot, 1)
            with act.Fori(0, EXPERTS // 2) as j:
                for c in range(2):
                    e = j * 2 + c
                    n_e = act.value_load(etab[0:1, 0, ds(e, 1)], min_val=1, max_val=NT)
                    b_e = act.value_load(etab[0:1, 1, ds(e, 1)], min_val=0, max_val=MAX_TILES)
                    with act.Fori(0, n_e) as i:
                        for f in range(FC):
                            if f % 2 == 0:
                                act.wait_ge(s_h, (b_e + i) * (FC // 2) + (f // 2 + 1))
                            act.activation(hid[:, f, :], bank[HB[f // 2]][:, (f % 2) * P:(f % 2 + 1) * P], ACT.Gelu,
                                           bias=cols[:, ds(e * FC + f, 1)]).then_inc(s_hg, 1)
            def store(t, s):
                act.wait_ge(s_o, t + 1)
                act.dma_start(out[ds(t * P, P), :], yo2[:, s, :]).then_inc(s_st[s], 16)
            for_tiles_but_last(act, store)
            act.wait_ge(s_o, NT)
            act.dma_start(out[(NT - 1) * P:N, :], yo2[0:LAST, 0, :]).then_inc(s_st[0], 16)
            act.wait_ge(s_st[0], 16 * (NT // 2 + 1))
            act.wait_ge(s_st[1], 16 * (NT // 2))

        @block.tensor
        def _(pe):
            pe.wait_ge(s_pool, 8)
            pe.wait_ge(s_cnt, 1)
            pe.matmul(bank[4][:, 0:NT + 3], ones[:, :], cnt[:, :], start=True, stop=True).then_inc(s_starts, 1)
            pe.matmul(bank[3][:, 0:NT + 1], upper[:, :], cnt[:, 0:NT + 1], start=True, stop=True).then_inc(s_below, 1)
            pe.wait_ge(s_vec, 16 * 5)
            pe.transpose(bank[5][:, 0:100], vecs[0:100, :], ident[0:100, 0:100]).then_inc(s_vecT, 1)
            pe.wait_ge(s_rows, 1)
            for c in range(VC):
                ins = pe.matmul(bank[4][0:1, c * VP:(c + 1) * VP], vt[0:VP, c:c + 1], ident[0:VP, 0:VP], start=True, stop=True)
            ins.then_inc(s_tilt, 1)
            pe.wait_ge(s_rf, 1)
            for k in range(2):
                for c in range(VC):
                    ins = pe.transpose(bank[6 + k][:, c * VP:(c + 1) * VP], rows_f[0:VP, k, c, :], ident[0:VP, 0:VP])
            ins.then_inc(s_rT, 1)

            def node_phase(ph, rhs, width):
                nb = ph * NT

                def T(t, s):
                    pe.wait_ge(s_xn, nb + t + 1)
                    ring(pe, s_TS, nb, t)
                    for k in range(2):
                        ins = pe.transpose(bank[s][:, k * P:(k + 1) * P], xn[:, s, k * P:(k + 1) * P], ident[:, :])
                    ins.then_inc(s_T, 1)

                def Hm(t, s):
                    pe.wait_ge(s_TS, nb + t + 1)
                    if ph < 2:
                        ring(pe, s_HS, nb, t)
                    ring(pe, s_HE, nb, t)
                    for k in range(2):
                        ins = pe.matmul(bank[2 + s][:, 0:width], xnT[:, s, k, :], rhs[:, k, :], start=(k == 0), stop=(k == 1))
                    ins.then_inc(s_H, 1)
                skewed(pe, T, Hm)

            for layer, (rhs, heads, width) in enumerate(((w1a, H1, W1T), (w2a, H2, W2T))):
                node_phase(layer, rhs, D + 2 * heads)

                def transpose_onehot(i, q):
                    if isinstance(i, int) and i * QB + q >= RUN:
                        return
                    b = i * QB + (layer * RUN + q)
                    pe.wait_ge(s_oh, b + 1)
                    after(pe, s_ohS, b - 1)
                    for k in range(BV):
                        ins = pe.transpose(bankb[q % 2][:, k * P:(k + 1) * P], OHB[:, q % QB, k, :], ident_b[:, :])
                    ins.then_inc(s_ohT, 1)

                def look_up(i, q):
                    b = i * QB + (layer * RUN + q)
                    pe.wait_ge(s_ohS, b + 1)
                    if not (isinstance(i, int) and i * QB + q < 2):
                        pe.wait_ge(s_u, i * QB + (layer * NB + q - 1))
                    for m in range(BV // 2):
                        col = i * (QB * BV) + (q * BV + 2 * m)
                        ti = pe.value_load(tile_v[0:1, ds(col, 1)] if not isinstance(col, int) else tile_v[0:1, col:col + 1],
                                           min_val=0, max_val=NT)
                        parts = edp[:, ds(ti, 1), :, :]
                        for k in (2 * m, 2 * m + 1):
                            ins = pe.matmul(bank[2 + q % 2][:, k * 6 * HEADS:(k + 1) * 6 * HEADS],
                                            OHT[:, q % 2, k * P:(k + 1) * P], parts, start=True, stop=True)
                    ins.then_inc(s_look, 1)

                def sum_messages(i, q):
                    b = i * QB + (layer * NB + q)
                    pe.wait_ge(s_ohf, b + 1)
                    pe.wait_ge(s_msg, b + 1)
                    after(pe, s_acc, (b - 1) * 2)
                    for k in range(BV):
                        ins = pe.matmul(bank[4 + (q % 2) * 2 + k // 2][:, 0:width], OH[:, q, k, :], MSG[:, q % 2, k, 0:width],
                                        start=(k % 2 == 0), stop=(k % 2 == 1))
                        if k % 2:
                            ins.then_inc(s_sum, 1)

                pe.wait_ge(s_flag, layer + 2)
                wide_spread = pe.value_load(flags[0:1, layer + 1:layer + 2], min_val=0, max_val=1)
                with pe.If(wide_spread > 0):
                    with pe.Fori(0, VIS) as n:
                        pe.wait_ge(s_md[layer], n + 1)
                        pe.transpose(bank[0][:, 0:P], OH[:, 0, 0, :], ident[:, :])
                        pe.matmul(bank[1][:, 0:heads * P], ones[:, :], wide[:, 0, 0:heads * P], start=True, stop=True
                                  ).then_inc(s_mt[layer], 1)
                pe.wait_ge(s_shift, layer + 1)
                transpose_onehot(0, 0)
                transpose_onehot(0, 1)
                look_up(0, 0)
                transpose_onehot(0, 2)
                look_up(0, 1)

                def body(i, batches=QB):
                    for q in range(batches):
                        look_up(i, q + 2)
                        transpose_onehot(i, q + AHEAD)
                        sum_messages(i, q)
                body(0)
                with pe.Fori(1, IT) as i:
                    body(i)
                body(IT, TAIL)

            node_phase(2, wr, EXPERTS)
            pe.wait_ge(s_ohm, 1)
            m = ohm[:, :, :].rearrange("p t e -> p (t e)")
            pe.matmul(bank[4][:, 0:NT * EXPERTS], upper[:, :], m, start=True, stop=True)
            pe.matmul(bank[5][:, 0:NT * EXPERTS], ones[:, :], m, start=True, stop=True).then_inc(s_pre, 1)

            def place(n, s, t_first, t_last):
                pe.wait_ge(s_ob, n + 1)
                pe.matmul(bank[6][:, 0:SLOT_TILES], ohb[:, s, :], oha[:, s, :], start=t_first, stop=t_last).then_inc(s_om, 1)
            place(0, 0, True, False)
            place(1, 1, False, False)
            with pe.Fori(1, NT - 1) as t:
                for k in range(2):
                    place(t * 2 + k, k, False, False)
            place(2 * NT - 2, 0, False, False)
            place(2 * NT - 1, 1, False, True)

            def tokens_T(g):
                pe.wait_ge(s_xg, g * 16 + 16)
                for k in range(2):
                    ins = pe.transpose(bank[2][:, k * P:(k + 1) * P], xg[:, k * P:(k + 1) * P], ident[:, :])
                ins.then_inc(s_xT, 1)

            pe.wait_ge(s_slot, 1)
            tokens_T(0)
            with pe.Fori(0, EXPERTS // 2) as j:
                for c in range(2):
                    e = j * 2 + c
                    n_e = pe.value_load(etab[0:1, 0, ds(e, 1)], min_val=1, max_val=NT)
                    b_e = pe.value_load(etab[0:1, 1, ds(e, 1)], min_val=0, max_val=MAX_TILES)
                    pe.wait_ge(s_fw[c], j * 48 + 48)
                    pe.sem_inc(s_begun, 1)
                    with pe.Fori(0, n_e) as i:
                        g = b_e + i
                        pe.wait_ge(s_xe, g + 1)
                        for f in range(FC):
                            for k in range(2):
                                ins = pe.matmul(bank[HB[f // 2]][:, (f % 2) * P:(f % 2 + 1) * P],
                                                fw1[:, c, k, f * P:(f + 1) * P], xeT[:, k, :], start=(k == 0), stop=(k == 1))
                            if f % 2:
                                ins.then_inc(s_h, 1)
                        tokens_T(g + 1)
                        pe.wait_ge(s_ys, g + 1)
                        for f in range(FC):
                            pe.wait_ge(s_hg, g * FC + (f + 1))
                            ins = pe.matmul(bank[3][:, 0:D], hid[:, f, :], fw2[:, c, f, :], start=(f == 0), stop=(f == FC - 1))
                        ins.then_inc(s_y, 1)

        @block.vector
        def _(v):
            ch = Chain(v, s_dve)
            link = ch.link

            def sort_edges():
                so = Chain(v, s_sort)
                v.wait_ge(s_below, 1)
                v.tensor_copy(below[:, 0:NT + 1], bank[3][:, 0:NT + 1])
                so.link(v.tensor_scalar(below[:, NT + 1:NT + 2], part_f[:, :], float(ROWS), None, ALU.mult))
                v.tensor_scalar(limit[:, :], iota_p[:, 0:NT + 2], float(P), None, ALU.mult)
                so.link(v.tensor_tensor(start[:, :], below[:, 1:NT + 2], below[:, 0:NT + 1], ALU.subtract))
                so.link(v.scalar_tensor_tensor(start[:, :], start[:, :], -1.0, st[:, 0:NT + 1], ALU.add, ALU.add))
                place, inside, rank, all_ones, d_f, junk = (tabs[:, 2 * k:2 * k + 2, :].rearrange("p t c -> p (t c)")[:, 0:ROWS]
                                                            for k in range(6))
                so.link(v.tensor_copy(d_f, d_i[:, :]))
                v.sem_inc(s_kept, 1)
                v.memset(all_ones, 1.0)
                so.link(v.memset(limit[:, NT + 1:NT + 2], 10.0 * PAD_DST))
                so.link(v.memset(place, 0.0))
                with v.Fori(0, NT + 1) as t:
                    so.enter(t, 0, 5)
                    so.link(v.tensor_scalar(junk, d_f, limit[:, ds(t + 1, 1)], None, ALU.is_lt))
                    so.link(v.scalar_tensor_tensor(inside, d_f, limit[:, ds(t, 1)], junk, ALU.is_ge, ALU.mult))
                    so.link(v.tensor_tensor_scan(rank, all_ones, inside, 0.0, ALU.mult, ALU.add))
                    so.link(v.scalar_tensor_tensor(rank, rank, start[:, ds(t, 1)], inside, ALU.add, ALU.mult))
                    so.link(v.tensor_tensor(place, place, rank, ALU.add))
                so.leave(NT + 1)
                v.wait_ge(s_src, 16)

                def move(j):
                    v.tensor_copy(gi[:, :], place[:, ds(j, 1)] if not isinstance(j, int) else place[:, j:j + 1])
                    v.tensor_copy(ends[:, 0:1], d_i[:, ds(j, 1)])
                    v.tensor_copy(ends[:, 1:2], d_f[:, ds(j, 1)]).then_inc(s_place, 1)
                move(0)
                with v.Fori(1, ROWS) as j:
                    v.wait_ge(s_moved, j * 32)
                    move(j)
                v.wait_ge(s_moved, ROWS * 32)

            def true_maxima(layer, heads, wt):
                mc = Chain(v, s_mc[layer])
                least = es_all[:, heads:2 * heads].unsqueeze(1).broadcast_to([P, NT + 1, heads])
                mc.link(v.tensor_scalar(bound[:, :, 0:heads], least, -1.0, None, ALU.mult))
                spread = wide[:, 0, 0:heads * P].rearrange("p (h e) -> p h e", h=heads)
                with v.Fori(0, VIS) as n:
                    mc.enter(n, 0, 5)
                    v.tensor_copy(gi[:, :], src_v[:, ds(n, 1)]).then_inc(s_mi[layer], 1)
                    v.tensor_scalar(OH[:, 0, 0, :], iota_p[:, :], dst_v[:, ds(n, 1)], None, ALU.is_equal)
                    v.wait_ge(s_mg[layer], n * 16 + 16)
                    for h in range(heads):
                        ins = v.tensor_scalar(spread[:, h, :], ident[:, :], G[:, 0, wt + h:wt + h + 1], None, ALU.mult)
                    mc.link(ins)
                    v.sem_inc(s_md[layer], 1)
                    v.wait_ge(s_mt[layer], n + 1)
                    mc.link(v.tensor_scalar(wide[:, 1, 0:P], bank[0][:, 0:P], 1e30, -1e30, ALU.mult, ALU.add))
                    mc.link(v.tensor_tensor(spread, bank[1][:, 0:heads * P].rearrange("p (h e) -> p h e", h=heads),
                                            wide[:, 1, 0:P].unsqueeze(1).broadcast_to([P, heads, P]), ALU.add))
                    mc.link(v.tensor_reduce(max_e[:, 0:heads], spread, AX.X, ALU.max))
                    ti = v.value_load(tile_v[0:1, ds(n, 1)], min_val=0, max_val=NT)
                    b = bound[:, ds(ti, 1), 0:heads].rearrange("p o h -> p (o h)")
                    mc.link(v.tensor_tensor(b, b, max_e[:, 0:heads], ALU.max))
                mc.leave(VIS)

            v.memset(dn_i[:, :], PAD_DST).then_inc(s_zero, 1)
            v.memset(xs[:, NT - 1, :], 0.0).then_inc(s_zero, 1)
            v.memset(dst_v[:, :], float(PAD_DST))
            v.memset(cnt[:, :], 0.0)
            link(v.memset(tile_v[:, :], 0))
            v.sem_inc(s_ph, 1)

            v.wait_ge(s_pool, 8)
            v.tensor_copy(iota_p[:, :], iota_i[:, :])
            v.tensor_copy(part_f[:, :], part_i[:, :])
            v.tensor_copy(vnum[:, :], v_i[:, :])
            v.tensor_copy(ident_b[:, :], ident[:, :])
            v.wait_ge(s_dst, 16)
            link(v.tensor_scalar(d_t[:, :], d_i[:, :], 7, None, ALU.arith_shift_right))
            link(v.tensor_copy(d_b[:, :], d_t[:, :]))
            for t in range(1, NT + 1):
                ins = v.tensor_scalar(junk_b[:, t % 2, :], d_b[:, :], float(t), 0.0, ALU.is_lt, ALU.add, accum_out=cnt[:, t:t + 1])
                if t % 2 == 0 or t == NT:
                    link(ins)
            link(v.tensor_tensor(junk_b[:, 0, 0:ROWS - 1], d_b[:, 0:ROWS - 1], d_b[:, 1:ROWS], ALU.is_gt))
            v.tensor_reduce(cnt[:, NT + 1:NT + 2], junk_b[:, 0, 0:ROWS - 1], AX.X, ALU.add)
            v.wait_ge(s_dn, 16)
            link(v.tensor_scalar(dn_i[:, :], dn_i[:, :], 7, None, ALU.arith_shift_right))
            link(v.tensor_tensor(cnt[:, NT + 2:NT + 3], d_t[:, ROWS - 1:ROWS], dn_i[:, 0:1], ALU.is_gt))
            v.sem_inc(s_cnt, 1)
            v.wait_ge(s_starts, 1)
            link(v.tensor_copy(st[:, :], bank[4][:, 0:NT + 3]))
            link(v.tensor_tensor(fl_f[:, 0:1], st[:, NT + 1:NT + 2], st[:, NT + 2:NT + 3], ALU.add))
            link(v.tensor_scalar(flags[:, 0:1], fl_f[:, 0:1], -1.0 if FORCE_SORT else 0.0, None, ALU.is_gt))
            v.sem_inc(s_flag, 1)
            unsorted = v.value_load(flags[0:1, 0:1], min_val=0, max_val=1)
            with v.If(unsorted > 0):
                sort_edges()
            v.tensor_copy(st_i[:, 0, :], st[:, 0:NT])
            link(v.tensor_scalar(st_i[:, 1, :], st[:, 1:NT + 1], float(P - 1), None, ALU.add))
            link(v.tensor_scalar(st_i[:, :, :], st_i[:, :, :], 7, None, ALU.arith_shift_right))
            link(v.tensor_copy(lo_hi[:, :, :], st_i[:, :, :]))
            link(v.tensor_tensor(nvis[:, :], lo_hi[:, 1, :], lo_hi[:, 0, :], ALU.subtract))
            link(v.tensor_tensor(off[:, :], st[:, 1:NT + 1], st[:, 0:NT], ALU.is_gt))
            link(v.tensor_tensor(nvis[:, :], nvis[:, :], off[:, :], ALU.mult))
            link(v.tensor_scalar(nall[:, :], iota_p[:, 0:NT], float(LOOP_ROWS), None, ALU.is_lt))
            link(v.tensor_tensor(nall[:, :], nall[:, :], nvis[:, :], ALU.add))
            link(v.tensor_scalar(st_i[:, 0, :], nall[:, :], 1.0, None, ALU.add))
            link(v.tensor_scalar(st_i[:, 0, :], st_i[:, 0, :], 1, None, ALU.arith_shift_right))
            link(v.tensor_scalar(nall[:, :], st_i[:, 0, :], 2.0, None, ALU.mult))
            link(v.tensor_tensor_scan(cum[:, :], ones[:, 0:NT], nall[:, :], 0.0, ALU.mult, ALU.add))
            link(v.tensor_tensor(nall[:, :], cum[:, :], nall[:, :], ALU.subtract))
            link(v.tensor_tensor(off[:, :], lo_hi[:, 0, :], nall[:, :], ALU.subtract))
            link(v.tensor_tensor(nall[:, :], nall[:, :], nvis[:, :], ALU.add))
            vb = vnum[:, :].unsqueeze(2).broadcast_to([P, VC, NT])
            link(v.tensor_tensor(ge[:, :, :], vb, cum[:, :].unsqueeze(1).broadcast_to([P, VC, NT]), ALU.is_ge))
            link(v.tensor_reduce(vt[:, :], ge[:, :, :], AX.X, ALU.add))
            link(v.tensor_tensor(ge[:, :, :], vt[:, :].unsqueeze(2).broadcast_to([P, VC, NT]),
                                 iota_p[:, 0:NT].unsqueeze(1).broadcast_to([P, VC, NT]), ALU.is_equal))
            link(v.tensor_tensor(ge2[:, :, :], ge[:, :, :], nall[:, :].unsqueeze(1).broadcast_to([P, VC, NT]), ALU.mult))
            link(v.tensor_tensor(ge[:, :, :], ge[:, :, :], off[:, :].unsqueeze(1).broadcast_to([P, VC, NT]), ALU.mult))
            v.tensor_reduce(vy[:, :], ge2[:, :, :], AX.X, ALU.add)
            link(v.tensor_reduce(vr[:, :], ge[:, :, :], AX.X, ALU.add))
            v.tensor_scalar(vx[:, :], vt[:, :], float(LOOP_ROWS), None, ALU.is_lt)
            link(v.tensor_tensor(vz[:, :], vnum[:, :], vy[:, :], ALU.is_equal))
            link(v.tensor_tensor(vx[:, :], vx[:, :], vz[:, :], ALU.mult))
            link(v.tensor_scalar(vz[:, :], vt[:, :], float(ROWS - EMPTY_ROW), None, ALU.add))
            link(v.tensor_tensor(vx[:, :], vx[:, :], vz[:, :], ALU.mult))
            v.tensor_tensor(vy[:, :], vnum[:, :], vy[:, :], ALU.is_lt)
            link(v.scalar_tensor_tensor(vr[:, :], vr[:, :], float(-EMPTY_ROW), vnum[:, :], ALU.add, ALU.add))
            link(v.tensor_tensor(vr[:, :], vr[:, :], vy[:, :], ALU.mult))
            link(v.scalar_tensor_tensor(vr[:, :], vr[:, :], float(EMPTY_ROW), vx[:, :], ALU.add, ALU.add))
            link(v.tensor_copy(row_i[:, :], vr[:, :]))
            v.sem_inc(s_rows, 1)
            link(v.tensor_scalar(vx[:, :], vt[:, :], float(-P), None, ALU.mult))

            v.wait_ge(s_w, 16 * 10)
            for wa, a, heads in ((w1a, a1, H1), (w2a, a2, H2)):
                for k in range(2):
                    for sd in range(2):
                        link(v.tensor_tensor(prod[:, :], wa[:, k, 0:D], a[:, sd, :], ALU.mult))
                        link(v.tensor_reduce(wa[:, k, D + sd * heads:D + (sd + 1) * heads],
                                             prod[:, :].rearrange("p (h c) -> p h c", h=heads), AX.X, ALU.add))
            v.sem_inc(s_ph, 1)
            v.wait_ge(s_vecT, 1)
            v.tensor_copy(cols[:, :], bank[5][:, 0:100]).then_inc(s_vecT, 1)
            v.wait_ge(s_tilt, 1)
            v.tensor_copy(tile_v[0:1, 0:VIS], bank[4][0:1, 0:VIS])
            v.wait_ge(s_rg, 16 * 2 * VC)
            v.tensor_copy(rows_f[0:VP, 0, :, :], rows_i[0:VP, 0, :, :])
            for c in range(VC):
                ins = v.tensor_scalar(rows_f[0:VP, 1, c, :], rows_i[0:VP, 1, c, :], vx[0:VP, c:c + 1], None, ALU.add)
            link(ins)
            v.sem_inc(s_rf, 1)
            v.wait_ge(s_rT, 1)
            v.tensor_copy(src_v[:, 0:VIS], bank[6][:, 0:VIS])
            link(v.tensor_copy(dst_v[:, 0:VIS], bank[7][:, 0:VIS]))
            v.sem_inc(s_vtab, 1)

            def combine():
                m0, m1 = stats[:, :, 1], stats[:, :, 4]
                v.tensor_tensor(tmp_a[:, :], stats[:, :, 2], stats[:, :, 5], ALU.add)
                v.tensor_tensor(tmp_b[:, :], m0, m1, ALU.subtract)
                link(v.tensor_tensor(mean[:, :], m0, m1, ALU.add))
                v.tensor_scalar(mean[:, :], mean[:, :], 0.5, None, ALU.mult)
                link(v.tensor_tensor(tmp_b[:, :], tmp_b[:, :], tmp_b[:, :], ALU.mult))
                link(v.tensor_scalar(tmp_b[:, :], tmp_b[:, :], 0.25, None, ALU.mult))
                link(v.scalar_tensor_tensor(var[:, :], tmp_a[:, :], 1.0 / D, tmp_b[:, :], ALU.mult, ALU.add))

            def inverse_root(n):
                link(v.tensor_scalar(tmp_a[:, :], var[:, :], EPS, None, ALU.add))
                v.sem_inc(s_var, 1)
                v.wait_ge(s_root, n)
                link(v.reciprocal(rstd[:, :], root[:, :]))
                link(v.tensor_tensor(tmp_c[:, :], rstd[:, :], rstd[:, :], ALU.mult))
                link(v.tensor_tensor(tmp_c[:, :], tmp_c[:, :], tmp_a[:, :], ALU.mult))
                link(v.tensor_scalar(tmp_c[:, :], tmp_c[:, :], -0.5, 1.5, ALU.mult, ALU.add))
                link(v.tensor_tensor(rstd[:, :], rstd[:, :], tmp_c[:, :], ALU.mult))

            def normalise(ph, source):
                def one(t, s):
                    ring(v, s_T, ph * NT, t)
                    v.tensor_scalar(xn[:, s, :], source(t), mean[:, ds(t, 1)], rstd[:, ds(t, 1)],
                                    ALU.subtract, ALU.mult).then_inc(s_xn, 1)
                return one

            def scores_out(ph, heads):
                def one(t, s):
                    v.wait_ge(s_H, ph * NT + t + 1)
                    wt = W1T if heads == H1 else W2T
                    v.tensor_copy(tabs[:, t, wt:wt + heads], bank[2 + s][:, D:D + heads])
                    v.tensor_scalar(tabs[:, t, wt + heads:wt + 2 * heads], bank[2 + s][:, D:D + heads], SLOPE, None, ALU.mult)
                    v.tensor_copy(ed[:, t, 0:heads], bank[2 + s][:, D + heads:D + 2 * heads]).then_inc(s_HE, 1)
                return one

            def shifts(layer, heads, wt):
                es = tabs[:, :, wt:wt + heads].rearrange("p t h -> p h t")
                v.wait_ge(s_HE, (layer + 1) * NT)
                link(v.tensor_reduce(es_mm[:, 0:heads], es, AX.X, ALU.max))
                link(v.tensor_reduce(es_mm[:, heads:2 * heads], es, AX.X, ALU.min))
                link(v.tensor_scalar(es_mm[:, heads:2 * heads], es_mm[:, heads:2 * heads], -1.0, None, ALU.mult))
                v.sem_inc(s_mm, 1)
                v.wait_ge(s_ar, layer + 1)
                v.tensor_copy(bound[:, :, 0:heads], es_all[:, 0:heads].unsqueeze(1).broadcast_to([P, NT + 1, heads]))
                link(v.tensor_tensor(fl_f[:, 0:heads], es_all[:, 0:heads], es_all[:, heads:2 * heads], ALU.add))
                link(v.tensor_reduce(fl_f[:, 0:1], fl_f[:, 0:heads], AX.X, ALU.max))
                link(v.tensor_scalar(flags[:, layer + 1:layer + 2], fl_f[:, 0:1], -1.0 if FORCE_MAX else SPREAD, None, ALU.is_gt))
                v.sem_inc(s_flag, 1)
                wide_spread = v.value_load(flags[0:1, layer + 1:layer + 2], min_val=0, max_val=1)
                with v.If(wide_spread > 0):
                    v.wait_ge(s_vtab, 1)
                    true_maxima(layer, heads, wt)
                c = shift[:, :, 0:heads]
                link(v.tensor_tensor(c, ed[:, :, 0:heads], bound[:, 0:NT, 0:heads], ALU.add))
                link(v.scalar_tensor_tensor(c, c, SLOPE, c, ALU.mult, ALU.max))
                v.tensor_tensor(edc[:, 0:NT, 0:heads], ed[:, :, 0:heads], c, ALU.subtract)
                link(v.scalar_tensor_tensor(edc[:, 0:NT, heads:2 * heads], ed[:, :, 0:heads], SLOPE, c, ALU.mult, ALU.subtract))
                rest = edr[:, :, :]
                link(v.tensor_copy(edp[:, :, 0, :], edc[:, :, :]))
                link(v.tensor_tensor(rest, edc[:, :, :], edp[:, :, 0, :], ALU.subtract))
                link(v.tensor_copy(edp[:, :, 1, :], rest))
                link(v.tensor_tensor(rest, rest, edp[:, :, 1, :], ALU.subtract))
                link(v.tensor_copy(edp[:, :, 2, :], rest))
                v.sem_inc(s_shift, 1)

            def edge_loop(layer, heads, wt):
                v.wait_ge(s_vtab, 1)
                v.wait_ge(s_clear, layer + 1)

                def onehot(i, q):
                    if isinstance(i, int) and i * QB + q >= RUN:
                        return
                    col = i * (QB * BV) + q * BV
                    if not (isinstance(i, int) and i * QB + q < QB):
                        v.wait_ge(s_ohf, i * QB + (layer * NB + q) - QB + 1)
                    cols_ = dst_v[:, ds(col, BV)] if not isinstance(col, int) else dst_v[:, col:col + BV]
                    v.tensor_tensor(OHB[:, q % QB, :, :], cols_.unsqueeze(2).broadcast_to([P, BV, P]),
                                    iota_p[:, :].unsqueeze(1).broadcast_to([P, BV, P]), ALU.is_equal).then_inc(s_oh, 1)

                def exponents(i, q):
                    if isinstance(i, int) and i * QB + q >= NB:
                        return
                    h = q % 2
                    v.wait_ge(s_look, i * QB + (layer * RUN + q + 1))
                    for k in range(BV):
                        slot = (q % QB) * BV + k
                        v.wait_ge(s_g[slot], i * 16 + ((q // QB) * 16 + layer * (IT + (q % QB < TAIL)) * 16 + 16))
                    ps = bank[2 + h][:, 0:BV * 6 * HEADS].rearrange("p (k t c) -> p k c t", k=BV, t=3)
                    scores = G[:, (q % QB) * BV:(q % QB + 1) * BV, wt:wt + 2 * heads]
                    link(v.tensor_reduce(Z[:, h, :, :], ps, AX.X, ALU.add))
                    link(v.tensor_tensor(Z[:, h, :, 0:2 * heads], scores, Z[:, h, :, 0:2 * heads], ALU.add))
                    v.tensor_tensor(U[:, h, :, 0:heads], Z[:, h, :, 0:heads], Z[:, h, :, heads:2 * heads], ALU.max).then_inc(s_u, 1)

                def accumulate(i, q):
                    for m in range(BV // 2):
                        col = i * (QB * BV) + (q * BV + 2 * m)
                        ti = v.value_load(tile_v[0:1, ds(col, 1)] if not isinstance(col, int) else tile_v[0:1, col:col + 1],
                                          min_val=0, max_val=NT)
                        n = i * (QB * 2) + (layer * NB * 2 + q * 2 + m)
                        v.wait_ge(s_sum, n + 1)
                        after(v, s_acc, n)
                        a = acc[:, ds(ti, 1), 0:wt].rearrange("p o c -> p (o c)")
                        v.tensor_tensor(a, a, bank[4 + (q % 2) * 2 + m][:, 0:wt], ALU.add).then_inc(s_acc, 1)

                def step(i, q, first=False):
                    exponents(i, q + 1)
                    onehot(i, q + AHEAD)
                    h, b = q % 2, i * QB + (layer * NB + q)
                    rows = G[:, q * BV:(q + 1) * BV, :]
                    v.wait_ge(s_exp, b + 1)
                    if not (isinstance(i, int) and i * QB + q < 2):
                        v.wait_ge(s_sum, (b - 1) * 2)
                    if heads == 4:
                        for k in range(BV):
                            ins = v.tensor_tensor(MSG[:, h, k, 0:wt].rearrange("p (h c) -> p h c", c=CH + 1),
                                                  rows[:, k, 0:wt].rearrange("p (h c) -> p h c", c=CH + 1),
                                                  WT[:, h, k, :].unsqueeze(2).broadcast_to([P, HEADS, CH + 1]), ALU.mult)
                    else:
                        ins = v.tensor_tensor(MSG[:, h, :, 0:wt], rows[:, :, 0:wt],
                                              WT[:, h, :, 0:1].broadcast_to([P, BV, wt]), ALU.mult)
                    ins.then_inc(s_msg, 1)
                    if not first:
                        accumulate(*((i, q - 1) if q else (i - 1, QB - 1)))

                for q in range(AHEAD):
                    onehot(0, q)
                exponents(0, 0)
                for q in range(QB):
                    step(0, q, first=(q == 0))
                with v.Fori(1, IT) as i:
                    ch.enter(i, 1, 2 * QB)
                    for q in range(QB):
                        step(i, q)
                ch.leave(IT - 1)
                for q in range(TAIL):
                    step(IT, q)
                accumulate(IT, TAIL - 1)
                v.wait_ge(s_acc, (layer + 1) * NB * 2)

            def row_stats(source, tiles=range(NT)):
                with v.Fori(tiles[0], tiles[-1] + 1) as t:
                    ins = v.bn_stats(stats[:, t, :], source(t))

            v.memset(tabs[:, :, 0:W1T].rearrange("p t (h c) -> p t h c", c=CH + 1)[:, :, :, CH:CH + 1], 1.0)
            link(v.memset(edc[:, :, :], 0.0))
            for c in range(NT // XCH):
                v.wait_ge(s_x[c], 16)
                row_stats(lambda t: xs[:, t, :], range(c * XCH, (c + 1) * XCH))
            v.wait_ge(s_x[4], 16)
            link(v.bn_stats(stats[:, NT - 1, :], xs[:, NT - 1, :]))
            combine()
            inverse_root(1)
            skewed_by_two(v, normalise(0, lambda t: xs[:, t, :]), scores_out(0, H1))
            shifts(0, H1, W1T)
            edge_loop(0, H1, W1T)

            heads_view = acc[:, 0:NT, :].rearrange("p t (h c) -> p (t h) c", c=CH + 1)
            rd = rden[:, :, :].rearrange("p t h -> p (t h)")
            link(v.tensor_scalar(rd, heads_view[:, :, CH], 1e-37, None, ALU.max))
            link(v.reciprocal(rd, rd))
            link(v.tensor_tensor(heads_view[:, :, 0:CH], heads_view[:, :, 0:CH],
                                 rd.unsqueeze(2).broadcast_to([P, NT * HEADS, CH]), ALU.mult))
            o1 = acc[:, 0:NT, :].rearrange("p t (h c) -> p t h c", c=CH + 1)[:, :, :, 0:CH]
            for h in range(HEADS):
                ins = v.tensor_tensor(o1[:, :, h, :], o1[:, :, h, :],
                                      b1r[:, h * CH:(h + 1) * CH].unsqueeze(1).broadcast_to([P, NT, CH]), ALU.add)
            link(ins)

            def o1_row(t):
                return acc[:, ds(t, 1), :].rearrange("p o (h c) -> p (o h) c", c=CH + 1)[:, :, 0:CH]
            row_stats(o1_row)
            link(v.tensor_copy(tmp_b[:, :], mean[:, :]))
            combine()
            inverse_root(2)
            v.wait_ge(s_tabw, 16 * NT)
            link(v.memset(tabs[:, :, D:D + 1], 1.0))
            v.sem_inc(s_ph, 1)

            def normalise1(t, s):
                ring(v, s_T, NT, t)
                v.tensor_scalar(xn[:, s, :].rearrange("p (h c) -> p h c", c=CH), o1_row(t), mean[:, ds(t, 1)], rstd[:, ds(t, 1)],
                                ALU.subtract, ALU.mult).then_inc(s_xn, 1)
            skewed_by_two(v, normalise1, scores_out(1, H2))
            shifts(1, H2, W2T)
            edge_loop(1, H2, W2T)

            rd2 = rden[:, :, 0]
            link(v.tensor_scalar(rd2, acc[:, 0:NT, D], 1e-37, None, ALU.max))
            link(v.reciprocal(rd2, rd2))
            link(v.tensor_tensor(acc[:, 0:NT, 0:D], acc[:, 0:NT, 0:D], rd2.unsqueeze(2).broadcast_to([P, NT, D]), ALU.mult))
            link(v.tensor_tensor(acc[:, 0:NT, 0:D], acc[:, 0:NT, 0:D], b2r[:, :].unsqueeze(1).broadcast_to([P, NT, D]), ALU.add))
            link(v.tensor_tensor(xs[:, :, :], xs[:, :, :], acc[:, 0:NT, 0:D], ALU.add))
            row_stats(lambda t: xs[:, t, :])
            link(v.tensor_copy(tmp_b[:, :], mean[:, :]))
            combine()
            inverse_root(3)
            link(v.tensor_copy(tmp_b[:, :], rstd[:, :]))
            for _ in range(2):
                link(v.tensor_tensor(var[:, :], var[:, :], rstd[:, :], ALU.mult))
            inverse_root(4)
            link(v.tensor_tensor(rstd[:, :], rstd[:, :], tmp_b[:, :], ALU.mult))

            def normalise2(t, s):
                ring(v, s_T, 2 * NT, t)
                if not isinstance(t, int) or t >= 2:
                    v.wait_ge(s_xt[s], (t - s) * 8)
                v.tensor_scalar(xn[:, s, :], xs[:, t, :], mean[:, ds(t, 1)], rstd[:, ds(t, 1)],
                                ALU.subtract, ALU.mult).then_inc(s_xn, 1)

            def logits_out(t, s):
                v.wait_ge(s_H, 2 * NT + t + 1)
                v.tensor_copy(lg[:, t, :], bank[2 + s][:, 0:EXPERTS]).then_inc(s_HE, 1)
            skewed_by_two(v, normalise2, logits_out)
            v.wait_ge(s_HE, 3 * NT)

            def over_e(a):
                return a.unsqueeze(2).broadcast_to([P, NT, EXPERTS])
            i8 = iota_m8[:, :].unsqueeze(1).broadcast_to([P, NT, EXPERTS])
            v.tensor_scalar(iota_m8[:, :], iota_p[:, 0:EXPERTS], float(-EXPERTS), None, ALU.add)
            v.memset(valid[:, :], 1.0)
            link(v.tensor_tensor(lg[:, :, :], lg[:, :, :], brr[:, :].unsqueeze(1).broadcast_to([P, NT, EXPERTS]), ALU.add))
            link(v.tensor_scalar(valid[:, NT - 1:NT], part_f[:, :], float(LAST), None, ALU.is_lt))
            for k in range(2):
                l = (lg, lg2)[k]
                link(v.tensor_reduce(top[:, k, :], l[:, :, :], AX.X, ALU.max))
                link(v.tensor_tensor(cand[:, :, :], l[:, :, :], over_e(top[:, k, :]), ALU.is_equal))
                link(v.tensor_tensor(cand[:, :, :], cand[:, :, :], i8, ALU.mult))
                link(v.tensor_reduce(first[:, :], cand[:, :, :], AX.X, ALU.min))
                link(v.tensor_tensor(oh[:, k, :, :], over_e(first[:, :]), i8, ALU.is_equal))
                if k == 0:
                    link(v.scalar_tensor_tensor(lg2[:, :, :], oh[:, 0, :, :], -BIG, lg[:, :, :], ALU.mult, ALU.add))
            link(v.tensor_tensor(first[:, :], top[:, 1, :], top[:, 0, :], ALU.subtract))
            v.sem_inc(s_gx, 1)
            link(v.tensor_tensor(ohm[:, :, :], oh[:, 0, :, :], oh[:, 1, :, :], ALU.add))
            link(v.tensor_tensor(ohm[:, :, :], ohm[:, :, :], over_e(valid[:, :]), ALU.mult))
            v.sem_inc(s_ohm, 1)
            v.wait_ge(s_ge, 1)
            link(v.tensor_scalar(gate[:, 0, :], gate[:, 1, :], 1.0, None, ALU.add))
            link(v.reciprocal(gate[:, 0, :], gate[:, 0, :]))
            link(v.tensor_tensor(gate[:, 1, :], gate[:, 1, :], gate[:, 0, :], ALU.mult))
            v.wait_ge(s_pre, 1)
            tot = bank[5][:, 0:NT * EXPERTS].rearrange("p (t e) -> p t e", e=EXPERTS)
            for e in range(EXPERTS):
                ins = v.tensor_tensor_scan(inc[:, :, e], ones[:, 0:NT], tot[:, :, e], 0.0, ALU.mult, ALU.add)
            link(ins)
            link(v.tensor_tensor(pos_e[:, :, :], inc[:, :, :], tot, ALU.subtract))
            link(v.tensor_tensor(pos_e[:, :, :], pos_e[:, :, :], bank[4][:, 0:NT * EXPERTS].rearrange("p (t e) -> p t e", e=EXPERTS), ALU.add))
            link(v.tensor_scalar(nt_i[:, :], inc[:, NT - 1, :], float(P - 1), None, ALU.add))
            link(v.tensor_scalar(nt_i[:, :], nt_i[:, :], 7, None, ALU.arith_shift_right))
            link(v.tensor_scalar(ntf[:, :], nt_i[:, :], 1.0, None, ALU.max))
            link(v.tensor_tensor_scan(ecum[:, :], ones[:, 0:EXPERTS], ntf[:, :], 0.0, ALU.mult, ALU.add))
            link(v.tensor_tensor(ebase[:, :], ecum[:, :], ntf[:, :], ALU.subtract))
            v.tensor_copy(etab[:, 0, :], ntf[:, :])
            v.tensor_copy(etab[:, 1, :], ebase[:, :])
            link(v.tensor_scalar(ebase[:, :], ebase[:, :], float(P), None, ALU.mult))
            link(v.tensor_tensor(pos_e[:, :, :], pos_e[:, :, :], ebase[:, :].unsqueeze(1).broadcast_to([P, NT, EXPERTS]), ALU.add))
            for k in range(2):
                link(v.tensor_tensor(cand[:, :, :], oh[:, k, :, :], pos_e[:, :, :], ALU.mult))
                link(v.tensor_reduce(pos[:, k, :], cand[:, :, :], AX.X, ALU.add))
            link(v.tensor_copy(pos_i[:, :, :], pos[:, :, :]))
            v.tensor_scalar(pai[:, :, :], pos_i[:, :, :], 7, None, ALU.arith_shift_right)
            link(v.tensor_scalar(pbi[:, :, :], pos_i[:, :, :], P - 1, None, ALU.bitwise_and))
            v.tensor_copy(pa[:, :, :], pai[:, :, :])
            v.tensor_copy(pb[:, :, :], pbi[:, :, :])
            link(v.tensor_copy(cid[:, :, :], cid_i[:, :, :]))
            link(v.tensor_tensor(cid[:, :, :], cid[:, :, :], valid[:, :].unsqueeze(1).broadcast_to([P, 2, NT]), ALU.mult))

            def one_place(t, k):
                n = t * 2 + k
                if not isinstance(t, int) or t >= 1:
                    v.wait_ge(s_om, n - 1)
                v.tensor_scalar(ohb[:, k, :], iota_p[:, :], pb[:, k, ds(t, 1)], None, ALU.is_equal)
                v.tensor_scalar(oha[:, k, :], iota_p[:, 0:SLOT_TILES], pa[:, k, ds(t, 1)], cid[:, k, ds(t, 1)],
                                ALU.is_equal, ALU.mult).then_inc(s_ob, 1)
            one_place(0, 0)
            one_place(0, 1)
            with v.Fori(1, NT) as t:
                one_place(t, 0)
                one_place(t, 1)
            v.wait_ge(s_om, 2 * NT)
            link(v.tensor_scalar(slot_f[:, :], bank[6][:, 0:SLOT_TILES], -1.0, None, ALU.add))
            link(v.tensor_scalar(slot_e[:, :], slot_f[:, :], 0.0, None, ALU.is_lt))
            link(v.tensor_scalar(slot_f[:, :], slot_f[:, :], 0.0, None, ALU.max))
            v.tensor_scalar(first[:, 0:1], part_f[:, :], float(CHOICE_ROWS), None, ALU.add)
            link(v.tensor_copy(slot_g[:, :], slot_f[:, :]))
            v.tensor_copy(si[:, :], first[:, 0:1])
            link(v.tensor_scalar(slot_g[:, :], slot_g[:, :], 1, None, ALU.arith_shift_right))
            link(v.tensor_scalar(slot_e[:, :], slot_e[:, :], first[:, 0:1], None, ALU.mult))
            link(v.tensor_tensor(slot_s[:, :], slot_f[:, :], slot_e[:, :], ALU.add))
            v.sem_inc(s_slot, 1)

            def token_indices(g):
                v.tensor_copy(gi[:, :], slot_g[:, ds(g, 1)] if not isinstance(g, int) else slot_g[:, g:g + 1]).then_inc(s_gi, 1)

            def expert_input(g, e):
                v.wait_ge(s_xT, g + 1)
                for k in range(2):
                    ins = v.tensor_scalar(xeT[:, k, :], bank[2][:, k * P:(k + 1) * P], cols[:, ds(e * 2 + (64 + k), 1)],
                                          cols[:, ds(e * 2 + (80 + k), 1)], ALU.mult, ALU.add)
                ins.then_inc(s_xe, 1)

            def results(g, c):
                v.wait_ge(s_y, g + 1)
                v.wait_ge(s_sc, g * 16 + 16)
                v.tensor_copy(si[:, :], slot_s[:, ds(g, 1)])
                v.tensor_tensor(ys, bank[3][:, 0:D], fb2[:, c, :], ALU.add).then_inc(s_ys, 1)

            v.sem_inc(s_ys, 1)
            token_indices(0)
            with v.Fori(0, EXPERTS // 2) as j:
                for c in range(2):
                    e = j * 2 + c
                    n_e = v.value_load(etab[0:1, 0, ds(e, 1)], min_val=1, max_val=NT)
                    b_e = v.value_load(etab[0:1, 1, ds(e, 1)], min_val=0, max_val=MAX_TILES)
                    v.wait_ge(s_fw[c], j * 48 + 48)
                    expert_input(b_e, e)
                    token_indices(b_e + 1)
                    with v.Fori(1, n_e) as i:
                        g = b_e + i
                        v.wait_ge(s_h, g * (FC // 2))
                        expert_input(g, e)
                        token_indices(g + 1)
                        results(g - 1, c)
                    results(b_e + n_e - 1, c)
                    v.wait_ge(s_ys, b_e + n_e + 1)
                    v.sem_inc(s_fwu, 1)
            total = v.value_load(etab[0:1, 1, EXPERTS - 1:EXPERTS], min_val=0, max_val=MAX_TILES)
            n_last = v.value_load(etab[0:1, 0, EXPERTS - 1:EXPERTS], min_val=1, max_val=NT)
            v.wait_ge(s_sc, (total + n_last) * 16 + 16)
            v.sem_inc(s_ph, 2)

            def one_out(t, s, j):
                v.wait_ge(s_yl[s], j * 16 + 16)
                if not isinstance(j, int) or j >= 1:
                    v.wait_ge(s_st[s], j * 16)
                r = slice(0, P)
                if isinstance(t, int) and t == NT - 1:
                    r = slice(0, LAST)
                link(v.scalar_tensor_tensor(yo[r, s, :], YL[r, s, 0:D], gate[r, 0, ds(t, 1)], xs[r, t, :], ALU.mult, ALU.add))
                v.scalar_tensor_tensor(yo2[r, s, :], YL[r, s, D:2 * D], gate[r, 1, ds(t, 1)], yo[r, s, :],
                                       ALU.mult, ALU.add).then_inc(s_o, 1)
            one_out(0, 0, 0)
            one_out(1, 1, 0)
            with v.Fori(1, NT // 2) as j:
                ch.enter(j, 1, 2)
                one_out(j * 2, 0, j)
                one_out(j * 2 + 1, 1, j)
            ch.leave(NT // 2 - 1)
            one_out(NT - 1, 0, NT // 2)


_INS = ['x', 'src', 'dst', 'L0_gnn_W1', 'L0_gnn_a1_src', 'L0_gnn_a1_dst', 'L0_gnn_b1', 'L0_gnn_ln_g', 'L0_gnn_ln_b',
        'L0_gnn_W2', 'L0_gnn_a2_src', 'L0_gnn_a2_dst', 'L0_gnn_b2', 'L0_ffn_Wr', 'L0_ffn_br', 'L0_ffn_ln_g',
        'L0_ffn_ln_b', 'L0_ffn_W1', 'L0_ffn_b1', 'L0_ffn_W2', 'L0_ffn_b2']


def edge_rows(a, spare, loops):
    rows = np.full((PAD_ROWS * P,), spare, a.dtype)
    rows[:E_IN] = a
    rows[ROWS * P:ROWS * P + LOOPS] = loops
    return rows.reshape(PAD_ROWS, P)


def kernel(**inputs):
    import concourse.bacc as bacc
    from concourse.bass_utils import run_bass_kernel_spmd as run

    nc = bacc.Bacc("TRN2", target_bir_lowering=False, num_devices=1)
    arrays, args = {}, []
    loops = np.arange(LOOPS)
    for name in _INS:
        a = np.ascontiguousarray(inputs[name])
        if name in ("src", "dst"):
            a = edge_rows(a, PAD_DST if name == "dst" else 0, loops)
        arrays[f"in_{name}"] = a
        args.append(nc.dram_tensor(f"in_{name}", a.shape, mybir.dt.from_np(a.dtype), kind="ExternalInput").ap())
    out = nc.dram_tensor("out_x", (N, D), mybir.dt.float32, kind="ExternalOutput").ap()
    build(nc, *args, out)
    result = run(nc, [arrays], core_ids=[0])
    return result.results[0]["out_x"]
```

```python
import numpy as np
import concourse.bass as bass
from concourse import mybir
from contextlib import ExitStack

P = 128
N, D = 3125, 256
HEADS, CH = 4, 64
E_IN = 53125
LOOPS = 625
EXPERTS, HID = 8, 1024
SLOPE, EPS = 0.2, 1e-5

NT = (N + P - 1) // P
LAST = N - (NT - 1) * P
NPAD = NT * P
ROWS = (E_IN + P - 1) // P
LOOP_ROWS = (LOOPS + P - 1) // P
BV = 4
VIS = 472
VC, VP = 4, VIS // 4
EMPTY_ROW = ROWS + LOOP_ROWS
PAD_ROWS = EMPTY_ROW + 1
PAD_DST = 9999
NB = VIS // BV
QB = 4
IT = NB // QB
TAIL = NB % QB
AHEAD = 3
RUN = NB + 2
VTAB = VIS + AHEAD * BV
H1, W1T, TAB1 = HEADS, HEADS * (CH + 1), HEADS * (CH + 1) + 2 * HEADS
H2, W2T, TAB2 = 1, D + 1, D + 3
SPREAD = 60.0
MAX_TILES = (2 * N + EXPERTS * (P - 1)) // P + EXPERTS - 1
SLOT_TILES = 96
CHOICE_ROWS = 2 * NPAD
SET = 5
FC = HID // P
XCH = 6
BIG = 3.0e38

assert (ROWS + NT - 1) + LOOP_ROWS + NT <= VIS and VIS % BV == 0 and 0 < TAIL < QB
assert MAX_TILES + NT + 1 <= SLOT_TILES


def build(nc, x, src, dst, g_w1, g_a1s, g_a1d, g_b1, g_lng, g_lnb, g_w2, g_a2s, g_a2d, g_b2,
          f_wr, f_br, f_lng, f_lnb, f_w1, f_b1, f_w2, f_b2, out):
    f32, i32, bf16 = mybir.dt.float32, mybir.dt.int32, mybir.dt.bfloat16
    ALU, ACT, AX = mybir.AluOpType, mybir.ActivationFunctionType, mybir.AxisListType
    RED = bass.bass_isa.ReduceOp
    ds = bass.ds

    def dram(name, shape, dt=f32):
        return nc.dram_tensor(name, shape, dt, kind="Internal").ap()

    edge_src = dram("edge_src", (PAD_ROWS * P, 1), i32)
    edge_dst = dram("edge_dst", (PAD_ROWS * P, 1), i32)
    tab1 = dram("tab1", (NPAD, TAB1))
    tab2 = dram("tab2", (NPAD, TAB2))
    xtab = dram("xtab", (NPAD, D))
    ytab = dram("ytab", (CHOICE_ROWS + P, D))

    with ExitStack() as ctx:
        def sb(name, shape, dt=f32):
            return ctx.enter_context(nc.sbuf_tensor(name, shape, dt))

        def sem(name):
            return ctx.enter_context(nc.semaphore(name))

        def sems(name, n):
            return [sem(f"{name}{k}") for k in range(n)]

        xs = sb("xs", [P, NT, D])
        tabs = sb("tabs", [P, NT, TAB1 + HEADS])
        acc = sb("acc", [P, NT + 1, W1T])
        G = sb("G", [P, QB * BV, TAB1])
        OH = sb("OH", [P, QB, BV, P])
        OHB = sb("OHB", [P, QB, BV, P], bf16)
        OHT = sb("OHT", [P, 2, BV * P], bf16)
        oh_flat = OH[:, :, :, :].rearrange("p q k c -> p (q k c)")
        wide = oh_flat[:, 2 * BV * P:4 * BV * P].rearrange("p (a n) -> p a n", a=2)
        ident_b = sb("ident_b", [P, P], bf16)
        MSG = sb("MSG", [P, 2, BV, W1T])
        m_flat = MSG[:, :, :, :].rearrange("p a k c -> p (a k c)")
        rows_f = MSG[:, 0:1, :, :].rearrange("p a k c -> p (a k c)")[:, 0:2 * VC * P].rearrange("p (k c n) -> p k c n", k=2, c=VC)
        src_v = sb("src_v", [P, VTAB], i32)
        dst_v = sb("dst_v", [P, VTAB])
        tile_v = sb("tile_v", [1, VTAB], i32)
        IDX = sb("IDX", [P, QB, BV], i32)
        ident = sb("ident", [P, P])
        ones = sb("ones", [P, P])
        upper = sb("upper", [P, P])
        iota_p = sb("iota_p", [P, P])
        iota_i = sb("iota_i", [P, P], i32)
        part_i = sb("part_i", [P, 1], i32)
        part_f = sb("part_f", [P, 1])
        shift = sb("shift", [P, NT, HEADS])
        edc = sb("edc", [P, NT + 1, 2 * HEADS])
        edp = sb("edp", [P, NT + 1, 3, 2 * HEADS], bf16)
        edr = sb("edr", [P, NT + 1, 2 * HEADS])
        es_mm = sb("es_mm", [P, 2 * HEADS])
        es_all = sb("es_all", [P, 2 * HEADS])
        Z = sb("Z", [P, 2, BV, 2 * HEADS])
        U = sb("U", [P, 2, BV, HEADS])
        WT = sb("WT", [P, 2, BV, HEADS])
        xn = sb("xn", [P, 4, D])
        xnT = sb("xnT", [P, 4, 2, P])
        stats = sb("stats", [P, NT, 6])
        mean = sb("mean", [P, NT])
        rstd = sb("rstd", [P, NT])
        tmp_a = sb("tmp_a", [P, NT])
        tmp_b = sb("tmp_b", [P, NT])
        var = sb("var", [P, NT])
        root = sb("root", [P, NT])
        tmp_c = sb("tmp_c", [P, NT])
        rden = sb("rden", [P, NT, HEADS])
        w1a = sb("w1a", [P, 2, D + 3 * HEADS])
        w2a = sb("w2a", [P, 2, D + 3])
        wr = sb("wr", [P, 2, EXPERTS])
        a1 = sb("a1", [P, 2, D])
        a2 = sb("a2", [P, 2, D])
        b1r = sb("b1r", [P, D])
        b2r = sb("b2r", [P, D])
        brr = sb("brr", [P, EXPERTS])
        prod = m_flat[:, 0:4 * D].rearrange("p (k s c) -> p k s c", k=2, s=2)
        vecs = sb("vecs", [P, P])
        cols = sb("cols", [P, 100])
        d_i = sb("d_i", [P, ROWS], i32)
        d_t = sb("d_t", [P, ROWS], i32)
        d_b = sb("d_b", [P, ROWS], bf16)
        junk_b = sb("junk_b", [P, 2, ROWS], bf16)
        dn_i = sb("dn_i", [P, 2], i32)
        cnt = sb("cnt", [P, NT + 3])
        st = sb("st", [P, NT + 3])
        st_i = sb("st_i", [P, 2, NT], i32)
        lo_hi = sb("lo_hi", [P, 2, NT])
        nvis = sb("nvis", [P, NT])
        cum = sb("cum", [P, NT])
        off = sb("off", [P, NT])
        vnum = sb("vnum", [P, VC])
        v_i = sb("v_i", [P, VC], i32)
        ge = sb("ge", [P, VC, NT])
        vt = sb("vt", [P, VC])
        vr = sb("vr", [P, VC])
        vx = sb("vx", [P, VC])
        vy = sb("vy", [P, VC])
        vz = sb("vz", [P, VC])
        ge2 = sb("ge2", [P, VC, NT])
        nall = sb("nall", [P, NT])
        row_i = sb("row_i", [P, VC], i32)
        rows_i = sb("rows_i", [P, 2, VC, P], i32)
        flags = sb("flags", [P, 3], i32)
        fl_f = sb("fl_f", [P, HEADS])
        bound = sb("bound", [P, NT + 1, HEADS])
        max_e = sb("max_e", [P, HEADS])
        below = sb("below", [P, NT + 2])
        limit = sb("limit", [P, NT + 2])
        start = sb("start", [P, NT + 1])
        ends = sb("ends", [P, 2], i32)
        lg = sb("lg", [P, NT, EXPERTS])
        lg2 = sb("lg2", [P, NT, EXPERTS])
        oh = sb("oh", [P, 2, NT, EXPERTS])
        ohm = sb("ohm", [P, NT, EXPERTS])
        cand = sb("cand", [P, NT, EXPERTS])
        inc = sb("inc", [P, NT, EXPERTS])
        pos_e = sb("pos_e", [P, NT, EXPERTS])
        top = sb("top", [P, 2, NT])
        first = sb("first", [P, NT])
        gate = sb("gate", [P, 2, NT])
        valid = sb("valid", [P, NT])
        iota_m8 = sb("iota_m8", [P, EXPERTS])
        pos = sb("pos", [P, 2, NT])
        pos_i = sb("pos_i", [P, 2, NT], i32)
        pa = sb("pa", [P, 2, NT])
        pb = sb("pb", [P, 2, NT])
        pai = sb("pai", [P, 2, NT], i32)
        pbi = sb("pbi", [P, 2, NT], i32)
        cid = sb("cid", [P, 2, NT])
        cid_i = sb("cid_i", [P, 2, NT], i32)
        nt_i = sb("nt_i", [P, EXPERTS], i32)
        ntf = sb("ntf", [P, EXPERTS])
        ecum = sb("ecum", [P, EXPERTS])
        ebase = sb("ebase", [P, EXPERTS])
        etab = sb("etab", [P, 2, EXPERTS], i32)
        slot_f = sb("slot_f", [P, SLOT_TILES])
        slot_e = sb("slot_e", [P, SLOT_TILES])
        slot_g = sb("slot_g", [P, SLOT_TILES], i32)
        slot_s = sb("slot_s", [P, SLOT_TILES], i32)
        gi = sb("gi", [P, 1], i32)
        si = sb("si", [P, 1], i32)
        fw1 = sb("fw1", [P, 2, 2, HID])
        fw2 = sb("fw2", [P, 2, FC, D])
        fb2 = sb("fb2", [P, 2, D])
        g_flat = G[:, :, :].rearrange("p s c -> p (s c)")
        acc_flat = acc[:, :, :].rearrange("p t c -> p (t c)")
        tabs_flat = tabs[:, :, :].rearrange("p t c -> p (t c)")
        ohb = acc_flat[:, 0:2 * NT * P].rearrange("p (k t n) -> p k t n", k=2, t=NT)
        oha = tabs_flat[:, 0:2 * NT * SLOT_TILES].rearrange("p (k t n) -> p k t n", k=2, t=NT)
        xg = m_flat[:, 0:D]
        xeT = m_flat[:, D:2 * D].rearrange("p (k n) -> p k n", k=2)
        ys = m_flat[:, 2 * D:3 * D]
        hid = oh_flat[:, 0:HID].rearrange("p (f n) -> p f n", n=P)
        yl = [b[:, i:i + SET * 2 * D].rearrange("p (t c) -> p t c", t=SET)
              for b, i in ((acc_flat, 0), (acc_flat, SET * 2 * D), (tabs_flat, 0), (tabs_flat, SET * 2 * D), (g_flat, 0))]

        bank = [ctx.enter_context(nc.psum_tensor(f"bank{k}", [P, 512], f32)) for k in range(8)]
        bankb = [bank[k][:, :].bitcast(bf16)[:, 0:BV * P] for k in range(2)]

        HB = (0, 1, 4, 5)

        s_x = sems("x_loaded", 5)
        s_dst = sem("dst_loaded")
        s_dn = sem("dst_next_loaded")
        s_copy = sem("edges_copied")
        s_w = sem("graph_weights_loaded")
        s_vec = sem("vectors_loaded")
        s_pool = sem("pool_constants")
        s_zero = sem("tail_zeroed")
        s_dve = sem("dve_chain")
        s_cnt = sem("counts_ready")
        s_starts = sem("starts_summed")
        s_rows = sem("visit_rows_ready")
        s_tilt = sem("visit_tiles_on_one_row")
        s_rg = sem("edge_rows_gathered")
        s_rf = sem("edge_rows_as_float")
        s_rT = sem("edge_rows_transposed")
        s_vtab = sem("visit_tables_ready")
        s_vecT = sem("vectors_transposed")
        s_xn = sem("xn_ready")
        s_T = sem("tile_transposed")
        s_TS = sem("transposed_tile_in_sbuf")
        s_H = sem("tile_projected")
        s_HS = sem("projection_in_sbuf")
        s_HE = sem("scores_in_sbuf")
        s_tabw = sem("table_written")
        s_mm = sem("local_extremes")
        s_ar = sem("global_extremes")
        s_shift = sem("shifts_ready")
        s_oh = sem("onehot_ready")
        s_ohf = sem("onehot_in_float32")
        s_ohT = sem("onehot_transposed")
        s_ohS = sem("onehot_T_in_sbuf")
        s_look = sem("destination_scores_looked_up")
        s_u = sem("exponents_ready")
        s_exp = sem("weights_ready")
        s_msg = sem("messages_ready")
        s_idx = sem("indices_ready")
        s_sum = sem("messages_summed")
        s_acc = sem("sums_accumulated")
        s_g = sems("row_gathered", QB * BV)
        s_gx = sem("gate_exponent_ready")
        s_ge = sem("gate_exp_done")
        s_ohm = sem("choices_ready")
        s_pre = sem("ranks_ready")
        s_ob = sem("slot_onehot_ready")
        s_ob2 = sem("slot_onehot_weighted")
        s_om = sem("slot_onehot_used")
        s_slot = sem("slots_ready")
        s_xt = sems("tokens_written", 4)
        s_fw = sems("expert_weights_loaded", 2)
        s_fwu = sem("expert_weights_used")
        s_gi = sem("token_indices_ready")
        s_xg = sem("tokens_gathered")
        s_xT = sem("tokens_transposed")
        s_xe = sem("expert_input_ready")
        s_h = sem("hidden_ready")
        s_hg = sem("hidden_activated")
        s_y = sem("expert_output_ready")
        s_ys = sem("expert_output_in_sbuf")
        s_sc = sem("results_scattered")
        s_yl = sems("results_loaded", NT // SET)
        s_o = sem("output_ready")
        s_st = sem("output_stored")
        s_var = sem("variances_ready")
        s_root = sem("roots_ready")
        s_all = sem("all_results_scattered")
        s_xb = sem("bias_added_to_x")
        s_clear = sem("sums_cleared")
        s_mark = sem("steps_marked")
        s_flag = sem("flags_ready")
        s_below = sem("edges_before_summed")
        s_kept = sem("destinations_kept")
        s_src = sem("sources_loaded")
        s_sort = sem("sort_chain")
        s_place = sem("edge_place_ready")
        s_moved = sem("edge_moved")
        s_mi = sems("max_source_ready", 2)
        s_mg = sems("max_row_gathered", 2)
        s_md = sems("max_operands_ready", 2)
        s_mt = sems("max_scores_spread", 2)
        s_mc = sems("max_chain", 2)

        class Chain:
            def __init__(self, eng, sem_):
                self.eng, self.sem, self.n, self.i = eng, sem_, 0, None

            def link(self, ins):
                self.n += 1
                ins.then_inc(self.sem, 1)
                at = self.n if self.i is None else self.i * self.per + (self.n - self.first * self.per)
                self.eng.wait_ge(self.sem, at)

            def enter(self, i, first, per):
                self.i, self.first, self.per, self.start = i, first, per, self.n

            def leave(self, passes):
                assert self.n - self.start == self.per, (self.n - self.start, self.per)
                self.n = self.start + self.per * passes
                self.i = None

        def after(eng, sem_, value):
            if not isinstance(value, int) or value > 0:
                eng.wait_ge(sem_, value)

        def ring(eng, sem_, base, t, n=2):
            if not isinstance(t, int) or t >= n:
                eng.wait_ge(sem_, base + t - (n - 1))

        def by_fours(eng, lead, follow=lambda t, k: None, d=1):
            for t in range(4 + d):
                lead(t, t % 4)
                if t >= d:
                    follow(t - d, (t - d) % 4)
            with eng.Fori(1, NT // 4 - 1) as j:
                for k in range(4):
                    lead(j * 4 + (k + d), (k + d) % 4)
                    follow(j * 4 + k, k)
            for t in range((NT // 4 - 1) * 4, NT):
                if t + d < NT:
                    lead(t + d, (t + d) % 4)
                follow(t, t % 4)

        block = ctx.enter_context(nc.Block())

        @block.sync
        def _(sp):
            sp.dma_start(d_i[:, :], dst[0:ROWS, :].rearrange("r c -> (r c)").rearrange("(p j) -> p j", p=P)).then_inc(s_dst, 16)
            for c in range(NT // XCH):
                sp.dma_start(xs[:, c * XCH:(c + 1) * XCH, :],
                             x[c * XCH * P:(c + 1) * XCH * P, :].rearrange("(t p) d -> p t d", p=P)).then_inc(s_x[c], 16)
            sp.wait_ge(s_zero, 2)
            sp.dma_start(xs[0:LAST, NT - 1, :], x[(NT - 1) * P:N, :]).then_inc(s_x[4], 16)
            for c in range(2):
                sp.dma_start(fw1[:, c, :, :], f_w1[c].rearrange("(k p) n -> p k n", p=P)).then_inc(s_fw[c], 16)
                sp.dma_start(fw2[:, c, :, :], f_w2[c].rearrange("(k p) n -> p k n", p=P)).then_inc(s_fw[c], 16)
                sp.dma_start(fb2[:, c, :], f_b2[c:c + 1, :].partition_broadcast(P)).then_inc(s_fw[c], 16)

            for layer, (tab, width) in enumerate(((tab1, TAB1), (tab2, TAB2))):
                def write_tab(t):
                    sp.wait_ge(s_HS, layer * NT + t + 1)
                    sp.wait_ge(s_HE, layer * NT + t + 1)
                    sp.dma_start(tab[ds(t * P, P), :], tabs[:, t, 0:width]).then_inc(s_tabw, 16)
                with sp.Fori(0, NT) as t:
                    write_tab(t)
            def write_tokens(t, s):
                sp.wait_ge(s_xn, 2 * NT + t + 1)
                sp.dma_start(xtab[ds(t * P, P), :], xn[:, s, :]).then_inc(s_xt[s], 16)
            by_fours(sp, write_tokens)
            with sp.Fori(1, EXPERTS // 2) as j:
                for c in range(2):
                    e = j * 2 + c
                    sp.wait_ge(s_fwu, e - 1)
                    sp.dma_start(fw1[:, c, :, :], f_w1[ds(e, 1)].rearrange("o (k p) n -> p (o k) n", p=P)).then_inc(s_fw[c], 16)
                    sp.dma_start(fw2[:, c, :, :], f_w2[ds(e, 1)].rearrange("o (k p) n -> p (o k) n", p=P)).then_inc(s_fw[c], 16)
                    sp.dma_start(fb2[:, c, :], f_b2[ds(e, 1), :].partition_broadcast(P)).then_inc(s_fw[c], 16)
            sp.wait_ge(s_all, 1)
            ypair = ytab[0:CHOICE_ROWS, :].rearrange("(n k) d -> n (k d)", k=2)

            for c in range(NT // SET):
                full = SET if c < NT // SET - 1 else SET - 1
                sp.dma_start(yl[c][:, 0:full, :],
                             ypair[c * SET * P:(c * SET + full) * P, :].rearrange("(t p) d -> p t d", p=P)).then_inc(s_yl[c], 16)
            sp.dma_start(yl[c][0:LAST, SET - 1, :], ypair[(NT - 1) * P:N, :]).then_inc(s_yl[c], 16)

        @block.gpsimd
        def _(pool):
            pool.memset(ident[:, :], 0.0).then_inc(s_pool, 1)
            pool.memset(ones[:, :], 1.0).then_inc(s_pool, 1)
            pool.iota(iota_i[:, :], [[1, P]], base=0, channel_multiplier=0).then_inc(s_pool, 1)
            pool.iota(part_i[:, :], [[1, 1]], base=0, channel_multiplier=1).then_inc(s_pool, 1)
            pool.iota(v_i[:, :], [[VP, VC]], base=0, channel_multiplier=1).then_inc(s_pool, 1)
            pool.iota(cid_i[:, :, :], [[1, 2], [2 * P, NT]], base=1, channel_multiplier=2).then_inc(s_pool, 1)
            pool.wait_ge(s_pool, 6)
            pool.affine_select(out=ident[:, :], in_=ident[:, :], compare_op=ALU.not_equal, fill=1.0,
                               base=0, pattern=[[-1, P]], channel_multiplier=1).then_inc(s_pool, 1)
            pool.affine_select(out=upper[:, :], in_=ones[:, :], compare_op=ALU.is_gt, fill=0.0,
                               base=0, pattern=[[1, P]], channel_multiplier=-1).then_inc(s_pool, 1)
            pool.wait_ge(s_flag, 1)
            unsorted = pool.value_load(flags[0:1, 0:1], min_val=0, max_val=1)
            pool.wait_ge(s_copy, 32)
            with pool.If(unsorted > 0):
                pool.wait_ge(s_kept, 1)
                pool.dma_start(d_i[:, :], src[0:ROWS, :].rearrange("r c -> (r c)").rearrange("(p j) -> p j", p=P)).then_inc(s_src, 16)
                with pool.Fori(0, ROWS) as j:
                    pool.wait_ge(s_place, j + 1)
                    pool.sem_inc(s_mark, 1)
                    for k, tab in enumerate((edge_src, edge_dst)):
                        pool.indirect_dma_start(tab, bass.IndirectOffsetOnAxis(gi[:, 0:1], 0), ends[:, k:k + 1], None
                                                ).then_inc(s_moved, 16)
                pool.wait_ge(s_moved, 32 * ROWS)
            pool.wait_ge(s_rows, 1)
            for k, tab in enumerate((edge_src, edge_dst)):
                for c in range(VC):
                    pool.indirect_dma_start(rows_i[0:VP, k, c, :], None, tab.rearrange("(r c) o -> r (c o)", c=P),
                                            bass.IndirectOffsetOnAxis(row_i[0:VP, c:c + 1], 0)).then_inc(s_rg, 16)
            for layer, (tab, width, heads) in enumerate(((tab1, TAB1, H1), (tab2, TAB2, H2))):
                if layer == 0:
                    pool.memset(acc[:, :, :], 0.0).then_inc(s_clear, 1)
                else:
                    pool.wait_ge(s_xn, NT)
                    pool.wait_ge(s_w, 16 * 10)
                    pool.tensor_tensor(xs[:, :, :], xs[:, :, :], b2r[:, :].unsqueeze(1).broadcast_to([P, NT, D]), ALU.add
                                       ).then_inc(s_xb, 1)
                pool.wait_ge(s_mm, layer + 1)
                pool.partition_all_reduce(es_all[:, 0:2 * heads], es_mm[:, 0:2 * heads], P, RED.max).then_inc(s_ar, 1)
                pool.wait_ge(s_tabw, 16 * NT * (layer + 1))
                pool.wait_ge(s_flag, layer + 2)
                wide_spread = pool.value_load(flags[0:1, layer + 1:layer + 2], min_val=0, max_val=1)
                with pool.If(wide_spread > 0):
                    with pool.Fori(0, VIS) as n:
                        pool.wait_ge(s_mi[layer], n + 1)
                        pool.sem_inc(s_mark, 1)
                        pool.indirect_dma_start(G[:, 0, 0:width], None, tab, bass.IndirectOffsetOnAxis(gi[:, 0:1], 0)
                                                ).then_inc(s_mg[layer], 16)
                    pool.wait_ge(s_mg[layer], 16 * VIS)
                    pool.wait_ge(s_mt[layer], VIS)
                def gather_batch(i, q):
                    pool.wait_ge(s_idx, i * QB + (layer * NB + q + 1))
                    pool.sem_inc(s_mark, 1)
                    for k in range(BV):
                        pool.indirect_dma_start(G[:, q * BV + k, 0:width], None, tab,
                                                bass.IndirectOffsetOnAxis(IDX[:, q, k:k + 1], 0)
                                                ).then_inc(s_g[q * BV + k], 16)
                with pool.Fori(0, IT) as i:
                    for q in range(QB):
                        gather_batch(i, q)
                for q in range(TAIL):
                    gather_batch(IT, q)
            for k in range(2):
                for t in range(0, NT, SET):
                    m = slice(t, t + SET)
                    pool.wait_ge(s_ob, k * (NT // SET) + t // SET + 1)
                    pool.tensor_tensor(oha[:, k, m, :], oha[:, k, m, :],
                                       cid[:, k, m].unsqueeze(2).broadcast_to([P, SET, SLOT_TILES]), ALU.mult).then_inc(s_ob2, 1)
            for k in range(4):
                pool.wait_ge(s_xt[k], 16 * ((NT - k + 3) // 4))
            pool.wait_ge(s_slot, 1)

            def gather_tokens(g):
                pool.wait_ge(s_gi, g + 1)
                pool.sem_inc(s_mark, 1)
                pool.indirect_dma_start(xg, None, xtab, bass.IndirectOffsetOnAxis(gi[:, 0:1], 0)).then_inc(s_xg, 16)

            def scatter_results(n):
                pool.wait_ge(s_ys, n + 1)
                pool.sem_inc(s_mark, 1)
                pool.indirect_dma_start(ytab, bass.IndirectOffsetOnAxis(si[:, 0:1], 0), ys, None).then_inc(s_sc, 16)

            gather_tokens(0)
            with pool.Fori(0, EXPERTS) as e:
                n_e = pool.value_load(etab[0:1, 0, ds(e, 1)], min_val=1, max_val=NT)
                b_e = pool.value_load(etab[0:1, 1, ds(e, 1)], min_val=0, max_val=MAX_TILES)
                with pool.Fori(0, n_e) as i:
                    gather_tokens(b_e + i + 1)
                    scatter_results(b_e + i)
            b_e = pool.value_load(etab[0:1, 1, EXPERTS - 1:EXPERTS], min_val=0, max_val=MAX_TILES)
            n_e = pool.value_load(etab[0:1, 0, EXPERTS - 1:EXPERTS], min_val=1, max_val=NT)
            scatter_results(b_e + n_e)

        @block.scalar
        def _(act):
            act.dma_start(edge_src.rearrange("(r c) o -> r (c o)", c=P), src).then_inc(s_copy, 16)
            act.dma_start(edge_dst.rearrange("(r c) o -> r (c o)", c=P), dst).then_inc(s_copy, 16)
            act.wait_ge(s_zero, 2)
            act.dma_start(dn_i[0:P - 1, :], dst[0:ROWS, :].rearrange("r c -> (r c)").rearrange("(p j) -> p j", p=P)[1:P, 0:2]).then_inc(s_dn, 16)
            act.dma_start(w1a[:, :, 0:D], g_w1.rearrange("(k p) n -> p k n", p=P)).then_inc(s_w, 16)
            for k, a in enumerate((g_a1s, g_a1d)):
                act.dma_start(a1[:, k, :], a.rearrange("h c -> (h c)").unsqueeze(0).partition_broadcast(P)).then_inc(s_w, 16)
            act.dma_start(w2a[:, :, 0:D], g_w2.rearrange("(k p) n -> p k n", p=P)).then_inc(s_w, 16)
            for k, a in enumerate((g_a2s, g_a2d)):
                act.dma_start(a2[:, k, :], a.partition_broadcast(P)).then_inc(s_w, 16)
            act.dma_start(wr[:, :, :], f_wr.rearrange("(k p) n -> p k n", p=P)).then_inc(s_w, 16)
            act.dma_start(b1r[:, :], g_b1.unsqueeze(0).partition_broadcast(P)).then_inc(s_w, 16)
            act.dma_start(b2r[:, :], g_b2.unsqueeze(0).partition_broadcast(P)).then_inc(s_w, 16)
            act.dma_start(brr[:, :], f_br.unsqueeze(0).partition_broadcast(P)).then_inc(s_w, 16)
            r = 0
            for v in (f_b1, f_lng, f_lnb):
                n = v.shape[0] * v.shape[1] // P
                act.dma_start(vecs[r:r + n, :], v.rearrange("e (c p) -> (e c) p", p=P)).then_inc(s_vec, 16)
                r += n
            for v in (g_lng, g_lnb):
                act.dma_start(vecs[r:r + 2, :], v.rearrange("(c p) -> c p", p=P)).then_inc(s_vec, 16)
                r += 2

            def roots(n):
                act.wait_ge(s_var, n)
                act.activation(root[:, :], tmp_a[:, :], ACT.Sqrt).then_inc(s_root, 1)

            for layer, heads in enumerate((H1, H2)):
                nb = layer * NT
                roots(layer + 1)
                def put_T(t, s):
                    act.wait_ge(s_T, nb + t + 1)
                    ring(act, s_H, nb, t, 4)
                    psT = bank[s % 2][:, 0:D].rearrange("p (k n) -> p k n", k=2)
                    if layer == 0:
                        act.activation(xnT[:, s, :, :], psT, ACT.Copy).then_inc(s_TS, 1)
                    else:
                        for k in range(2):
                            ins = act.activation(xnT[:, s, k, :], psT[:, k, :], ACT.Relu,
                                                 scale=cols[:, 96 + k:97 + k], bias=cols[:, 98 + k:99 + k])
                        ins.then_inc(s_TS, 1)

                def put_H(t, s):
                    s = s % 2
                    act.wait_ge(s_HE, nb + t + 1)
                    if layer == 0:
                        row = tabs[:, t, 0:W1T].rearrange("p (h c) -> p h c", c=CH + 1)[:, :, 0:CH]
                        act.activation(row, bank[2 + s][:, 0:D].rearrange("p (h c) -> p h c", c=CH), ACT.Copy).then_inc(s_HS, 1)
                    else:
                        act.activation(tabs[:, t, 0:D], bank[2 + s][:, 0:D], ACT.Copy).then_inc(s_HS, 1)
                if layer == 1:
                    act.wait_ge(s_vecT, 2)
                    act.wait_ge(s_tabw, 16 * NT)
                by_fours(act, put_T, put_H, 2)

                def local(i, q):
                    return i * QB + q if isinstance(i, int) else None

                def put_onehot_T(i, q):
                    if local(i, q) is None or local(i, q) < RUN:
                        b = i * QB + (layer * RUN + q)
                        act.wait_ge(s_ohT, b + 1)
                        after(act, s_look, b - 1)
                        act.activation(OHT[:, q % 2, :], bankb[q % 2], ACT.Copy).then_inc(s_ohS, 1)

                def put_onehot(i, q):
                    if local(i, q) is None or local(i, q) < NB:
                        act.wait_ge(s_oh, i * QB + (layer * RUN + q + 1))
                        if local(i, q) is None or local(i, q) >= QB:
                            act.wait_ge(s_sum, (i * QB + (layer * NB + q) - QB + 1) * 2)
                        act.activation(OH[:, q % QB, :, :], OHB[:, q % QB, :, :], ACT.Copy).then_inc(s_ohf, 1)

                def put_indices(i, q):
                    if local(i, q) is None or local(i, q) < NB:
                        col = i * (QB * BV) + q * BV
                        act.activation(IDX[:, q % QB, :], src_v[:, ds(col, BV)] if not isinstance(col, int) else src_v[:, col:col + BV],
                                       ACT.Copy).then_inc(s_idx, 1)

                def weights(i, q):
                    if local(i, q) is None or local(i, q) < NB:
                        act.wait_ge(s_u, i * QB + (layer * NB + q + 1))
                        act.activation(WT[:, q % 2, :, 0:heads], U[:, q % 2, :, 0:heads], ACT.Exp).then_inc(s_exp, 1)

                if layer == 0:
                    act.wait_ge(s_vtab, 1)
                after(act, s_msg, layer * NB)
                for q in range(3):
                    put_indices(0, q)
                for q in range(AHEAD):
                    put_onehot_T(0, q)
                weights(0, 0)
                put_onehot(0, 0)

                def body(i, batches=QB):
                    for q in range(batches):
                        after(act, s_msg, i * QB + (layer * NB + q))
                        put_indices(i, q + 3)
                        weights(i, q + 1)
                        put_onehot(i, q + 1)
                        put_onehot_T(i, q + AHEAD)
                body(0)
                with act.Fori(1, IT - 1) as i:
                    body(i)
                body(IT - 1)
                body(IT, TAIL)

            roots(3)
            roots(4)
            def put_T3(t, s):
                act.wait_ge(s_T, 2 * NT + t + 1)
                ring(act, s_H, 2 * NT, t, 4)
                act.activation(xnT[:, s, :, :], bank[s % 2][:, 0:D].rearrange("p (k n) -> p k n", k=2), ACT.Copy).then_inc(s_TS, 1)
            by_fours(act, put_T3)
            act.wait_ge(s_gx, 1)
            act.activation(gate[:, 1, :], first[:, :], ACT.Exp).then_inc(s_ge, 1)

            act.wait_ge(s_slot, 1)
            with act.Fori(0, EXPERTS // 2) as j:
                for c in range(2):
                    e = j * 2 + c
                    n_e = act.value_load(etab[0:1, 0, ds(e, 1)], min_val=1, max_val=NT)
                    b_e = act.value_load(etab[0:1, 1, ds(e, 1)], min_val=0, max_val=MAX_TILES)
                    with act.Fori(0, n_e) as i:
                        for f in range(FC):
                            if f % 2 == 0:
                                act.wait_ge(s_h, (b_e + i) * (FC // 2) + (f // 2 + 1))
                            act.activation(hid[:, f, :], bank[HB[f // 2]][:, (f % 2) * P:(f % 2 + 1) * P], ACT.Gelu,
                                           bias=cols[:, ds(e * FC + f, 1)]).then_inc(s_hg, 1)
            for c in range(NT // SET):
                full = SET if c < NT // SET - 1 else SET - 1
                act.wait_ge(s_o, c + 1)
                act.dma_start(out[c * SET * P:(c * SET + full) * P, :].rearrange("(t p) d -> p t d", p=P),
                              xs[:, c * SET:c * SET + full, :]).then_inc(s_st, 16)
            act.dma_start(out[(NT - 1) * P:N, :], xs[0:LAST, NT - 1, :]).then_inc(s_st, 16)
            act.wait_ge(s_st, 16 * (NT // SET + 1))

        @block.tensor
        def _(pe):
            pe.wait_ge(s_pool, 8)
            pe.wait_ge(s_cnt, 1)
            pe.matmul(bank[4][:, 0:NT + 3], ones[:, :], cnt[:, :], start=True, stop=True).then_inc(s_starts, 1)
            pe.matmul(bank[3][:, 0:NT + 1], upper[:, :], cnt[:, 0:NT + 1], start=True, stop=True).then_inc(s_below, 1)
            pe.wait_ge(s_vec, 16 * 5)
            pe.transpose(bank[5][:, 0:100], vecs[0:100, :], ident[0:100, 0:100]).then_inc(s_vecT, 1)
            pe.wait_ge(s_rows, 1)
            for c in range(VC):
                ins = pe.matmul(bank[4][0:1, c * VP:(c + 1) * VP], vt[0:VP, c:c + 1], ident[0:VP, 0:VP], start=True, stop=True)
            ins.then_inc(s_tilt, 1)
            pe.wait_ge(s_rf, 1)
            for k in range(2):
                for c in range(VC):
                    ins = pe.transpose(bank[6 + k][:, c * VP:(c + 1) * VP], rows_f[0:VP, k, c, :], ident[0:VP, 0:VP])
            ins.then_inc(s_rT, 1)

            def node_phase(ph, rhs, width):
                nb = ph * NT

                def T(t, s):
                    pe.wait_ge(s_xn, nb + t + 1)
                    ring(pe, s_TS, nb, t)
                    for k in range(2):
                        ins = pe.transpose(bank[s % 2][:, k * P:(k + 1) * P], xn[:, s, k * P:(k + 1) * P], ident[:, :])
                    ins.then_inc(s_T, 1)

                def Hm(t, s):
                    pe.wait_ge(s_TS, nb + t + 1)
                    if ph < 2:
                        ring(pe, s_HS, nb, t)
                    ring(pe, s_HE, nb, t)
                    for k in range(2):
                        ins = pe.matmul(bank[2 + s % 2][:, 0:width], xnT[:, s, k, :], rhs[:, k, 0:width], start=(k == 0), stop=(k == 1))
                    ins.then_inc(s_H, 1)
                by_fours(pe, T, Hm, 2)

            for layer, (rhs, heads, width) in enumerate(((w1a, H1, W1T), (w2a, H2, W2T))):
                node_phase(layer, rhs, D + 3 * heads)

                def transpose_onehot(i, q):
                    if isinstance(i, int) and i * QB + q >= RUN:
                        return
                    b = i * QB + (layer * RUN + q)
                    pe.wait_ge(s_oh, b + 1)
                    after(pe, s_ohS, b - 1)
                    for k in range(BV):
                        ins = pe.transpose(bankb[q % 2][:, k * P:(k + 1) * P], OHB[:, q % QB, k, :], ident_b[:, :])
                    ins.then_inc(s_ohT, 1)

                def look_up(i, q):
                    b = i * QB + (layer * RUN + q)
                    pe.wait_ge(s_ohS, b + 1)
                    if not (isinstance(i, int) and i * QB + q < 2):
                        pe.wait_ge(s_u, i * QB + (layer * NB + q - 1))
                    for m in range(BV // 2):
                        col = i * (QB * BV) + (q * BV + 2 * m)
                        ti = pe.value_load(tile_v[0:1, ds(col, 1)] if not isinstance(col, int) else tile_v[0:1, col:col + 1],
                                           min_val=0, max_val=NT)
                        parts = edp[:, ds(ti, 1), :, :]
                        for k in (2 * m, 2 * m + 1):
                            ins = pe.matmul(bank[2 + q % 2][:, k * 6 * HEADS:(k + 1) * 6 * HEADS],
                                            OHT[:, q % 2, k * P:(k + 1) * P], parts, start=True, stop=True)
                    ins.then_inc(s_look, 1)

                def sum_messages(i, q):
                    b = i * QB + (layer * NB + q)
                    pe.wait_ge(s_ohf, b + 1)
                    pe.wait_ge(s_msg, b + 1)
                    after(pe, s_acc, (b - 1) * 2)
                    for k in range(BV):
                        ins = pe.matmul(bank[4 + (q % 2) * 2 + k // 2][:, 0:width], OH[:, q, k, :], MSG[:, q % 2, k, 0:width],
                                        start=(k % 2 == 0), stop=(k % 2 == 1))
                        if k % 2:
                            ins.then_inc(s_sum, 1)

                pe.wait_ge(s_flag, layer + 2)
                wide_spread = pe.value_load(flags[0:1, layer + 1:layer + 2], min_val=0, max_val=1)
                with pe.If(wide_spread > 0):
                    with pe.Fori(0, VIS) as n:
                        pe.wait_ge(s_md[layer], n + 1)
                        pe.transpose(bank[0][:, 0:P], OH[:, 0, 0, :], ident[:, :])
                        pe.matmul(bank[1][:, 0:heads * P], ones[:, :], wide[:, 0, 0:heads * P], start=True, stop=True
                                  ).then_inc(s_mt[layer], 1)
                pe.wait_ge(s_shift, layer + 1)
                transpose_onehot(0, 0)
                transpose_onehot(0, 1)
                look_up(0, 0)
                transpose_onehot(0, 2)
                look_up(0, 1)

                def body(i, batches=QB):
                    for q in range(batches):
                        look_up(i, q + 2)
                        transpose_onehot(i, q + AHEAD)
                        sum_messages(i, q)
                body(0)
                with pe.Fori(1, IT) as i:
                    body(i)
                body(IT, TAIL)

            node_phase(2, wr, EXPERTS)
            pe.wait_ge(s_ohm, 1)
            m = ohm[:, :, :].rearrange("p t e -> p (t e)")
            pe.matmul(bank[4][:, 0:NT * EXPERTS], upper[:, :], m, start=True, stop=True)
            pe.matmul(bank[5][:, 0:NT * EXPERTS], ones[:, :], m, start=True, stop=True).then_inc(s_pre, 1)

            for k in range(2):
                for t in range(NT):
                    if t % SET == 0:
                        pe.wait_ge(s_ob, k * (NT // SET) + t // SET + 1)
                        pe.wait_ge(s_ob2, k * (NT // SET) + t // SET + 1)
                    ins = pe.matmul(bank[6][:, 0:SLOT_TILES], ohb[:, k, t, :], oha[:, k, t, :],
                                    start=(k == 0 and t == 0), stop=(k == 1 and t == NT - 1))
            ins.then_inc(s_om, 1)

            def tokens_T(g):
                pe.wait_ge(s_xg, g * 16 + 16)
                for k in range(2):
                    ins = pe.transpose(bank[2][:, k * P:(k + 1) * P], xg[:, k * P:(k + 1) * P], ident[:, :])
                ins.then_inc(s_xT, 1)

            pe.wait_ge(s_slot, 1)
            tokens_T(0)
            with pe.Fori(0, EXPERTS // 2) as j:
                for c in range(2):
                    e = j * 2 + c
                    n_e = pe.value_load(etab[0:1, 0, ds(e, 1)], min_val=1, max_val=NT)
                    b_e = pe.value_load(etab[0:1, 1, ds(e, 1)], min_val=0, max_val=MAX_TILES)
                    pe.wait_ge(s_fw[c], j * 48 + 48)
                    pe.sem_inc(s_mark, 1)
                    with pe.Fori(0, n_e) as i:
                        g = b_e + i
                        pe.wait_ge(s_xe, g + 1)
                        for f in range(FC):
                            for k in range(2):
                                ins = pe.matmul(bank[HB[f // 2]][:, (f % 2) * P:(f % 2 + 1) * P],
                                                fw1[:, c, k, f * P:(f + 1) * P], xeT[:, k, :], start=(k == 0), stop=(k == 1))
                            if f % 2:
                                ins.then_inc(s_h, 1)
                        tokens_T(g + 1)
                        pe.wait_ge(s_ys, g + 1)
                        for f in range(FC):
                            pe.wait_ge(s_hg, g * FC + (f + 1))
                            ins = pe.matmul(bank[3][:, 0:D], hid[:, f, :], fw2[:, c, f, :], start=(f == 0), stop=(f == FC - 1))
                        ins.then_inc(s_y, 1)

        @block.vector
        def _(v):
            ch = Chain(v, s_dve)
            link = ch.link

            def sort_edges():
                so = Chain(v, s_sort)
                v.wait_ge(s_below, 1)
                v.tensor_copy(below[:, 0:NT + 1], bank[3][:, 0:NT + 1])
                so.link(v.tensor_scalar(below[:, NT + 1:NT + 2], part_f[:, :], float(ROWS), None, ALU.mult))
                v.tensor_scalar(limit[:, :], iota_p[:, 0:NT + 2], float(P), None, ALU.mult)
                so.link(v.tensor_tensor(start[:, :], below[:, 1:NT + 2], below[:, 0:NT + 1], ALU.subtract))
                so.link(v.scalar_tensor_tensor(start[:, :], start[:, :], -1.0, st[:, 0:NT + 1], ALU.add, ALU.add))
                place, inside, rank, all_ones, d_f, junk = (tabs[:, 2 * k:2 * k + 2, :].rearrange("p t c -> p (t c)")[:, 0:ROWS]
                                                            for k in range(6))
                so.link(v.tensor_copy(d_f, d_i[:, :]))
                v.sem_inc(s_kept, 1)
                v.memset(all_ones, 1.0)
                so.link(v.memset(limit[:, NT + 1:NT + 2], 10.0 * PAD_DST))
                so.link(v.memset(place, 0.0))
                with v.Fori(0, NT + 1) as t:
                    so.enter(t, 0, 5)
                    so.link(v.tensor_scalar(junk, d_f, limit[:, ds(t + 1, 1)], None, ALU.is_lt))
                    so.link(v.scalar_tensor_tensor(inside, d_f, limit[:, ds(t, 1)], junk, ALU.is_ge, ALU.mult))
                    so.link(v.tensor_tensor_scan(rank, all_ones, inside, 0.0, ALU.mult, ALU.add))
                    so.link(v.scalar_tensor_tensor(rank, rank, start[:, ds(t, 1)], inside, ALU.add, ALU.mult))
                    so.link(v.tensor_tensor(place, place, rank, ALU.add))
                so.leave(NT + 1)
                v.wait_ge(s_src, 16)

                def move(j):
                    v.tensor_copy(gi[:, :], place[:, ds(j, 1)] if not isinstance(j, int) else place[:, j:j + 1])
                    v.tensor_copy(ends[:, 0:1], d_i[:, ds(j, 1)])
                    v.tensor_copy(ends[:, 1:2], d_f[:, ds(j, 1)]).then_inc(s_place, 1)
                move(0)
                with v.Fori(1, ROWS) as j:
                    v.wait_ge(s_moved, j * 32)
                    move(j)
                v.wait_ge(s_moved, ROWS * 32)

            def true_maxima(layer, heads, wt):
                mc = Chain(v, s_mc[layer])
                least = es_all[:, heads:2 * heads].unsqueeze(1).broadcast_to([P, NT + 1, heads])
                mc.link(v.tensor_scalar(bound[:, :, 0:heads], least, -1.0, None, ALU.mult))
                spread = wide[:, 0, 0:heads * P].rearrange("p (h e) -> p h e", h=heads)
                with v.Fori(0, VIS) as n:
                    mc.enter(n, 0, 5)
                    v.tensor_copy(gi[:, :], src_v[:, ds(n, 1)]).then_inc(s_mi[layer], 1)
                    v.tensor_scalar(OH[:, 0, 0, :], iota_p[:, :], dst_v[:, ds(n, 1)], None, ALU.is_equal)
                    v.wait_ge(s_mg[layer], n * 16 + 16)
                    for h in range(heads):
                        ins = v.tensor_scalar(spread[:, h, :], ident[:, :], G[:, 0, wt + h:wt + h + 1], None, ALU.mult)
                    mc.link(ins)
                    v.sem_inc(s_md[layer], 1)
                    v.wait_ge(s_mt[layer], n + 1)
                    mc.link(v.tensor_scalar(wide[:, 1, 0:P], bank[0][:, 0:P], 1e30, -1e30, ALU.mult, ALU.add))
                    mc.link(v.tensor_tensor(spread, bank[1][:, 0:heads * P].rearrange("p (h e) -> p h e", h=heads),
                                            wide[:, 1, 0:P].unsqueeze(1).broadcast_to([P, heads, P]), ALU.add))
                    mc.link(v.tensor_reduce(max_e[:, 0:heads], spread, AX.X, ALU.max))
                    ti = v.value_load(tile_v[0:1, ds(n, 1)], min_val=0, max_val=NT)
                    b = bound[:, ds(ti, 1), 0:heads].rearrange("p o h -> p (o h)")
                    mc.link(v.tensor_tensor(b, b, max_e[:, 0:heads], ALU.max))
                mc.leave(VIS)

            v.memset(dn_i[:, :], PAD_DST).then_inc(s_zero, 1)
            v.memset(xs[:, NT - 1, :], 0.0).then_inc(s_zero, 1)
            v.memset(dst_v[:, :], float(PAD_DST))
            v.memset(cnt[:, :], 0.0)
            link(v.memset(tile_v[:, :], 0))

            v.wait_ge(s_pool, 8)
            v.tensor_copy(iota_p[:, :], iota_i[:, :])
            v.tensor_copy(part_f[:, :], part_i[:, :])
            v.tensor_copy(vnum[:, :], v_i[:, :])
            v.tensor_copy(ident_b[:, :], ident[:, :])
            v.wait_ge(s_dst, 16)
            link(v.tensor_scalar(d_t[:, :], d_i[:, :], 7, None, ALU.arith_shift_right))
            link(v.tensor_copy(d_b[:, :], d_t[:, :]))
            for t in range(1, NT + 1):
                ins = v.tensor_scalar(junk_b[:, t % 2, :], d_b[:, :], float(t), 0.0, ALU.is_lt, ALU.add, accum_out=cnt[:, t:t + 1])
                if t % 2 == 0 or t == NT:
                    link(ins)
            link(v.tensor_tensor(junk_b[:, 0, 0:ROWS - 1], d_b[:, 0:ROWS - 1], d_b[:, 1:ROWS], ALU.is_gt))
            v.tensor_reduce(cnt[:, NT + 1:NT + 2], junk_b[:, 0, 0:ROWS - 1], AX.X, ALU.add)
            v.wait_ge(s_dn, 16)
            link(v.tensor_scalar(dn_i[:, :], dn_i[:, :], 7, None, ALU.arith_shift_right))
            link(v.tensor_tensor(cnt[:, NT + 2:NT + 3], d_t[:, ROWS - 1:ROWS], dn_i[:, 0:1], ALU.is_gt))
            v.sem_inc(s_cnt, 1)
            v.wait_ge(s_starts, 1)
            link(v.tensor_copy(st[:, :], bank[4][:, 0:NT + 3]))
            link(v.tensor_tensor(fl_f[:, 0:1], st[:, NT + 1:NT + 2], st[:, NT + 2:NT + 3], ALU.add))
            link(v.tensor_scalar(flags[:, 0:1], fl_f[:, 0:1], 0.0, None, ALU.is_gt))
            v.sem_inc(s_flag, 1)
            unsorted = v.value_load(flags[0:1, 0:1], min_val=0, max_val=1)
            with v.If(unsorted > 0):
                sort_edges()
            v.tensor_copy(st_i[:, 0, :], st[:, 0:NT])
            link(v.tensor_scalar(st_i[:, 1, :], st[:, 1:NT + 1], float(P - 1), None, ALU.add))
            link(v.tensor_scalar(st_i[:, :, :], st_i[:, :, :], 7, None, ALU.arith_shift_right))
            link(v.tensor_copy(lo_hi[:, :, :], st_i[:, :, :]))
            link(v.tensor_tensor(nvis[:, :], lo_hi[:, 1, :], lo_hi[:, 0, :], ALU.subtract))
            link(v.tensor_tensor(off[:, :], st[:, 1:NT + 1], st[:, 0:NT], ALU.is_gt))
            link(v.tensor_tensor(nvis[:, :], nvis[:, :], off[:, :], ALU.mult))
            link(v.tensor_scalar(nall[:, :], iota_p[:, 0:NT], float(LOOP_ROWS), None, ALU.is_lt))
            link(v.tensor_tensor(nall[:, :], nall[:, :], nvis[:, :], ALU.add))
            link(v.tensor_scalar(st_i[:, 0, :], nall[:, :], 1.0, None, ALU.add))
            link(v.tensor_scalar(st_i[:, 0, :], st_i[:, 0, :], 1, None, ALU.arith_shift_right))
            link(v.tensor_scalar(nall[:, :], st_i[:, 0, :], 2.0, None, ALU.mult))
            link(v.tensor_tensor_scan(cum[:, :], ones[:, 0:NT], nall[:, :], 0.0, ALU.mult, ALU.add))
            link(v.tensor_tensor(nall[:, :], cum[:, :], nall[:, :], ALU.subtract))
            link(v.tensor_tensor(off[:, :], lo_hi[:, 0, :], nall[:, :], ALU.subtract))
            link(v.tensor_tensor(nall[:, :], nall[:, :], nvis[:, :], ALU.add))
            vb = vnum[:, :].unsqueeze(2).broadcast_to([P, VC, NT])
            link(v.tensor_tensor(ge[:, :, :], vb, cum[:, :].unsqueeze(1).broadcast_to([P, VC, NT]), ALU.is_ge))
            link(v.tensor_reduce(vt[:, :], ge[:, :, :], AX.X, ALU.add))
            link(v.tensor_tensor(ge[:, :, :], vt[:, :].unsqueeze(2).broadcast_to([P, VC, NT]),
                                 iota_p[:, 0:NT].unsqueeze(1).broadcast_to([P, VC, NT]), ALU.is_equal))
            link(v.tensor_tensor(ge2[:, :, :], ge[:, :, :], nall[:, :].unsqueeze(1).broadcast_to([P, VC, NT]), ALU.mult))
            link(v.tensor_tensor(ge[:, :, :], ge[:, :, :], off[:, :].unsqueeze(1).broadcast_to([P, VC, NT]), ALU.mult))
            v.tensor_reduce(vy[:, :], ge2[:, :, :], AX.X, ALU.add)
            link(v.tensor_reduce(vr[:, :], ge[:, :, :], AX.X, ALU.add))
            v.tensor_scalar(vx[:, :], vt[:, :], float(LOOP_ROWS), None, ALU.is_lt)
            link(v.tensor_tensor(vz[:, :], vnum[:, :], vy[:, :], ALU.is_equal))
            link(v.tensor_tensor(vx[:, :], vx[:, :], vz[:, :], ALU.mult))
            link(v.tensor_scalar(vz[:, :], vt[:, :], float(ROWS - EMPTY_ROW), None, ALU.add))
            link(v.tensor_tensor(vx[:, :], vx[:, :], vz[:, :], ALU.mult))
            v.tensor_tensor(vy[:, :], vnum[:, :], vy[:, :], ALU.is_lt)
            link(v.scalar_tensor_tensor(vr[:, :], vr[:, :], float(-EMPTY_ROW), vnum[:, :], ALU.add, ALU.add))
            link(v.tensor_tensor(vr[:, :], vr[:, :], vy[:, :], ALU.mult))
            link(v.scalar_tensor_tensor(vr[:, :], vr[:, :], float(EMPTY_ROW), vx[:, :], ALU.add, ALU.add))
            link(v.tensor_copy(row_i[:, :], vr[:, :]))
            v.sem_inc(s_rows, 1)
            link(v.tensor_scalar(vx[:, :], vt[:, :], float(-P), None, ALU.mult))

            def score_columns(wa, a, heads):
                for k in range(2):
                    for sd in range(2):
                        ins = v.tensor_tensor(prod[:, k, sd, :], wa[:, k, 0:D], a[:, sd, :], ALU.mult)
                link(ins)
                for sd in range(2):
                    ins = v.tensor_reduce(wa[:, :, D + 2 * sd * heads:D + (2 * sd + 1) * heads],
                                          prod[:, :, sd, :].rearrange("p k (h c) -> p k h c", h=heads), AX.X, ALU.add)
                link(ins)
                link(v.tensor_scalar(wa[:, :, D + heads:D + 2 * heads], wa[:, :, D:D + heads], SLOPE, None, ALU.mult))

            def combine():
                m0, m1 = stats[:, :, 1], stats[:, :, 4]
                v.tensor_tensor(tmp_a[:, :], stats[:, :, 2], stats[:, :, 5], ALU.add)
                v.tensor_tensor(tmp_b[:, :], m0, m1, ALU.subtract)
                link(v.tensor_tensor(mean[:, :], m0, m1, ALU.add))
                v.tensor_scalar(mean[:, :], mean[:, :], 0.5, None, ALU.mult)
                link(v.tensor_tensor(tmp_b[:, :], tmp_b[:, :], tmp_b[:, :], ALU.mult))
                link(v.tensor_scalar(tmp_b[:, :], tmp_b[:, :], 0.25, None, ALU.mult))
                link(v.scalar_tensor_tensor(var[:, :], tmp_a[:, :], 1.0 / D, tmp_b[:, :], ALU.mult, ALU.add))

            def inverse_root(n):
                link(v.tensor_scalar(tmp_a[:, :], var[:, :], EPS, None, ALU.add))
                v.sem_inc(s_var, 1)
                v.wait_ge(s_root, n)
                link(v.reciprocal(rstd[:, :], root[:, :]))
                link(v.tensor_tensor(tmp_c[:, :], rstd[:, :], rstd[:, :], ALU.mult))
                link(v.tensor_tensor(tmp_c[:, :], tmp_c[:, :], tmp_a[:, :], ALU.mult))
                link(v.tensor_scalar(tmp_c[:, :], tmp_c[:, :], -0.5, 1.5, ALU.mult, ALU.add))
                link(v.tensor_tensor(rstd[:, :], rstd[:, :], tmp_c[:, :], ALU.mult))

            def row_stats(source, tiles=range(NT)):
                for t in tiles:
                    ins = v.bn_stats(stats[:, t, :], source(t))
                link(ins)

            for c in range(NT // XCH):
                v.wait_ge(s_x[c], 16)
                row_stats(lambda t: xs[:, t, :], range(c * XCH, (c + 1) * XCH))
            v.wait_ge(s_x[4], 16)
            link(v.bn_stats(stats[:, NT - 1, :], xs[:, NT - 1, :]))
            combine()
            inverse_root(1)
            v.wait_ge(s_w, 16 * 10)
            score_columns(w1a, a1, H1)
            v.wait_ge(s_vecT, 1)
            v.tensor_copy(cols[:, :], bank[5][:, 0:100]).then_inc(s_vecT, 1)
            v.wait_ge(s_tilt, 1)
            v.tensor_copy(tile_v[0:1, 0:VIS], bank[4][0:1, 0:VIS])
            v.wait_ge(s_rg, 16 * 2 * VC)
            v.tensor_copy(rows_f[0:VP, 0, :, :], rows_i[0:VP, 0, :, :])
            for c in range(VC):
                ins = v.tensor_scalar(rows_f[0:VP, 1, c, :], rows_i[0:VP, 1, c, :], vx[0:VP, c:c + 1], None, ALU.add)
            link(ins)
            v.sem_inc(s_rf, 1)
            v.wait_ge(s_rT, 1)
            v.tensor_copy(src_v[:, 0:VIS], bank[6][:, 0:VIS])
            link(v.tensor_copy(dst_v[:, 0:VIS], bank[7][:, 0:VIS]))
            v.sem_inc(s_vtab, 1)

            def normalise(ph, source):
                def one(t, s):
                    ring(v, s_T, ph * NT, t, 4)
                    v.tensor_scalar(xn[:, s, :], source(t), mean[:, ds(t, 1)], rstd[:, ds(t, 1)],
                                    ALU.subtract, ALU.mult).then_inc(s_xn, 1)
                return one

            def scores_out(ph, heads):
                def one(t, s):
                    v.wait_ge(s_H, ph * NT + t + 1)
                    wt = W1T if heads == H1 else W2T
                    v.tensor_copy(tabs[:, t, wt:wt + 3 * heads], bank[2 + s % 2][:, D:D + 3 * heads]).then_inc(s_HE, 1)
                return one

            def shifts(layer, heads, wt):
                es = tabs[:, :, wt:wt + heads].rearrange("p t h -> p h t")
                v.wait_ge(s_HE, (layer + 1) * NT)
                link(v.tensor_reduce(es_mm[:, 0:heads], es, AX.X, ALU.max))
                link(v.tensor_reduce(es_mm[:, heads:2 * heads], es, AX.X, ALU.min))
                link(v.tensor_scalar(es_mm[:, heads:2 * heads], es_mm[:, heads:2 * heads], -1.0, None, ALU.mult))
                v.sem_inc(s_mm, 1)
                v.wait_ge(s_ar, layer + 1)
                v.tensor_copy(bound[:, :, 0:heads], es_all[:, 0:heads].unsqueeze(1).broadcast_to([P, NT + 1, heads]))
                link(v.tensor_tensor(fl_f[:, 0:heads], es_all[:, 0:heads], es_all[:, heads:2 * heads], ALU.add))
                link(v.tensor_reduce(fl_f[:, 0:1], fl_f[:, 0:heads], AX.X, ALU.max))
                link(v.tensor_scalar(flags[:, layer + 1:layer + 2], fl_f[:, 0:1], SPREAD, None, ALU.is_gt))
                v.sem_inc(s_flag, 1)
                wide_spread = v.value_load(flags[0:1, layer + 1:layer + 2], min_val=0, max_val=1)
                with v.If(wide_spread > 0):
                    v.wait_ge(s_vtab, 1)
                    true_maxima(layer, heads, wt)
                c = shift[:, :, 0:heads]
                ed = tabs[:, :, wt + 2 * heads:wt + 3 * heads]
                link(v.tensor_tensor(c, ed, bound[:, 0:NT, 0:heads], ALU.add))
                link(v.scalar_tensor_tensor(c, c, SLOPE, c, ALU.mult, ALU.max))
                v.tensor_tensor(edc[:, 0:NT, 0:heads], ed, c, ALU.subtract)
                link(v.scalar_tensor_tensor(edc[:, 0:NT, heads:2 * heads], ed, SLOPE, c, ALU.mult, ALU.subtract))
                rest = edr[:, :, :]
                link(v.tensor_copy(edp[:, :, 0, :], edc[:, :, :]))
                link(v.tensor_tensor(rest, edc[:, :, :], edp[:, :, 0, :], ALU.subtract))
                link(v.tensor_copy(edp[:, :, 1, :], rest))
                link(v.tensor_tensor(rest, rest, edp[:, :, 1, :], ALU.subtract))
                link(v.tensor_copy(edp[:, :, 2, :], rest))
                v.sem_inc(s_shift, 1)

            def edge_loop(layer, heads, wt):
                v.wait_ge(s_vtab, 1)
                if layer == 0:
                    v.wait_ge(s_clear, 1)

                def onehot(i, q):
                    if isinstance(i, int) and i * QB + q >= RUN:
                        return
                    col = i * (QB * BV) + q * BV
                    if not (isinstance(i, int) and i * QB + q < QB):
                        v.wait_ge(s_ohf, i * QB + (layer * NB + q) - QB + 1)
                    cols_ = dst_v[:, ds(col, BV)] if not isinstance(col, int) else dst_v[:, col:col + BV]
                    v.tensor_tensor(OHB[:, q % QB, :, :], cols_.unsqueeze(2).broadcast_to([P, BV, P]),
                                    iota_p[:, :].unsqueeze(1).broadcast_to([P, BV, P]), ALU.is_equal).then_inc(s_oh, 1)

                def exponents(i, q):
                    if isinstance(i, int) and i * QB + q >= NB:
                        return
                    h = q % 2
                    v.wait_ge(s_look, i * QB + (layer * RUN + q + 1))
                    for k in range(BV):
                        slot = (q % QB) * BV + k
                        v.wait_ge(s_g[slot], i * 16 + ((q // QB) * 16 + layer * (IT + (q % QB < TAIL)) * 16 + 16))
                    ps = bank[2 + h][:, 0:BV * 6 * HEADS].rearrange("p (k t c) -> p k c t", k=BV, t=3)
                    scores = G[:, (q % QB) * BV:(q % QB + 1) * BV, wt:wt + 2 * heads]
                    link(v.tensor_reduce(Z[:, h, :, :], ps, AX.X, ALU.add))
                    link(v.tensor_tensor(Z[:, h, :, 0:2 * heads], scores, Z[:, h, :, 0:2 * heads], ALU.add))
                    v.tensor_tensor(U[:, h, :, 0:heads], Z[:, h, :, 0:heads], Z[:, h, :, heads:2 * heads], ALU.max).then_inc(s_u, 1)

                def accumulate(i, q):
                    for m in range(BV // 2):
                        col = i * (QB * BV) + (q * BV + 2 * m)
                        ti = v.value_load(tile_v[0:1, ds(col, 1)] if not isinstance(col, int) else tile_v[0:1, col:col + 1],
                                          min_val=0, max_val=NT)
                        n = i * (QB * 2) + (layer * NB * 2 + q * 2 + m)
                        v.wait_ge(s_sum, n + 1)
                        after(v, s_acc, n)
                        a = acc[:, ds(ti, 1), 0:wt].rearrange("p o c -> p (o c)")
                        v.tensor_tensor(a, a, bank[4 + (q % 2) * 2 + m][:, 0:wt], ALU.add).then_inc(s_acc, 1)

                def step(i, q, first=False):
                    exponents(i, q + 1)
                    onehot(i, q + AHEAD)
                    h, b = q % 2, i * QB + (layer * NB + q)
                    rows = G[:, q * BV:(q + 1) * BV, :]
                    v.wait_ge(s_exp, b + 1)
                    if not (isinstance(i, int) and i * QB + q < 2):
                        v.wait_ge(s_sum, (b - 1) * 2)
                    if heads == 4:
                        for k in range(BV):
                            ins = v.tensor_tensor(MSG[:, h, k, 0:wt].rearrange("p (h c) -> p h c", c=CH + 1),
                                                  rows[:, k, 0:wt].rearrange("p (h c) -> p h c", c=CH + 1),
                                                  WT[:, h, k, :].unsqueeze(2).broadcast_to([P, HEADS, CH + 1]), ALU.mult)
                    else:
                        ins = v.tensor_tensor(MSG[:, h, :, 0:wt], rows[:, :, 0:wt],
                                              WT[:, h, :, 0:1].broadcast_to([P, BV, wt]), ALU.mult)
                    ins.then_inc(s_msg, 1)
                    if not first:
                        accumulate(*((i, q - 1) if q else (i - 1, QB - 1)))

                for q in range(AHEAD):
                    onehot(0, q)
                if layer == 0:
                    score_columns(w2a, a2, H2)
                else:
                    v.wait_ge(s_xn, 2 * NT)
                    link(v.memset(acc[:, :, :], 0.0))
                exponents(0, 0)
                for q in range(QB):
                    step(0, q, first=(q == 0))
                with v.Fori(1, IT) as i:
                    ch.enter(i, 1, 2 * QB)
                    for q in range(QB):
                        step(i, q)
                ch.leave(IT - 1)
                for q in range(TAIL):
                    step(IT, q)
                accumulate(IT, TAIL - 1)
                v.wait_ge(s_acc, (layer + 1) * NB * 2)

            v.memset(tabs[:, :, 0:W1T].rearrange("p t (h c) -> p t h c", c=CH + 1)[:, :, :, CH:CH + 1], 1.0)
            link(v.memset(edc[:, :, :], 0.0))
            by_fours(v, normalise(0, lambda t: xs[:, t, :]), scores_out(0, H1), 3)
            shifts(0, H1, W1T)
            edge_loop(0, H1, W1T)

            heads_view = acc[:, 0:NT, :].rearrange("p t (h c) -> p (t h) c", c=CH + 1)
            rd = rden[:, :, :].rearrange("p t h -> p (t h)")
            link(v.tensor_scalar(rd, heads_view[:, :, CH], 1e-37, None, ALU.max))
            link(v.reciprocal(rd, rd))
            link(v.tensor_tensor(heads_view[:, :, 0:CH], heads_view[:, :, 0:CH],
                                 rd.unsqueeze(2).broadcast_to([P, NT * HEADS, CH]), ALU.mult))
            o1 = acc[:, 0:NT, :].rearrange("p t (h c) -> p t h c", c=CH + 1)[:, :, :, 0:CH]
            for h in range(HEADS):
                ins = v.tensor_tensor(o1[:, :, h, :], o1[:, :, h, :],
                                      b1r[:, h * CH:(h + 1) * CH].unsqueeze(1).broadcast_to([P, NT, CH]), ALU.add)
            link(ins)

            def o1_row(t):
                return (acc[:, t:t + 1, :] if isinstance(t, int) else acc[:, ds(t, 1), :]).rearrange("p o (h c) -> p (o h) c", c=CH + 1)[:, :, 0:CH]
            row_stats(o1_row)
            combine()
            inverse_root(2)
            v.wait_ge(s_tabw, 16 * NT)
            link(v.memset(tabs[:, :, D:D + 1], 1.0))

            def normalise1(t, s):
                ring(v, s_T, NT, t, 4)
                v.tensor_scalar(xn[:, s, :].rearrange("p (h c) -> p h c", c=CH), o1_row(t), mean[:, ds(t, 1)], rstd[:, ds(t, 1)],
                                ALU.subtract, ALU.mult).then_inc(s_xn, 1)
            by_fours(v, normalise1, scores_out(1, H2), 3)
            shifts(1, H2, W2T)
            edge_loop(1, H2, W2T)

            rd2 = rden[:, :, 0]
            link(v.tensor_scalar(rd2, acc[:, 0:NT, D], 1e-37, None, ALU.max))
            link(v.reciprocal(rd2, rd2))
            v.wait_ge(s_xb, 1)
            for t in range(NT):
                ins = v.scalar_tensor_tensor(xs[:, t, :], acc[:, t, 0:D], rden[:, t, 0:1], xs[:, t, :], ALU.mult, ALU.add)
            link(ins)
            row_stats(lambda t: xs[:, t, :])
            combine()
            inverse_root(3)
            link(v.tensor_copy(tmp_b[:, :], rstd[:, :]))
            for _ in range(2):
                link(v.tensor_tensor(var[:, :], var[:, :], rstd[:, :], ALU.mult))
            inverse_root(4)
            link(v.tensor_tensor(rstd[:, :], rstd[:, :], tmp_b[:, :], ALU.mult))

            def normalise2(t, s):
                ring(v, s_T, 2 * NT, t, 4)
                if not isinstance(t, int) or t >= 4:
                    v.wait_ge(s_xt[s], (t - s) * 4)
                v.tensor_scalar(xn[:, s, :], xs[:, t, :], mean[:, ds(t, 1)], rstd[:, ds(t, 1)],
                                ALU.subtract, ALU.mult).then_inc(s_xn, 1)

            def logits_out(t, s):
                v.wait_ge(s_H, 2 * NT + t + 1)
                v.tensor_copy(lg[:, t, :], bank[2 + s % 2][:, 0:EXPERTS]).then_inc(s_HE, 1)
            by_fours(v, normalise2, logits_out, 3)
            v.wait_ge(s_HE, 3 * NT)

            def over_e(a):
                return a.unsqueeze(2).broadcast_to([P, NT, EXPERTS])
            i8 = iota_m8[:, :].unsqueeze(1).broadcast_to([P, NT, EXPERTS])
            v.tensor_scalar(iota_m8[:, :], iota_p[:, 0:EXPERTS], float(-EXPERTS), None, ALU.add)
            v.memset(valid[:, :], 1.0)
            link(v.tensor_tensor(lg[:, :, :], lg[:, :, :], brr[:, :].unsqueeze(1).broadcast_to([P, NT, EXPERTS]), ALU.add))
            link(v.tensor_scalar(valid[:, NT - 1:NT], part_f[:, :], float(LAST), None, ALU.is_lt))
            for k in range(2):
                l = (lg, lg2)[k]
                link(v.tensor_reduce(top[:, k, :], l[:, :, :], AX.X, ALU.max))
                link(v.tensor_tensor(cand[:, :, :], l[:, :, :], over_e(top[:, k, :]), ALU.is_equal))
                link(v.tensor_tensor(cand[:, :, :], cand[:, :, :], i8, ALU.mult))
                link(v.tensor_reduce(first[:, :], cand[:, :, :], AX.X, ALU.min))
                link(v.tensor_tensor(oh[:, k, :, :], over_e(first[:, :]), i8, ALU.is_equal))
                if k == 0:
                    link(v.scalar_tensor_tensor(lg2[:, :, :], oh[:, 0, :, :], -BIG, lg[:, :, :], ALU.mult, ALU.add))
            link(v.tensor_tensor(first[:, :], top[:, 1, :], top[:, 0, :], ALU.subtract))
            v.sem_inc(s_gx, 1)
            link(v.tensor_tensor(ohm[:, :, :], oh[:, 0, :, :], oh[:, 1, :, :], ALU.add))
            link(v.tensor_tensor(ohm[:, :, :], ohm[:, :, :], over_e(valid[:, :]), ALU.mult))
            v.sem_inc(s_ohm, 1)
            v.wait_ge(s_ge, 1)
            link(v.tensor_scalar(gate[:, 0, :], gate[:, 1, :], 1.0, None, ALU.add))
            link(v.reciprocal(gate[:, 0, :], gate[:, 0, :]))
            link(v.tensor_tensor(gate[:, 1, :], gate[:, 1, :], gate[:, 0, :], ALU.mult))
            v.wait_ge(s_pre, 1)
            tot = bank[5][:, 0:NT * EXPERTS].rearrange("p (t e) -> p t e", e=EXPERTS)
            for e in range(EXPERTS):
                ins = v.tensor_tensor_scan(inc[:, :, e], ones[:, 0:NT], tot[:, :, e], 0.0, ALU.mult, ALU.add)
            link(ins)
            link(v.tensor_tensor(pos_e[:, :, :], inc[:, :, :], tot, ALU.subtract))
            link(v.tensor_tensor(pos_e[:, :, :], pos_e[:, :, :], bank[4][:, 0:NT * EXPERTS].rearrange("p (t e) -> p t e", e=EXPERTS), ALU.add))
            link(v.tensor_scalar(nt_i[:, :], inc[:, NT - 1, :], float(P - 1), None, ALU.add))
            link(v.tensor_scalar(nt_i[:, :], nt_i[:, :], 7, None, ALU.arith_shift_right))
            link(v.tensor_scalar(ntf[:, :], nt_i[:, :], 1.0, None, ALU.max))
            link(v.tensor_tensor_scan(ecum[:, :], ones[:, 0:EXPERTS], ntf[:, :], 0.0, ALU.mult, ALU.add))
            link(v.tensor_tensor(ebase[:, :], ecum[:, :], ntf[:, :], ALU.subtract))
            v.tensor_copy(etab[:, 0, :], ntf[:, :])
            v.tensor_copy(etab[:, 1, :], ebase[:, :])
            link(v.tensor_scalar(ebase[:, :], ebase[:, :], float(P), None, ALU.mult))
            link(v.tensor_tensor(pos_e[:, :, :], pos_e[:, :, :], ebase[:, :].unsqueeze(1).broadcast_to([P, NT, EXPERTS]), ALU.add))
            for k in range(2):
                link(v.tensor_tensor(cand[:, :, :], oh[:, k, :, :], pos_e[:, :, :], ALU.mult))
                link(v.tensor_reduce(pos[:, k, :], cand[:, :, :], AX.X, ALU.add))
            link(v.tensor_copy(pos_i[:, :, :], pos[:, :, :]))
            v.tensor_scalar(pai[:, :, :], pos_i[:, :, :], 7, None, ALU.arith_shift_right)
            link(v.tensor_scalar(pbi[:, :, :], pos_i[:, :, :], P - 1, None, ALU.bitwise_and))
            v.tensor_copy(pa[:, :, :], pai[:, :, :])
            v.tensor_copy(pb[:, :, :], pbi[:, :, :])
            link(v.tensor_copy(cid[:, :, :], cid_i[:, :, :]))
            link(v.tensor_tensor(cid[:, :, :], cid[:, :, :], valid[:, :].unsqueeze(1).broadcast_to([P, 2, NT]), ALU.mult))

            for k in range(2):
                for t in range(0, NT, SET):
                    m = slice(t, t + SET)
                    v.tensor_tensor(ohb[:, k, m, :], iota_p[:, :].unsqueeze(1).broadcast_to([P, SET, P]),
                                    pb[:, k, m].unsqueeze(2).broadcast_to([P, SET, P]), ALU.is_equal)
                    v.tensor_tensor(oha[:, k, m, :], iota_p[:, 0:SLOT_TILES].unsqueeze(1).broadcast_to([P, SET, SLOT_TILES]),
                                    pa[:, k, m].unsqueeze(2).broadcast_to([P, SET, SLOT_TILES]), ALU.is_equal).then_inc(s_ob, 1)
            v.wait_ge(s_om, 1)
            link(v.tensor_scalar(slot_f[:, :], bank[6][:, 0:SLOT_TILES], -1.0, None, ALU.add))
            link(v.tensor_scalar(slot_e[:, :], slot_f[:, :], 0.0, None, ALU.is_lt))
            link(v.tensor_scalar(slot_f[:, :], slot_f[:, :], 0.0, None, ALU.max))
            v.tensor_scalar(first[:, 0:1], part_f[:, :], float(CHOICE_ROWS), None, ALU.add)
            link(v.tensor_copy(slot_g[:, :], slot_f[:, :]))
            v.tensor_copy(si[:, :], first[:, 0:1])
            link(v.tensor_scalar(slot_g[:, :], slot_g[:, :], 1, None, ALU.arith_shift_right))
            link(v.tensor_scalar(slot_e[:, :], slot_e[:, :], first[:, 0:1], None, ALU.mult))
            link(v.tensor_tensor(slot_s[:, :], slot_f[:, :], slot_e[:, :], ALU.add))
            v.sem_inc(s_slot, 1)

            def token_indices(g):
                v.tensor_copy(gi[:, :], slot_g[:, ds(g, 1)] if not isinstance(g, int) else slot_g[:, g:g + 1]).then_inc(s_gi, 1)

            def expert_input(g, e):
                v.wait_ge(s_xT, g + 1)
                for k in range(2):
                    gain, bias = ((cols[:, 64 + k:65 + k], cols[:, 80 + k:81 + k]) if isinstance(e, int) else
                                  (cols[:, ds(e * 2 + (64 + k), 1)], cols[:, ds(e * 2 + (80 + k), 1)]))
                    ins = v.tensor_scalar(xeT[:, k, :], bank[2][:, k * P:(k + 1) * P], gain, bias, ALU.mult, ALU.add)
                ins.then_inc(s_xe, 1)

            def results(g, c):
                v.wait_ge(s_y, g + 1)
                v.wait_ge(s_sc, g * 16 + 16)
                v.tensor_copy(si[:, :], slot_s[:, ds(g, 1)])
                v.tensor_tensor(ys, bank[3][:, 0:D], fb2[:, c, :], ALU.add).then_inc(s_ys, 1)

            v.sem_inc(s_ys, 1)
            token_indices(0)
            expert_input(0, 0)
            token_indices(1)
            with v.Fori(0, EXPERTS // 2) as j:
                for c in range(2):
                    e = j * 2 + c
                    n_e = v.value_load(etab[0:1, 0, ds(e, 1)], min_val=1, max_val=NT)
                    b_e = v.value_load(etab[0:1, 1, ds(e, 1)], min_val=0, max_val=MAX_TILES)
                    v.wait_ge(s_fw[c], j * 48 + 48)
                    v.sem_inc(s_mark, 1)
                    with v.Fori(1, n_e) as i:
                        g = b_e + i
                        v.wait_ge(s_h, g * (FC // 2))
                        expert_input(g, e)
                        token_indices(g + 1)
                        results(g - 1, c)
                    v.wait_ge(s_h, (b_e + n_e) * (FC // 2))
                    expert_input(b_e + n_e, e + 1)
                    token_indices(b_e + n_e + 1)
                    results(b_e + n_e - 1, c)
                    v.wait_ge(s_ys, b_e + n_e + 1)
                    v.sem_inc(s_fwu, 1)
            total = v.value_load(etab[0:1, 1, EXPERTS - 1:EXPERTS], min_val=0, max_val=MAX_TILES)
            n_last = v.value_load(etab[0:1, 0, EXPERTS - 1:EXPERTS], min_val=1, max_val=NT)
            v.wait_ge(s_sc, (total + n_last) * 16 + 16)
            v.sem_inc(s_all, 1)

            for c in range(NT // SET):
                v.wait_ge(s_yl[c], 16 if c < NT // SET - 1 else 32)
                for k in range(2):
                    for t in range(c * SET, (c + 1) * SET):
                        r = slice(0, P if t < NT - 1 else LAST)
                        ins = v.scalar_tensor_tensor(xs[r, t, :], yl[c][r, t - c * SET, k * D:(k + 1) * D], gate[r, k, t:t + 1],
                                                     xs[r, t, :], ALU.mult, ALU.add)
                    link(ins)
                v.sem_inc(s_o, 1)


_INS = ['x', 'src', 'dst', 'L0_gnn_W1', 'L0_gnn_a1_src', 'L0_gnn_a1_dst', 'L0_gnn_b1', 'L0_gnn_ln_g', 'L0_gnn_ln_b',
        'L0_gnn_W2', 'L0_gnn_a2_src', 'L0_gnn_a2_dst', 'L0_gnn_b2', 'L0_ffn_Wr', 'L0_ffn_br', 'L0_ffn_ln_g',
        'L0_ffn_ln_b', 'L0_ffn_W1', 'L0_ffn_b1', 'L0_ffn_W2', 'L0_ffn_b2']


def edge_rows(a, spare, loops):
    rows = np.full((PAD_ROWS * P,), spare, a.dtype)
    rows[:E_IN] = a
    rows[ROWS * P:ROWS * P + LOOPS] = loops
    return rows.reshape(PAD_ROWS, P)


def kernel(**inputs):
    import concourse.bacc as bacc
    from concourse.bass_utils import run_bass_kernel_spmd as run

    nc = bacc.Bacc("TRN2", target_bir_lowering=False, num_devices=1)
    arrays, args = {}, []
    loops = np.arange(LOOPS)
    for name in _INS:
        a = np.ascontiguousarray(inputs[name])
        if name in ("src", "dst"):
            a = edge_rows(a, PAD_DST if name == "dst" else 0, loops)
        arrays[f"in_{name}"] = a
        args.append(nc.dram_tensor(f"in_{name}", a.shape, mybir.dt.from_np(a.dtype), kind="ExternalInput").ap())
    out = nc.dram_tensor("out_x", (N, D), mybir.dt.float32, kind="ExternalOutput").ap()
    build(nc, *args, out)
    result = run(nc, [arrays], core_ids=[0])
    return result.results[0]["out_x"]
```
